# Optimizing a Trainium2 kernel written in Bass

```python
import numpy as np
import jax
import jax.numpy as jnp

def _softmax(x, axis=-1):
    return jax.nn.softmax(x, axis=axis)

def _gelu(x):
    return jax.nn.gelu(x, approximate=True)

def _silu(x):
    return jax.nn.silu(x)

def _sigmoid(x):
    return jax.nn.sigmoid(x)

def _layernorm(x, axis=-1, eps=1e-05):
    m = jnp.mean(x, axis=axis, keepdims=True)
    v = jnp.var(x, axis=axis, keepdims=True)
    return (x - m) / jnp.sqrt(v + eps)

def _scatter_add(tgt, idx, src, axis=0):
    return tgt.at[idx].add(src)

def _segment_sum(src, seg, n):
    return jax.ops.segment_sum(src, seg, n)
kernel_name = 'mk_adaln_d4_jaxref_r8_b0dc43'

def setup_inputs(seed: int=0):
    np.random.seed(seed)
    _w = jnp.asarray

    def _L0_attn_setup():
        import jax, jax.numpy as jnp
        import numpy as np
        import math
        TALA_CYCLES = [5, 6, 7, 8]
        N_HEADS = 16
        key = jax.random.key(seed)
        k1, k2, k3, k4 = jax.random.split(key, 4)
        B, T, D = (2, 256, 128)
        x = jax.random.normal(k1, (B, T, D), dtype=jnp.float32)
        w_qkv = jax.random.normal(k2, (D, 3 * D), dtype=jnp.float32) * (1.0 / math.sqrt(D))
        w_out = jax.random.normal(k3, (D, D), dtype=jnp.float32) * (1.0 / math.sqrt(D))
        bandha_gate = jax.random.normal(k4, (N_HEADS, max(TALA_CYCLES)), dtype=jnp.float32)
        return {'x': x, 'w_qkv': w_qkv, 'w_out': w_out, 'bandha_gate': bandha_gate}
    _L0_attn_in = _L0_attn_setup()

    def _L0_ffn_setup():
        import jax, jax.numpy as jnp
        import numpy as np
        B, S, H, I = (2, 256, 128, 64)
        E, K, G, TG = (64, 8, 8, 4)
        SCALE = 2.5
        CAP = 128
        key = jax.random.key(seed)
        ks = jax.random.split(key, 6)
        hidden_states = jax.random.normal(ks[0], (B, S, H), jnp.float32)
        gate_w = jax.random.normal(ks[1], (E, H), jnp.float32) * 0.02
        gate_bias = jax.random.normal(ks[2], (E,), jnp.float32) * 0.02
        w_gate = jax.random.normal(ks[3], (E, H, I), jnp.float32) * (1.0 / np.sqrt(H))
        w_up = jax.random.normal(ks[4], (E, H, I), jnp.float32) * (1.0 / np.sqrt(H))
        w_down = jax.random.normal(ks[5], (E, I, H), jnp.float32) * (1.0 / np.sqrt(I))
        return {'hidden_states': hidden_states, 'gate_w': gate_w, 'gate_bias': gate_bias, 'w_gate': w_gate, 'w_up': w_up, 'w_down': w_down}
    _L0_ffn_in = _L0_ffn_setup()
    _L0_c = _w((lambda *s: np.random.randn(*s).astype(np.float32) * 0.05)(16, 128))
    _L0_wmod = _w((lambda *s: np.random.randn(*s).astype(np.float32) * 0.05)(128, 6 * 128) * 128 ** (-0.5))

    def _L1_attn_setup():
        import jax, jax.numpy as jnp
        import numpy as np
        D_MODEL = 128
        NUM_HEADS = 16
        D_HEAD = D_MODEL // NUM_HEADS
        LAMBDA_INIT = 0.8
        EPS = 1e-05
        key = jax.random.key(seed)
        ks = jax.random.split(key, 10)
        B, N = (2, 256)

        def xav(k, shape):
            fan_in, fan_out = (shape[0], shape[1])
            lim = np.sqrt(6.0 / (fan_in + fan_out))
            return jax.random.uniform(k, shape, jnp.float32, -lim, lim)
        return {'X': jax.random.normal(ks[0], (B, N, D_MODEL), jnp.float32), 'Wq': xav(ks[1], (D_MODEL, 2 * D_MODEL)), 'Wk': xav(ks[2], (D_MODEL, 2 * D_MODEL)), 'Wv': xav(ks[3], (D_MODEL, 2 * D_MODEL)), 'Wo': xav(ks[4], (2 * D_MODEL, D_MODEL)), 'lambda_q1': jax.random.normal(ks[5], (NUM_HEADS, D_HEAD), jnp.float32), 'lambda_k1': jax.random.normal(ks[6], (NUM_HEADS, D_HEAD), jnp.float32), 'lambda_q2': jax.random.normal(ks[7], (NUM_HEADS, D_HEAD), jnp.float32), 'lambda_k2': jax.random.normal(ks[8], (NUM_HEADS, D_HEAD), jnp.float32), 'rms_scale': jnp.ones((2 * D_HEAD,), jnp.float32)}
    _L1_attn_in = _L1_attn_setup()

    def _L1_ffn_setup():
        import jax, jax.numpy as jnp
        import numpy as np
        import math
        N_EMBD = 128
        HIDDEN = 4 * N_EMBD
        N_EXPERTS = 8
        TOP_K = 2
        B, T = (4, 256)

        def new_gelu(x):
            c = math.sqrt(2.0 / math.pi)
            return 0.5 * x * (1.0 + jnp.tanh(c * (x + 0.044715 * x * x * x)))

        def _moe_forward(x, Wfc_s, bfc_s, Wproj_s, bproj_s, Wr, Wfc, bfc, Wproj, bproj):
            Bb, Tt, C = x.shape
            xf = x.reshape(Bb * Tt, C)
            N = Bb * Tt
            shared = new_gelu(xf @ Wfc_s + bfc_s) @ Wproj_s + bproj_s
            logits = xf @ Wr
            probs = jax.nn.softmax(logits, axis=-1)
            topk_p, topk_i = jax.lax.top_k(probs, TOP_K)
            topk_p = topk_p / jnp.sum(topk_p, axis=-1, keepdims=True)
            gate = jnp.zeros((N, N_EXPERTS), dtype=xf.dtype)
            gate = gate.at[jnp.arange(N)[:, None], topk_i].add(topk_p)
            routed = jnp.zeros_like(xf)
            for e in range(N_EXPERTS):
                h = new_gelu(xf @ Wfc[e] + bfc[e]) @ Wproj[e] + bproj[e]
                routed = routed + h * gate[:, e:e + 1]
            return (shared + routed).reshape(Bb, Tt, C)
        key = jax.random.key(seed)
        ks = jax.random.split(key, 10)
        s = 0.02
        return {'x': jax.random.normal(ks[0], (B, T, N_EMBD), dtype=jnp.float32), 'Wfc_s': jax.random.normal(ks[1], (N_EMBD, HIDDEN), dtype=jnp.float32) * s, 'bfc_s': jnp.zeros((HIDDEN,), dtype=jnp.float32), 'Wproj_s': jax.random.normal(ks[2], (HIDDEN, N_EMBD), dtype=jnp.float32) * s, 'bproj_s': jnp.zeros((N_EMBD,), dtype=jnp.float32), 'Wr': jax.random.normal(ks[3], (N_EMBD, N_EXPERTS), dtype=jnp.float32) * s, 'Wfc': jax.random.normal(ks[4], (N_EXPERTS, N_EMBD, HIDDEN), dtype=jnp.float32) * s, 'bfc': jnp.zeros((N_EXPERTS, HIDDEN), dtype=jnp.float32), 'Wproj': jax.random.normal(ks[5], (N_EXPERTS, HIDDEN, N_EMBD), dtype=jnp.float32) * s, 'bproj': jnp.zeros((N_EXPERTS, N_EMBD), dtype=jnp.float32)}
    _L1_ffn_in = _L1_ffn_setup()
    _L1_c = _w((lambda *s: np.random.randn(*s).astype(np.float32) * 0.05)(16, 128))
    _L1_wmod = _w((lambda *s: np.random.randn(*s).astype(np.float32) * 0.05)(128, 6 * 128) * 128 ** (-0.5))

    def _L2_attn_setup():
        import jax, jax.numpy as jnp
        import numpy as np
        EMBED_DIM = 128
        NUM_HEADS = 16
        HEAD_DIM = EMBED_DIM // NUM_HEADS
        SCALING = HEAD_DIM ** (-0.5)
        B, T = (2, 256)
        key = jax.random.key(seed)
        ks = jax.random.split(key, 8)
        s = 0.02
        return {'hidden_states': jax.random.normal(ks[0], (B, T, EMBED_DIM), jnp.float32), 'Wq': jax.random.normal(ks[1], (EMBED_DIM, EMBED_DIM), jnp.float32) * s, 'bq': jax.random.normal(ks[2], (EMBED_DIM,), jnp.float32) * s, 'Wk': jax.random.normal(ks[3], (HEAD_DIM, EMBED_DIM), jnp.float32) * s, 'Wv': jax.random.normal(ks[4], (HEAD_DIM, EMBED_DIM), jnp.float32) * s, 'bv': jax.random.normal(ks[5], (HEAD_DIM,), jnp.float32) * s, 'Wo': jax.random.normal(ks[6], (EMBED_DIM, EMBED_DIM), jnp.float32) * s, 'bo': jax.random.normal(ks[7], (EMBED_DIM,), jnp.float32) * s}
    _L2_attn_in = _L2_attn_setup()

    def _L2_ffn_setup():
        import jax, jax.numpy as jnp
        import numpy as np
        DIM = 128
        N_HEADS = 16
        N_KV_HEADS = 4
        HEAD_DIM = DIM // N_HEADS
        N_REP = N_HEADS // N_KV_HEADS
        N_EXPERTS = 4
        TOP_K = 2
        HIDDEN = 3 * DIM
        EPS = 1.1920928955078125e-07

        def _rmsnorm(x, g):
            var = jnp.mean(jnp.square(x), axis=-1, keepdims=True)
            return x * jax.lax.rsqrt(var + EPS) * g

        def _rotate_half(x):
            x1, x2 = jnp.split(x, 2, axis=-1)
            return jnp.concatenate([-x2, x1], axis=-1)

        def _rope_tables(S):
            inv_freq = 1.0 / 10000.0 ** (jnp.arange(0, HEAD_DIM, 2, dtype=jnp.float32) / HEAD_DIM)
            freqs = jnp.arange(S, dtype=jnp.float32)[:, None] * inv_freq[None, :]
            emb = jnp.concatenate([freqs, freqs], axis=-1)
            return (jnp.cos(emb), jnp.sin(emb))

        def _attention(x, wq, wk, wv, wo):
            B, S, D = x.shape
            q = (x @ wq).reshape(B, S, N_HEADS, HEAD_DIM).transpose(0, 2, 1, 3)
            k = (x @ wk).reshape(B, S, N_KV_HEADS, HEAD_DIM).transpose(0, 2, 1, 3)
            v = (x @ wv).reshape(B, S, N_KV_HEADS, HEAD_DIM).transpose(0, 2, 1, 3)
            cos, sin = _rope_tables(S)
            q = q * cos + _rotate_half(q) * sin
            k = k * cos + _rotate_half(k) * sin
            k = jnp.repeat(k, N_REP, axis=1)
            v = jnp.repeat(v, N_REP, axis=1)
            scores = jnp.einsum('bhqd,bhkd->bhqk', q, k) / jnp.sqrt(jnp.float32(HEAD_DIM))
            causal = jnp.tril(jnp.ones((S, S), dtype=bool))
            scores = jnp.where(causal, scores, -jnp.inf)
            attn = jax.nn.softmax(scores, axis=-1)
            out = jnp.einsum('bhqk,bhkd->bhqd', attn, v)
            return out.transpose(0, 2, 1, 3).reshape(B, S, D) @ wo

        def _moe(x, gate, w1, w2, w3):
            B, S, D = x.shape
            xf = x.reshape(-1, D)
            probs = jax.nn.softmax(xf @ gate, axis=-1)
            w, idx = jax.lax.top_k(probs, TOP_K)
            w = w / jnp.sum(w, axis=-1, keepdims=True)
            oh = jax.nn.one_hot(idx, N_EXPERTS, dtype=xf.dtype)
            comb = jnp.einsum('nk,nke->ne', w, oh)
            out = jnp.zeros_like(xf)
            for e in range(N_EXPERTS):
                h = jax.nn.silu(xf @ w1[e]) * (xf @ w3[e])
                out = out + comb[:, e:e + 1] * (h @ w2[e])
            return out.reshape(B, S, D)
        key = jax.random.key(seed)
        ks = jax.random.split(key, 12)
        s = 0.02
        B, S = (2, 256)
        return {'x': jax.random.normal(ks[0], (B, S, DIM), jnp.float32), 'g1': jnp.ones((DIM,), jnp.float32), 'g2': jnp.ones((DIM,), jnp.float32), 'wq': jax.random.normal(ks[1], (DIM, N_HEADS * HEAD_DIM), jnp.float32) * s, 'wk': jax.random.normal(ks[2], (DIM, N_KV_HEADS * HEAD_DIM), jnp.float32) * s, 'wv': jax.random.normal(ks[3], (DIM, N_KV_HEADS * HEAD_DIM), jnp.float32) * s, 'wo': jax.random.normal(ks[4], (N_HEADS * HEAD_DIM, DIM), jnp.float32) * s, 'gate': jax.random.normal(ks[5], (DIM, N_EXPERTS), jnp.float32) * s, 'w1': jax.random.normal(ks[6], (N_EXPERTS, DIM, HIDDEN), jnp.float32) * s, 'w2': jax.random.normal(ks[7], (N_EXPERTS, HIDDEN, DIM), jnp.float32) * s, 'w3': jax.random.normal(ks[8], (N_EXPERTS, DIM, HIDDEN), jnp.float32) * s}
    _L2_ffn_in = _L2_ffn_setup()
    _L2_c = _w((lambda *s: np.random.randn(*s).astype(np.float32) * 0.05)(16, 128))
    _L2_wmod = _w((lambda *s: np.random.randn(*s).astype(np.float32) * 0.05)(128, 6 * 128) * 128 ** (-0.5))

    def _L3_attn_setup():
        import jax, jax.numpy as jnp
        import numpy as np
        B, N, D, H = (4, 512, 128, 16)
        HD = D // H
        MLP = 4 * D

        def _ln(x, w, b):
            m = x.mean(-1, keepdims=True)
            v = x.var(-1, keepdims=True)
            return (x - m) / jnp.sqrt(v + 1e-05) * w + b
        key = jax.random.key(seed)
        ks = jax.random.split(key, 12)
        s = 1.0 / np.sqrt(D)
        sm = 1.0 / np.sqrt(MLP)
        return {'q_x': jax.random.normal(ks[0], (B, N, D), jnp.float32), 'ln1_w': jnp.ones((D,), jnp.float32), 'ln1_b': jnp.zeros((D,), jnp.float32), 'wq': jax.random.normal(ks[1], (D, D), jnp.float32) * s, 'bq': jnp.zeros((D,), jnp.float32), 'wk': jax.random.normal(ks[2], (D, D), jnp.float32) * s, 'bk': jnp.zeros((D,), jnp.float32), 'wv': jax.random.normal(ks[3], (D, D), jnp.float32) * s, 'bv': jnp.zeros((D,), jnp.float32), 'wo': jax.random.normal(ks[4], (D, D), jnp.float32) * s, 'bo': jnp.zeros((D,), jnp.float32), 'ln2_w': jnp.ones((D,), jnp.float32), 'ln2_b': jnp.zeros((D,), jnp.float32), 'fc_w': jax.random.normal(ks[5], (D, MLP), jnp.float32) * s, 'fc_b': jnp.zeros((MLP,), jnp.float32), 'proj_w': jax.random.normal(ks[6], (MLP, D), jnp.float32) * sm, 'proj_b': jnp.zeros((D,), jnp.float32)}
    _L3_attn_in = _L3_attn_setup()

    def _L3_ffn_setup():
        import jax, jax.numpy as jnp
        import numpy as np
        B, S, D = (4, 256, 128)
        E, K = (8, 2)
        H = 176
        key = jax.random.key(seed)
        kx, kr, k1, k2, k3 = jax.random.split(key, 5)
        s = 0.02
        return {'x': jax.random.normal(kx, (B, S, D), dtype=jnp.float32), 'w_router': jax.random.normal(kr, (E, D), dtype=jnp.float32) * s, 'w1': jax.random.normal(k1, (E, D, H), dtype=jnp.float32) * s, 'w2': jax.random.normal(k2, (E, H, D), dtype=jnp.float32) * s, 'w3': jax.random.normal(k3, (E, D, H), dtype=jnp.float32) * s}
    _L3_ffn_in = _L3_ffn_setup()
    _L3_c = _w((lambda *s: np.random.randn(*s).astype(np.float32) * 0.05)(16, 128))
    _L3_wmod = _w((lambda *s: np.random.randn(*s).astype(np.float32) * 0.05)(128, 6 * 128) * 128 ** (-0.5))
    _d = {'L0_attn_x': _L0_attn_in['x'], 'L0_attn_w_qkv': _L0_attn_in['w_qkv'], 'L0_attn_w_out': _L0_attn_in['w_out'], 'L0_attn_bandha_gate': _L0_attn_in['bandha_gate'], 'L0_ffn_gate_w': _L0_ffn_in['gate_w'], 'L0_ffn_gate_bias': _L0_ffn_in['gate_bias'], 'L0_ffn_w_gate': _L0_ffn_in['w_gate'], 'L0_ffn_w_up': _L0_ffn_in['w_up'], 'L0_ffn_w_down': _L0_ffn_in['w_down'], 'L0_c': _L0_c, 'L0_wmod': _L0_wmod, 'L1_attn_Wq': _L1_attn_in['Wq'], 'L1_attn_Wk': _L1_attn_in['Wk'], 'L1_attn_Wv': _L1_attn_in['Wv'], 'L1_attn_Wo': _L1_attn_in['Wo'], 'L1_attn_lambda_q1': _L1_attn_in['lambda_q1'], 'L1_attn_lambda_k1': _L1_attn_in['lambda_k1'], 'L1_attn_lambda_q2': _L1_attn_in['lambda_q2'], 'L1_attn_lambda_k2': _L1_attn_in['lambda_k2'], 'L1_attn_rms_scale': _L1_attn_in['rms_scale'], 'L1_ffn_Wfc_s': _L1_ffn_in['Wfc_s'], 'L1_ffn_bfc_s': _L1_ffn_in['bfc_s'], 'L1_ffn_Wproj_s': _L1_ffn_in['Wproj_s'], 'L1_ffn_bproj_s': _L1_ffn_in['bproj_s'], 'L1_ffn_Wr': _L1_ffn_in['Wr'], 'L1_ffn_Wfc': _L1_ffn_in['Wfc'], 'L1_ffn_bfc': _L1_ffn_in['bfc'], 'L1_ffn_Wproj': _L1_ffn_in['Wproj'], 'L1_ffn_bproj': _L1_ffn_in['bproj'], 'L1_c': _L1_c, 'L1_wmod': _L1_wmod, 'L2_attn_Wq': _L2_attn_in['Wq'], 'L2_attn_bq': _L2_attn_in['bq'], 'L2_attn_Wk': _L2_attn_in['Wk'], 'L2_attn_Wv': _L2_attn_in['Wv'], 'L2_attn_bv': _L2_attn_in['bv'], 'L2_attn_Wo': _L2_attn_in['Wo'], 'L2_attn_bo': _L2_attn_in['bo'], 'L2_ffn_g1': _L2_ffn_in['g1'], 'L2_ffn_g2': _L2_ffn_in['g2'], 'L2_ffn_wq': _L2_ffn_in['wq'], 'L2_ffn_wk': _L2_ffn_in['wk'], 'L2_ffn_wv': _L2_ffn_in['wv'], 'L2_ffn_wo': _L2_ffn_in['wo'], 'L2_ffn_gate': _L2_ffn_in['gate'], 'L2_ffn_w1': _L2_ffn_in['w1'], 'L2_ffn_w2': _L2_ffn_in['w2'], 'L2_ffn_w3': _L2_ffn_in['w3'], 'L2_c': _L2_c, 'L2_wmod': _L2_wmod, 'L3_attn_ln1_w': _L3_attn_in['ln1_w'], 'L3_attn_ln1_b': _L3_attn_in['ln1_b'], 'L3_attn_wq': _L3_attn_in['wq'], 'L3_attn_bq': _L3_attn_in['bq'], 'L3_attn_wk': _L3_attn_in['wk'], 'L3_attn_bk': _L3_attn_in['bk'], 'L3_attn_wv': _L3_attn_in['wv'], 'L3_attn_bv': _L3_attn_in['bv'], 'L3_attn_wo': _L3_attn_in['wo'], 'L3_attn_bo': _L3_attn_in['bo'], 'L3_attn_ln2_w': _L3_attn_in['ln2_w'], 'L3_attn_ln2_b': _L3_attn_in['ln2_b'], 'L3_attn_fc_w': _L3_attn_in['fc_w'], 'L3_attn_fc_b': _L3_attn_in['fc_b'], 'L3_attn_proj_w': _L3_attn_in['proj_w'], 'L3_attn_proj_b': _L3_attn_in['proj_b'], 'L3_ffn_w_router': _L3_ffn_in['w_router'], 'L3_ffn_w1': _L3_ffn_in['w1'], 'L3_ffn_w2': _L3_ffn_in['w2'], 'L3_ffn_w3': _L3_ffn_in['w3'], 'L3_c': _L3_c, 'L3_wmod': _L3_wmod}
    _x0 = _d['L0_attn_x']
    _d['L0_attn_x'] = jax.random.normal(jax.random.fold_in(jax.random.key(seed), 1), (16, 256, 128), dtype=_x0.dtype)
    del _x0
    return _d

def reference(L0_attn_x, L0_attn_w_qkv, L0_attn_w_out, L0_attn_bandha_gate, L0_ffn_gate_w, L0_ffn_gate_bias, L0_ffn_w_gate, L0_ffn_w_up, L0_ffn_w_down, L0_c, L0_wmod, L1_attn_Wq, L1_attn_Wk, L1_attn_Wv, L1_attn_Wo, L1_attn_lambda_q1, L1_attn_lambda_k1, L1_attn_lambda_q2, L1_attn_lambda_k2, L1_attn_rms_scale, L1_ffn_Wfc_s, L1_ffn_bfc_s, L1_ffn_Wproj_s, L1_ffn_bproj_s, L1_ffn_Wr, L1_ffn_Wfc, L1_ffn_bfc, L1_ffn_Wproj, L1_ffn_bproj, L1_c, L1_wmod, L2_attn_Wq, L2_attn_bq, L2_attn_Wk, L2_attn_Wv, L2_attn_bv, L2_attn_Wo, L2_attn_bo, L2_ffn_g1, L2_ffn_g2, L2_ffn_wq, L2_ffn_wk, L2_ffn_wv, L2_ffn_wo, L2_ffn_gate, L2_ffn_w1, L2_ffn_w2, L2_ffn_w3, L2_c, L2_wmod, L3_attn_ln1_w, L3_attn_ln1_b, L3_attn_wq, L3_attn_bq, L3_attn_wk, L3_attn_bk, L3_attn_wv, L3_attn_bv, L3_attn_wo, L3_attn_bo, L3_attn_ln2_w, L3_attn_ln2_b, L3_attn_fc_w, L3_attn_fc_b, L3_attn_proj_w, L3_attn_proj_b, L3_ffn_w_router, L3_ffn_w1, L3_ffn_w2, L3_ffn_w3, L3_c, L3_wmod):

    def _L0_attn_ref(x, w_qkv, w_out, bandha_gate):
        import jax, jax.numpy as jnp
        import numpy as np
        import math
        TALA_CYCLES = [5, 6, 7, 8]
        N_HEADS = 16
        B, T, D = x.shape
        H = N_HEADS
        hd = D // H
        scale = math.sqrt(hd)
        qkv = x @ w_qkv
        q, k, v = jnp.split(qkv, 3, axis=-1)
        to_heads = lambda t: t.reshape(B, T, H, hd).transpose(0, 2, 1, 3)
        q, k, v = (to_heads(q), to_heads(k), to_heads(v))
        cycles = np.array([TALA_CYCLES[i % len(TALA_CYCLES)] for i in range(H)])
        phases = np.arange(T)[None, :] % cycles[:, None]
        gate = jax.nn.sigmoid(jnp.take_along_axis(bandha_gate, jnp.asarray(phases), axis=1))
        q = q * gate[None, :, :, None]
        scores = jnp.einsum('bhqd,bhkd->bhqk', q, k) / scale
        causal = np.tril(np.ones((T, T), dtype=bool))
        scores = jnp.where(jnp.asarray(causal), scores, -jnp.inf)
        attn = jax.nn.softmax(scores, axis=-1)
        out = jnp.einsum('bhqk,bhkd->bhqd', attn, v)
        out = out.transpose(0, 2, 1, 3).reshape(B, T, D)
        return out @ w_out

    def _L0_ffn_ref(hidden_states, gate_w, gate_bias, w_gate, w_up, w_down):
        import jax, jax.numpy as jnp
        import numpy as np
        B, S, H, I = (2, 256, 128, 64)
        E, K, G, TG = (64, 8, 8, 4)
        SCALE = 2.5
        CAP = 128
        b, s, h = hidden_states.shape
        x = hidden_states.reshape(-1, h)
        n = x.shape[0]
        logits = x.astype(jnp.float32) @ gate_w.astype(jnp.float32).T
        scores = jax.nn.sigmoid(logits)
        sfc = scores + gate_bias[None, :]
        group_scores = jax.lax.top_k(sfc.reshape(n, G, E // G), 2)[0].sum(-1)
        gidx = jax.lax.top_k(group_scores, TG)[1]
        gmask = jnp.zeros((n, G), bool).at[jnp.arange(n)[:, None], gidx].set(True)
        smask = jnp.repeat(gmask, E // G, axis=1)
        tmp = jnp.where(smask, sfc, -jnp.inf)
        topk_idx = jax.lax.top_k(tmp, K)[1]
        topk_w = jnp.take_along_axis(scores, topk_idx, axis=1)
        topk_w = topk_w / (topk_w.sum(-1, keepdims=True) + 1e-20)
        topk_w = topk_w * SCALE
        e = topk_idx.reshape(-1)
        token = jnp.repeat(jnp.arange(n), K)
        oh = jax.nn.one_hot(e, E, dtype=jnp.int32)
        pos = jnp.take_along_axis(jnp.cumsum(oh, 0) - 1, e[:, None], 1)[:, 0]
        valid = pos < CAP
        pos_c = jnp.where(valid, pos, CAP)
        buf = jnp.zeros((E, CAP + 1, h), x.dtype).at[e, pos_c].set(x[token])[:, :CAP]
        g = jnp.einsum('ech,ehi->eci', buf, w_gate)
        u = jnp.einsum('ech,ehi->eci', buf, w_up)
        y = jnp.einsum('eci,eih->ech', jax.nn.silu(g) * u, w_down)
        y_slots = y[e, jnp.minimum(pos, CAP - 1)]
        w_slot = topk_w.reshape(-1) * valid.astype(topk_w.dtype)
        out = jnp.zeros((n, h), jnp.float32).at[token].add(y_slots * w_slot[:, None])
        return out.reshape(b, s, h)

    def _L1_attn_ref(X, Wq, Wk, Wv, Wo, lambda_q1, lambda_k1, lambda_q2, lambda_k2, rms_scale):
        import jax, jax.numpy as jnp
        import numpy as np
        D_MODEL = 128
        NUM_HEADS = 16
        D_HEAD = D_MODEL // NUM_HEADS
        LAMBDA_INIT = 0.8
        EPS = 1e-05
        B, N, _ = X.shape
        H, Dh = (NUM_HEADS, D_HEAD)
        Q = (X @ Wq).reshape(B, N, H, 2 * Dh).transpose(0, 2, 1, 3)
        K = (X @ Wk).reshape(B, N, H, 2 * Dh).transpose(0, 2, 1, 3)
        V = (X @ Wv).reshape(B, N, H, 2 * Dh).transpose(0, 2, 1, 3)
        Q1, Q2 = (Q[..., :Dh], Q[..., Dh:])
        K1, K2 = (K[..., :Dh], K[..., Dh:])
        lam = jnp.exp(jnp.sum(lambda_q1 * lambda_k1, -1)) - jnp.exp(jnp.sum(lambda_q2 * lambda_k2, -1)) + LAMBDA_INIT
        scaling = 1.0 / np.sqrt(Dh)
        causal = jnp.tril(jnp.ones((N, N), bool))
        neg_inf = jnp.float32(-jnp.inf)
        A1 = jnp.einsum('bhqd,bhkd->bhqk', Q1, K1) * scaling
        A2 = jnp.einsum('bhqd,bhkd->bhqk', Q2, K2) * scaling
        A1 = jnp.where(causal, A1, neg_inf)
        A2 = jnp.where(causal, A2, neg_inf)
        attn = jax.nn.softmax(A1, axis=-1) - lam[None, :, None, None] * jax.nn.softmax(A2, axis=-1)
        O = jnp.einsum('bhqk,bhkd->bhqd', attn, V)
        rms = jnp.sqrt(jnp.mean(O * O, axis=-1, keepdims=True) + EPS)
        O = O / rms * rms_scale
        O = O * (1.0 - LAMBDA_INIT)
        O = O.transpose(0, 2, 1, 3).reshape(B, N, H * 2 * Dh)
        return O @ Wo

    def _L1_ffn_ref(x, Wfc_s, bfc_s, Wproj_s, bproj_s, Wr, Wfc, bfc, Wproj, bproj):
        import jax, jax.numpy as jnp
        import numpy as np
        import math
        N_EMBD = 128
        HIDDEN = 4 * N_EMBD
        N_EXPERTS = 8
        TOP_K = 2
        B, T = (4, 256)

        def new_gelu(x):
            c = math.sqrt(2.0 / math.pi)
            return 0.5 * x * (1.0 + jnp.tanh(c * (x + 0.044715 * x * x * x)))

        def _moe_forward(x, Wfc_s, bfc_s, Wproj_s, bproj_s, Wr, Wfc, bfc, Wproj, bproj):
            Bb, Tt, C = x.shape
            xf = x.reshape(Bb * Tt, C)
            N = Bb * Tt
            shared = new_gelu(xf @ Wfc_s + bfc_s) @ Wproj_s + bproj_s
            logits = xf @ Wr
            probs = jax.nn.softmax(logits, axis=-1)
            topk_p, topk_i = jax.lax.top_k(probs, TOP_K)
            topk_p = topk_p / jnp.sum(topk_p, axis=-1, keepdims=True)
            gate = jnp.zeros((N, N_EXPERTS), dtype=xf.dtype)
            gate = gate.at[jnp.arange(N)[:, None], topk_i].add(topk_p)
            routed = jnp.zeros_like(xf)
            for e in range(N_EXPERTS):
                h = new_gelu(xf @ Wfc[e] + bfc[e]) @ Wproj[e] + bproj[e]
                routed = routed + h * gate[:, e:e + 1]
            return (shared + routed).reshape(Bb, Tt, C)
        return _moe_forward(x, Wfc_s, bfc_s, Wproj_s, bproj_s, Wr, Wfc, bfc, Wproj, bproj)

    def _L2_attn_ref(hidden_states, Wq, bq, Wk, Wv, bv, Wo, bo):
        import jax, jax.numpy as jnp
        import numpy as np
        EMBED_DIM = 128
        NUM_HEADS = 16
        HEAD_DIM = EMBED_DIM // NUM_HEADS
        SCALING = HEAD_DIM ** (-0.5)
        B, T = (2, 256)
        bsz, tgt_len, _ = hidden_states.shape
        q = (hidden_states @ Wq.T + bq) * SCALING
        k = hidden_states @ Wk.T
        v = hidden_states @ Wv.T + bv
        q = q.reshape(bsz, tgt_len, NUM_HEADS, HEAD_DIM)
        scores = jnp.einsum('bthd,bsd->bhts', q, k)
        probs = jax.nn.softmax(scores, axis=-1)
        ctx = jnp.einsum('bhts,bsd->bthd', probs, v)
        ctx = ctx.reshape(bsz, tgt_len, EMBED_DIM)
        return ctx @ Wo.T + bo

    def _L2_ffn_ref(x, g1, g2, wq, wk, wv, wo, gate, w1, w2, w3):
        import jax, jax.numpy as jnp
        import numpy as np
        DIM = 128
        N_HEADS = 16
        N_KV_HEADS = 4
        HEAD_DIM = DIM // N_HEADS
        N_REP = N_HEADS // N_KV_HEADS
        N_EXPERTS = 4
        TOP_K = 2
        HIDDEN = 3 * DIM
        EPS = 1.1920928955078125e-07

        def _rmsnorm(x, g):
            var = jnp.mean(jnp.square(x), axis=-1, keepdims=True)
            return x * jax.lax.rsqrt(var + EPS) * g

        def _rotate_half(x):
            x1, x2 = jnp.split(x, 2, axis=-1)
            return jnp.concatenate([-x2, x1], axis=-1)

        def _rope_tables(S):
            inv_freq = 1.0 / 10000.0 ** (jnp.arange(0, HEAD_DIM, 2, dtype=jnp.float32) / HEAD_DIM)
            freqs = jnp.arange(S, dtype=jnp.float32)[:, None] * inv_freq[None, :]
            emb = jnp.concatenate([freqs, freqs], axis=-1)
            return (jnp.cos(emb), jnp.sin(emb))

        def _attention(x, wq, wk, wv, wo):
            B, S, D = x.shape
            q = (x @ wq).reshape(B, S, N_HEADS, HEAD_DIM).transpose(0, 2, 1, 3)
            k = (x @ wk).reshape(B, S, N_KV_HEADS, HEAD_DIM).transpose(0, 2, 1, 3)
            v = (x @ wv).reshape(B, S, N_KV_HEADS, HEAD_DIM).transpose(0, 2, 1, 3)
            cos, sin = _rope_tables(S)
            q = q * cos + _rotate_half(q) * sin
            k = k * cos + _rotate_half(k) * sin
            k = jnp.repeat(k, N_REP, axis=1)
            v = jnp.repeat(v, N_REP, axis=1)
            scores = jnp.einsum('bhqd,bhkd->bhqk', q, k) / jnp.sqrt(jnp.float32(HEAD_DIM))
            causal = jnp.tril(jnp.ones((S, S), dtype=bool))
            scores = jnp.where(causal, scores, -jnp.inf)
            attn = jax.nn.softmax(scores, axis=-1)
            out = jnp.einsum('bhqk,bhkd->bhqd', attn, v)
            return out.transpose(0, 2, 1, 3).reshape(B, S, D) @ wo

        def _moe(x, gate, w1, w2, w3):
            B, S, D = x.shape
            xf = x.reshape(-1, D)
            probs = jax.nn.softmax(xf @ gate, axis=-1)
            w, idx = jax.lax.top_k(probs, TOP_K)
            w = w / jnp.sum(w, axis=-1, keepdims=True)
            oh = jax.nn.one_hot(idx, N_EXPERTS, dtype=xf.dtype)
            comb = jnp.einsum('nk,nke->ne', w, oh)
            out = jnp.zeros_like(xf)
            for e in range(N_EXPERTS):
                h = jax.nn.silu(xf @ w1[e]) * (xf @ w3[e])
                out = out + comb[:, e:e + 1] * (h @ w2[e])
            return out.reshape(B, S, D)
        x = x + _attention(_rmsnorm(x, g1), wq, wk, wv, wo)
        x = x + _moe(_rmsnorm(x, g2), gate, w1, w2, w3)
        return x

    def _L3_attn_ref(q_x, ln1_w, ln1_b, wq, bq, wk, bk, wv, bv, wo, bo, ln2_w, ln2_b, fc_w, fc_b, proj_w, proj_b):
        import jax, jax.numpy as jnp
        import numpy as np
        B, N, D, H = (4, 512, 128, 16)
        HD = D // H
        MLP = 4 * D

        def _ln(x, w, b):
            m = x.mean(-1, keepdims=True)
            v = x.var(-1, keepdims=True)
            return (x - m) / jnp.sqrt(v + 1e-05) * w + b
        b, n, c = q_x.shape
        xn = _ln(q_x, ln1_w, ln1_b)
        q = (xn @ wq + bq).reshape(b, n, H, HD).transpose(0, 2, 1, 3)
        k = (xn @ wk + bk).reshape(b, n, H, HD).transpose(0, 2, 1, 3)
        v = (xn @ wv + bv).reshape(b, n, H, HD).transpose(0, 2, 1, 3)
        fq = jax.nn.elu(q) + 1.0
        fk = jax.nn.elu(k) + 1.0
        kv = jnp.einsum('bhnd,bhne->bnde', fk, v)
        qkv = jnp.einsum('bhnd,bnde->bhne', fq, kv)
        k_sum = fk.sum(axis=1)
        qk = jnp.einsum('bhnd,bnd->bhn', fq, k_sum)
        attn = qkv / (qk[..., None] + 1e-06)
        attn = attn.transpose(0, 2, 1, 3).reshape(b, n, c)
        attn = attn @ wo + bo
        x = q_x + attn
        h = _ln(x, ln2_w, ln2_b)
        h = jax.nn.gelu(h @ fc_w + fc_b, approximate=False)
        return x + (h @ proj_w + proj_b)

    def _L3_ffn_ref(x, w_router, w1, w2, w3):
        import jax, jax.numpy as jnp
        import numpy as np
        B, S, D = (4, 256, 128)
        E, K = (8, 2)
        H = 176
        bsz, seqlen, dim = x.shape
        xf = x.reshape(-1, dim)
        scores = jax.nn.softmax(xf @ w_router.T, axis=-1)
        expert_weights, expert_indices = jax.lax.top_k(scores, K)
        h = jax.nn.silu(jnp.einsum('td,edh->eth', xf, w1)) * jnp.einsum('td,edh->eth', xf, w3)
        y = jnp.einsum('eth,ehd->etd', h, w2)
        y_t = jnp.swapaxes(y, 0, 1)
        sel = jnp.take_along_axis(y_t, expert_indices[:, :, None], axis=1)
        out = jnp.sum(expert_weights[:, :, None] * sel, axis=1)
        return out.reshape(bsz, seqlen, dim)
    x = L0_attn_x
    mod = (_silu(L0_c) @ L0_wmod).reshape(L0_c.shape[0], 6, 1, -1)
    sa, ca, ga, sb, cb, gb = (mod[:, 0], mod[:, 1], mod[:, 2], mod[:, 3], mod[:, 4], mod[:, 5])
    ga = (2 * (ga >= 0) - 1) * jnp.maximum(jnp.abs(ga), 0.25)
    gb = (2 * (gb >= 0) - 1) * jnp.maximum(jnp.abs(gb), 0.25)
    h = _layernorm(x, axis=-1) * (1 + ca) + sa
    x = x + ga * _L0_attn_ref(h, L0_attn_w_qkv, L0_attn_w_out, L0_attn_bandha_gate)
    h = _layernorm(x, axis=-1) * (1 + cb) + sb
    x = x + gb * _L0_ffn_ref(h, L0_ffn_gate_w, L0_ffn_gate_bias, L0_ffn_w_gate, L0_ffn_w_up, L0_ffn_w_down)
    mod = (_silu(L1_c) @ L1_wmod).reshape(L1_c.shape[0], 6, 1, -1)
    sa, ca, ga, sb, cb, gb = (mod[:, 0], mod[:, 1], mod[:, 2], mod[:, 3], mod[:, 4], mod[:, 5])
    ga = (2 * (ga >= 0) - 1) * jnp.maximum(jnp.abs(ga), 0.25)
    gb = (2 * (gb >= 0) - 1) * jnp.maximum(jnp.abs(gb), 0.25)
    h = _layernorm(x, axis=-1) * (1 + ca) + sa
    x = x + ga * _L1_attn_ref(h, L1_attn_Wq, L1_attn_Wk, L1_attn_Wv, L1_attn_Wo, L1_attn_lambda_q1, L1_attn_lambda_k1, L1_attn_lambda_q2, L1_attn_lambda_k2, L1_attn_rms_scale)
    h = _layernorm(x, axis=-1) * (1 + cb) + sb
    x = x + gb * _L1_ffn_ref(h, L1_ffn_Wfc_s, L1_ffn_bfc_s, L1_ffn_Wproj_s, L1_ffn_bproj_s, L1_ffn_Wr, L1_ffn_Wfc, L1_ffn_bfc, L1_ffn_Wproj, L1_ffn_bproj)
    mod = (_silu(L2_c) @ L2_wmod).reshape(L2_c.shape[0], 6, 1, -1)
    sa, ca, ga, sb, cb, gb = (mod[:, 0], mod[:, 1], mod[:, 2], mod[:, 3], mod[:, 4], mod[:, 5])
    ga = (2 * (ga >= 0) - 1) * jnp.maximum(jnp.abs(ga), 0.25)
    gb = (2 * (gb >= 0) - 1) * jnp.maximum(jnp.abs(gb), 0.25)
    h = _layernorm(x, axis=-1) * (1 + ca) + sa
    x = x + ga * _L2_attn_ref(h, L2_attn_Wq, L2_attn_bq, L2_attn_Wk, L2_attn_Wv, L2_attn_bv, L2_attn_Wo, L2_attn_bo)
    h = _layernorm(x, axis=-1) * (1 + cb) + sb
    x = x + gb * _L2_ffn_ref(h, L2_ffn_g1, L2_ffn_g2, L2_ffn_wq, L2_ffn_wk, L2_ffn_wv, L2_ffn_wo, L2_ffn_gate, L2_ffn_w1, L2_ffn_w2, L2_ffn_w3)
    mod = (_silu(L3_c) @ L3_wmod).reshape(L3_c.shape[0], 6, 1, -1)
    sa, ca, ga, sb, cb, gb = (mod[:, 0], mod[:, 1], mod[:, 2], mod[:, 3], mod[:, 4], mod[:, 5])
    ga = (2 * (ga >= 0) - 1) * jnp.maximum(jnp.abs(ga), 0.25)
    gb = (2 * (gb >= 0) - 1) * jnp.maximum(jnp.abs(gb), 0.25)
    h = _layernorm(x, axis=-1) * (1 + ca) + sa
    x = x + ga * _L3_attn_ref(h, L3_attn_ln1_w, L3_attn_ln1_b, L3_attn_wq, L3_attn_bq, L3_attn_wk, L3_attn_bk, L3_attn_wv, L3_attn_bv, L3_attn_wo, L3_attn_bo, L3_attn_ln2_w, L3_attn_ln2_b, L3_attn_fc_w, L3_attn_fc_b, L3_attn_proj_w, L3_attn_proj_b)
    h = _layernorm(x, axis=-1) * (1 + cb) + sb
    x = x + gb * _L3_ffn_ref(h, L3_ffn_w_router, L3_ffn_w1, L3_ffn_w2, L3_ffn_w3)
    return x

_drawn_inputs = setup_inputs


def setup_inputs(seed=0):
    import zlib

    import numpy as np

    out = dict(_drawn_inputs(seed))
    spreads = {'L1_attn_rms_scale': (1.0, 0.6),
     'L1_ffn_bfc_s': (0.0, 0.8),
     'L1_ffn_bproj_s': (0.0, 0.313),
     'L1_ffn_bfc': (0.0, 0.8),
     'L1_ffn_bproj': (0.0, 0.441),
     'L2_ffn_g1': (1.0, 0.6),
     'L2_ffn_g2': (1.0, 0.6),
     'L3_attn_ln1_w': (1.0, 0.6),
     'L3_attn_ln1_b': (0.0, 0.8),
     'L3_attn_bq': (0.0, 2.0),
     'L3_attn_bk': (0.0, 2.0),
     'L3_attn_bv': (0.0, 0.8),
     'L3_attn_bo': (0.0, 0.291),
     'L3_attn_ln2_w': (1.0, 0.6),
     'L3_attn_ln2_b': (0.0, 0.456),
     'L3_attn_fc_b': (0.0, 0.489),
     'L3_attn_proj_b': (0.0, 0.376)}
    factors = {'L0_attn_bandha_gate': 4.388,
     'L1_ffn_Wfc_s': 4.29,
     'L1_ffn_Wproj_s': 3.84,
     'L1_ffn_Wr': 3.182,
     'L1_ffn_Wfc': 6.007,
     'L1_ffn_Wproj': 5.471,
     'L2_attn_Wq': 8.0,
     'L2_attn_bq': 8.0,
     'L2_attn_Wk': 8.0,
     'L2_attn_Wv': 8.0,
     'L2_attn_bv': 8.0,
     'L2_attn_Wo': 8.0,
     'L2_attn_bo': 8.0,
     'L2_ffn_wq': 8.0,
     'L2_ffn_wk': 8.0,
     'L2_ffn_wv': 8.0,
     'L2_ffn_wo': 8.0,
     'L2_ffn_gate': 8.0,
     'L2_ffn_w1': 8.0,
     'L2_ffn_w2': 8.0,
     'L2_ffn_w3': 8.0,
     'L3_attn_wq': 4.744,
     'L3_attn_wk': 2.701,
     'L3_ffn_w_router': 8.0,
     'L3_ffn_w1': 8.0,
     'L3_ffn_w2': 8.0,
     'L3_ffn_w3': 8.0}
    for name, (base, spread) in spreads.items():
        noise = np.random.default_rng([zlib.crc32(name.encode()), seed]).standard_normal(out[name].shape)
        drawn = base * np.exp(spread * noise) if base else spread * noise
        out[name] = jnp.asarray(drawn.astype(out[name].dtype))
    for name, factor in factors.items():
        out[name] = (out[name] * factor).astype(out[name].dtype)
    return out
```

```python
from contextlib import ExitStack

import numpy as np
import concourse.bass as bass
from concourse import mybir

P = 128
F32 = mybir.dt.float32
BF16 = mybir.dt.bfloat16
ALU = mybir.AluOpType
ACT = mybir.ActivationFunctionType
AX = mybir.AxisListType.X

NB, T, D = 16, 256, 128
NTOK = NB * T
HD = 8
NEG = -1.0e30
PAIRS = [(0, 0), (0, 1), (1, 0), (0, 2), (2, 0), (1, 1)]
ROWS = HD * len(PAIRS)
MROW = 66
KROWS = MROW + 3

C_ID, C_MEAN, C_MQ, C_MK, C_TRI, C_COS, C_SIN = 0, 128, 256, 384, 512, 640, 896
C_END = C_SIN + T


def constants():
    c = np.zeros((P, C_END), np.float32)
    i = np.arange(P)
    c[:, C_ID:C_ID + P] = np.eye(P)
    c[:, C_MEAN:C_MEAN + P] = 1.0 / D
    c[:, C_MQ:C_MQ + P] = np.where(i[None, :] > i[:, None], NEG, 0.0)
    c[:, C_MK:C_MK + P] = np.where(i[:, None] > i[None, :], NEG, 0.0)
    c[:, C_TRI:C_TRI + P] = (i[:, None] < i[None, :])
    freq = (1.0 / 10000.0 ** (np.arange(0, HD, 2, dtype=np.float32) / HD)).astype(np.float32)
    ang = (np.arange(T, dtype=np.float32)[None, :] * freq[:, None]).astype(np.float32)
    cos, sin = np.cos(ang), np.sin(ang)
    for r in range(P):
        d = r // 16 % HD
        c[r, C_COS:C_COS + T] = cos[d % 4]
        c[r, C_SIN:C_SIN + T] = sin[d % 4] * (-1.0 if d < 4 else 1.0)
    return c


class Chip:

    def __init__(self, nc, ctx, ins):
        self.nc, self.ctx, self.ins = nc, ctx, ins
        self.sems, self.free = {}, []
        self.XT = self.sb("XT", [P, NTOK])
        self.HT = self.sb("HT", [P, NTOK])
        self.CST = self.sb("CST", [P, C_END])
        self.IDB = self.sb("IDB", [P, P], BF16)
        self.MASKS = self.sb("MASKS", [P, 2, 2, P], BF16)
        self.MOD = self.sb("MOD", [P, 4, 6, NB])
        self.HALF = self.sb("HALF", [P, 64])
        self.ONES = self.sb("ONES", [P, P])
        self.counts = {k: 0 for k in ("in", "act", "step", "run", "pos", "val", "t", "hi", "res", "mid", "lo", "z", "tm")}
        self.bank = [ctx.enter_context(nc.psum_tensor(f"bank{i}", [P, 512], F32)) for i in range(8)]
        self.ID = self.CST[:, C_ID:C_ID + P]
        self.MEAN = self.CST[:, C_MEAN:C_MEAN + P]

    def sb(self, name, shape, dt=F32, ctx=None):
        return (ctx or self.ctx).enter_context(self.nc.sbuf_tensor(name, shape, dt))

    def sem(self, name):
        if name not in self.sems:
            self.sems[name] = self.ctx.enter_context(self.nc.semaphore(name))
        return self.sems[name]


def start_phase(c, x_in):
    nc, b = c.nc, c.bank
    G = 4
    NG = NTOK // (G * P)
    with ExitStack() as ctx:
        WM = c.sb("WM", [P, 4, 6 * D], ctx=ctx)
        CT = c.sb("CTm", [P, 4, NB], ctx=ctx)
        SC = c.sb("SCm", [P, 4, NB], ctx=ctx)
        SG = c.sb("SGm", [P, 4, 2, NB], ctx=ctx)
        AG = c.sb("AGm", [P, 4, 2, NB], ctx=ctx)
        XS = c.sb("XS", [P, NG, G, D], ctx=ctx)
        const_in, mod_in, x_landed = c.sem("const_in"), c.sem("mod_in"), [c.sem(f"landed{g}") for g in range(NG)]
        const_ready, silu_ready, mod_mm, mod_copied, mod_done, sign_done = (
            c.sem(n) for n in ("const_ready", "silu_ready", "mod_mm", "mod_copied", "mod_done", "sign_done"))
        x_turned, x_copied = c.sem("x_turned"), c.sem("x_copied")
        xv = x_in.rearrange("b (g p) d -> p (b g) d", p=P)
        block = ctx.enter_context(nc.Block())

        @block.sync
        def _(sp):
            sp.dma_start(c.CST[:, :], c.ins["consts"]).then_inc(const_in, 16)
            for g in range(NG):
                sp.dma_start(XS[:, g, :, :], xv[:, g * G:(g + 1) * G, :]).then_inc(x_landed[g], 16)

        @block.scalar
        def _(act):
            for l in range(4):
                act.dma_start(CT[:, l, :], c.ins[f"cT{l}"]).then_inc(mod_in, 16)
                act.dma_start(WM[:, l, :], c.ins[f"wmod{l}"]).then_inc(mod_in, 16)
            act.wait_ge(mod_in, 16 * 8)
            nc.scalar.activation(SC[:, :, :], CT[:, :, :], ACT.Silu).then_inc(silu_ready, 1)

        @block.gpsimd
        def _(pool):
            nc.gpsimd.memset(c.HALF[:, :], -0.5).then_inc(const_ready, 1)
            nc.gpsimd.memset(c.ONES[:, :], 1.0).then_inc(const_ready, 1)

        @block.tensor
        def _(pe):
            pe.wait_ge(const_in, 16)
            for g in range(NG):
                pe.wait_ge(x_landed[g], 16)
                if g >= 2:
                    pe.wait_ge(x_copied, g - 1)
                for k in range(G):
                    m = pe.transpose(b[g % 2][:, k * P:(k + 1) * P], XS[:, g, k, :], c.ID)
                m.then_inc(x_turned, 1)
            pe.wait_ge(silu_ready, 1)
            for l in range(4):
                for j in range(6):
                    m = pe.matmul(b[2][:, (l * 6 + j) * NB:(l * 6 + j + 1) * NB],
                                  WM[:, l, j * D:(j + 1) * D], SC[:, l, :], start=True, stop=True)
            m.then_inc(mod_mm, 1)

        @block.vector
        def _(v):
            v.wait_ge(const_in, 16)
            v.tensor_copy(c.IDB[:, :], c.ID).then_inc(const_ready, 1)
            for k in range(2):
                v.tensor_copy(c.MASKS[:, 0, k, :], c.CST[:, C_MQ:C_MQ + P]).then_inc(const_ready, 1)
                v.tensor_copy(c.MASKS[:, 1, k, :], c.CST[:, C_MK:C_MK + P]).then_inc(const_ready, 1)
            for g in range(NG):
                v.wait_ge(x_turned, g + 1)
                v.tensor_copy(c.XT[:, g * G * P:(g + 1) * G * P], b[g % 2][:, :]).then_inc(x_copied, 1)
            v.wait_ge(mod_mm, 1)
            v.tensor_copy(c.MOD[:, :, :, :].rearrange("p l j b -> p (l j b)"), b[2][:, 0:24 * NB]).then_inc(mod_copied, 1)
            v.wait_ge(mod_copied, 1)
            for n, j in enumerate((2, 5)):
                g = c.MOD[:, :, j, :]
                v.scalar_tensor_tensor(AG[:, :, n, :], g, -1.0, g, ALU.mult, ALU.max).then_inc(sign_done, 1)
                v.tensor_scalar(SG[:, :, n, :], g, 0.0, 2.0, ALU.is_ge, ALU.mult).then_inc(sign_done, 1)
                v.wait_ge(sign_done, 4 * n + 2)
                v.tensor_scalar(SG[:, :, n, :], SG[:, :, n, :], -1.0, None, ALU.add).then_inc(sign_done, 1)
                v.tensor_scalar(AG[:, :, n, :], AG[:, :, n, :], 0.25, None, ALU.max).then_inc(sign_done, 1)
                v.wait_ge(sign_done, 4 * n + 4)
                v.tensor_tensor(g, AG[:, :, n, :], SG[:, :, n, :], ALU.mult).then_inc(mod_done, 1)
            for j in (1, 4):
                v.tensor_scalar(c.MOD[:, :, j, :], c.MOD[:, :, j, :], 1.0, None, ALU.add).then_inc(mod_done, 1)


def end_phase(c, out):
    nc, b = c.nc, c.bank
    G = 4
    NG = NTOK // (G * P)
    ov = out.rearrange("b (g p) d -> p (b g) d", p=P)
    with ExitStack() as ctx:
        XS = c.sb("XO", [P, NG, G, D], ctx=ctx)
        o_turned, o_copied, o_out = c.sem("o_turned"), c.sem("o_copied"), c.sem("o_out")
        block = ctx.enter_context(nc.Block())

        @block.tensor
        def _(pe):
            for g in range(NG):
                if g >= 2:
                    pe.wait_ge(o_copied, g - 1)
                for k in range(G):
                    t = g * G + k
                    m = pe.transpose(b[g % 2][:, k * P:(k + 1) * P], c.XT[:, t * P:(t + 1) * P], c.ID)
                m.then_inc(o_turned, 1)

        @block.vector
        def _(v):
            for g in range(NG):
                v.wait_ge(o_turned, g + 1)
                v.tensor_copy(XS[:, g, :, :].rearrange("p k d -> p (k d)"), b[g % 2][:, :]).then_inc(o_copied, 1)

        @block.sync
        def _(sp):
            for g in range(NG):
                sp.wait_ge(o_copied, g + 1)
                sp.dma_start(ov[:, g * G:(g + 1) * G, :], XS[:, g, :, :]).then_inc(o_out, 16)
            sp.wait_ge(o_out, 16 * NG)


class Signal:

    def __init__(self, sem):
        self.sem, self.base, self.per = sem, 0, 1

    def value(self, b, k=None):
        return b * self.per + (self.base + (self.per if k is None else k))


def after(eng, signal, b, k=None):
    value = signal.value(b, k)
    if not isinstance(value, int) or value > 0:
        eng.wait_ge(signal.sem, value)


def signals(c, **per):
    found = []
    for name, n in per.items():
        s = c.free.pop() if c.free else Signal(c.sem(name))
        s.per = n
        found.append(s)
    return found


def close(c, found, n=NB):
    for s in found:
        s.base += n * s.per
    c.free.extend(reversed(found))


def attention_phase(c, cfg):
    nc, bank = c.nc, c.bank
    NH, HK, HV, VW = cfg["NH"], cfg["HK"], cfg["HV"], cfg["VW"]
    causal, rope, diff = cfg["causal"], cfg.get("rope"), cfg.get("diff")
    centered, eps = cfg["centered"], cfg["eps"]
    R = NH // 16
    KR = HD * min(HK, 16)
    QK = 2 if rope else R
    U = NH // 16
    DF = int(bool(diff))
    NS = NH // 4
    R2 = cfg["CW"] // P
    OW = VW + 1
    kof = lambda h: h * HK // NH
    vof = lambda h: h * HV // NH
    NC = 3 * P if causal else 4 * P
    SCALE = float(HD) ** -0.5
    l = cfg["layer"]
    SRC, DST = cfg["src"], cfg["dst"]

    with ExitStack() as ctx:
        sb = lambda name, shape, dt=F32: c.sb(cfg["name"] + name, shape, dt, ctx)
        QH = sb("QH", [KROWS, 3, NH, T], BF16)
        KH = sb("KH", [KROWS, 3, HK, T], BF16)
        VX = sb("VX", [P, 3, 2, HV, 32])
        PR = sb("PR", [P, 4, NC])
        XC, SQ, XN, H = (sb(n, [P, T]) for n in ("XC", "SQ", "XN", "H"))
        VE, RS, DG = sb("VE", [P, 2]), sb("RS", [P, 2]), sb("DG", [P, 2, P])
        QKF = sb("QKF", [P, 2, T])
        RES = sb("RES", [P, 2, T])
        SPL = sb("SPL", [P, R, 3, 2, T], BF16)
        NM3 = sb("NM3", [P, NH, 3])
        NMQ = sb("NMQ", [P, 2, NH])
        MF, MR = sb("MF", [NH, T]), sb("MR", [NH, T])
        M3 = sb("M3", [NH, 3, T], BF16)
        CTS = sb("CTS", [P, 2, T])
        RC = sb("RC", [P, 2, 4])
        CX = sb("CX", [P, 3, 2, cfg["CW"] // VW, VW])
        CTT = sb("CTT", [P, R2, T])
        TMP = sb("TMP", [P, T])
        ONE = sb("ONE", [3, T], BF16)
        WQ = sb("WQ", [P, (2 if rope else 1) * R * P])
        WK = sb("WK", [P, (2 if rope else 1) * (R * P if HK > 1 else HD)])
        WV = sb("WV", [P, HV * VW])
        WO = sb("WO", [P, R2, D])
        COL = sb("COL", [P, 4])
        if cfg.get("bv"):
            BV = sb("BV", [P, HV * VW])
        if cfg.get("gate"):
            HM, OH, SG, SGM, GATE = sb("HM", [P, P]), sb("OH", [P, T]), sb("SG", [P, 1]), sb("SGM", [P, P]), sb("GATE", [P, T])
        if diff:
            CX2 = sb("CX2", [P, 2, 4, VW])
            LQ = sb("LQ", [P, 4, 16, HD])
            LS, LE, NLAM = sb("LS", [P, 2, 16]), sb("LE", [P, 2, 16]), sb("NLAM", [P, 16])
            CSQ = sb("CSQ", [P, 2, 16, VW])
            CM, CR = sb("CM", [P, 2, 16]), sb("CR", [P, 2, 16])

        w_in, ones_in, zeroed, vx_ones, sg_ready, sgm_ready, gate_mm, gate_ready, ls_ready, le_ready, lam_ready = (
            c.sem(cfg["name"][0:2] + n) if n in ("w_in", "ones_in", "zeroed", "vx_ones") else c.sem(n)
            for n in ("w_in", "ones_in", "zeroed", "vx_ones", "sg_ready", "sgm_ready", "gate_mm", "gate_ready",
                      "ls_ready", "le_ready", "lam_ready"))
        S = signals(c, mean_ready=int(centered), xc_ready=int(centered), sq_ready=1, var_ready=1, ve_ready=1, rs_ready=1, dg_ready=1, bc_ready=1,
                    xn_ready=1, h_ready=1, qk_ready=QK, qk_copied=QK, half_ready=int(bool(rope)), rope_ready=int(bool(rope)),
                    hi_ready=R, res_ready=R, mid_ready=R, lo_ready=R, parts_sent=16 * 12, parts_sent_1=16 * 12 * (R - 1),
                    v_ready=1, v_copied=1, s_ready=NH, s_used=NH, nmq_ready=2 * int(causal), mt_ready=1, mf_ready=1,
                    mhi_ready=1, mres_ready=1, mmid_ready=1, mlo_ready=1, m_sent=16 * 3,
                    st_ready=NH, p_ready=NH, pv_done=NH, ct_ready=NS, t_ready=NS, rc_ready=NS, cx_ready=NS,
                    dif_ready=2 * NS * DF, csq_ready=DF, cm_ready=2 * DF, cr_ready=DF, cxn_ready=DF,
                    ctt_ready=1, ctt_copied=1, o_ready=1, tmp_ready=1, x_updated=1)
        (mean_ready, xc_ready, sq_ready, var_ready, ve_ready, rs_ready, dg_ready, bc_ready, xn_ready, h_ready, qk_ready,
         qk_copied, half_ready, rope_ready, hi_ready, res_ready, mid_ready, lo_ready, parts_sent_0, parts_sent_1,
         v_ready, v_copied, s_ready, s_used, nmq_ready, mt_ready, mf_ready, mhi_ready, mres_ready,
         mmid_ready, mlo_ready, m_sent, st_ready, p_ready, pv_done, ct_ready, t_ready, rc_ready,
         cx_ready, dif_ready, csq_ready, cm_ready, cr_ready, cxn_ready, ctt_ready, ctt_copied,
         o_ready, tmp_ready, x_updated) = S
        parts_sent = (parts_sent_0, parts_sent_1)[:R]
        f_ready = rope_ready if rope else qk_copied

        loads = [(WQ[:, :], cfg["wq"]), (WK[:, :], cfg["wk"]), (WV[:, :], cfg["wv"]),
                 (WO[:, :, :].rearrange("p r d -> p (r d)"), cfg["wo"])]
        for n, key in enumerate(("bq", "bo", "cscale", "gain")):
            loads.append((COL[:, n:n + 1], cfg.get(key) or "zero"))
        if cfg.get("bv"):
            loads.append((BV[:, :], cfg["bv"]))
        if cfg.get("gate"):
            loads += [(HM[:, :], "headmask"), (OH[:, :], "phases"), (SG[:, :], cfg["gate"])]
        if diff:
            loads += [(LQ[:, n, :, :].rearrange("p h d -> p (h d)"), f"lam{n}") for n in range(4)]
        NW = 16 * len(loads)
        has = lambda stage, t: not isinstance(t, int) or 0 <= t + stage < NB
        tok = lambda b: slice(b * T, (b + 1) * T) if isinstance(b, int) else bass.ds(b * T, T)
        one = lambda b: slice(b, b + 1) if isinstance(b, int) else bass.ds(b, 1)

        def steps(eng, step):
            for t in range(-2, 2):
                step(t, t % 3)
            with eng.Fori(0, 4) as i:
                for k in range(2, 5):
                    step(i * 3 + k, k % 3)
            for t in range(14, 17):
                step(t, t % 3)

        L_MEAN, L_VAR, L_POW, L_DG, L_BC, L_XN, L_QK, L_V = 0, 2 * U, 2 * U, 3 * U, 4 * U, 5 * U, 6 * U, 11 * U
        L_SPLIT = [10] if rope else [L_QK + 2 + 2 * r * U for r in range(R)]
        L_SCORES = 2
        L_NMQ = L_SCORES + NH // 2
        L_MT = L_NMQ
        L_MSPLIT = L_MT + 1
        L_LAST, L_COMBINE = 1, 2
        L_CTT, L_OUT, L_TMP = (9, 10, 10) if diff else (3, 4, 5)
        out_at = int(bool(diff))
        turn_at = {4 * s + 7: s for s in range(NS - 1)}
        S_MT = (L_MT - 8) // 4

        nc.disable_value_cache = True
        block = ctx.enter_context(nc.Block())

        @block.sync
        def _(sp):
            for dst, src in loads:
                sp.dma_start(dst, c.ins[src]).then_inc(w_in, 16)
            sp.wait_ge(zeroed, 5)
            for j in range(3):
                sp.dma_start(KH[MROW:KROWS, j, :, :], ONE[:, :].unsqueeze(1).to_broadcast([3, HK, T])).then_inc(ones_in, 16)

            def send_maxima(t, m):
                after(sp, mlo_ready, t + 1)
                for a in range(3):
                    sp.dma_start(QH[MROW + a:MROW + a + 1, (m + 1) % 3, :, :], M3[:, a, :]).then_inc(m_sent.sem, 16)

            def step(t, m):
                if not has(2, t) and has(1, t):
                    send_maxima(t, m)
                if has(2, t):
                    b, j = t + 2, (m + 2) % 3
                    for r in range(R):
                        after(sp, pv_done, b - 3)
                        for a, ready in enumerate((hi_ready, mid_ready, lo_ready)):
                            if has(1, t) and r == R - 1 and a == 2:
                                send_maxima(t, m)
                            after(sp, ready, b, r + 1)
                            for n, pair in enumerate(PAIRS):
                                rows = slice(HD * n, HD * n + HD)
                                if pair[0] == a:
                                    sp.dma_start(QH[rows, j, 16 * r:16 * r + 16, :], SPL[:, r, a, 0, :]).then_inc(parts_sent[r].sem, 16)
                                if pair[1] == a:
                                    sp.dma_start(KH[rows, j, 16 * r:16 * r + min(HK, 16), :], SPL[0:KR, r, a, 1, :]).then_inc(parts_sent[r].sem, 16)
            steps(sp, step)

        @block.gpsimd
        def _(pool):
            nc.gpsimd.memset(KH[:, :, :, :].rearrange("p j h t -> p (j h t)").bitcast(F32), 0.0).then_inc(zeroed, 1)
            nc.gpsimd.memset(ONE[:, :], 1.0).then_inc(zeroed, 1)
            nc.gpsimd.memset(VX[:, :, :, :, :], 0.0).then_inc(zeroed, 1)
            nc.gpsimd.memset(QKF[:, :, :], 0.0).then_inc(zeroed, 1)

            def step(t, m):
                for h in range(NH):
                    if has(2, t):
                        b = t + 2
                        if h == L_POW:
                            after(pool, ve_ready, b)
                            after(pool, dg_ready, b - 1)
                            nc.gpsimd.tensor_tensor(RS[:, :], VE[:, :], c.HALF[:, 0:2], ALU.pow).then_inc(rs_ready.sem, 1)
                        for n in range(2 if rope else 0):
                            if h == L_QK + 1 + 2 * n:
                                after(pool, qk_copied, b, n + 1)
                                nc.gpsimd.tensor_tensor(QKF[:, n, :], RES[:, 0, :], RES[:, 1, :], ALU.add)\
                                    .then_inc((half_ready, rope_ready)[n].sem, 1)
                        for r in range(R):
                            if h == L_SPLIT[r]:
                                after(pool, hi_ready, b, r + 1)
                                after(pool, lo_ready, b, r)
                                nc.gpsimd.tensor_tensor(RES[:, :, :], QKF[:, :, :], SPL[:, r, 0, :, :], ALU.subtract)\
                                    .then_inc(res_ready.sem, 1)
                                after(pool, mid_ready, b, r + 1)
                                nc.gpsimd.tensor_tensor(SPL[:, r, 2, :, :], RES[:, :, :], SPL[:, r, 1, :, :], ALU.subtract)\
                                    .then_inc(lo_ready.sem, 1)
                    if has(1, t) and h == L_MSPLIT:
                        b = t + 1
                        after(pool, mhi_ready, b)
                        nc.gpsimd.tensor_tensor(MR[:, :], MF[:, :], M3[:, 0, :], ALU.subtract).then_inc(mres_ready.sem, 1)
                        after(pool, mmid_ready, b)
                        nc.gpsimd.tensor_tensor(M3[:, 2, :], MR[:, :], M3[:, 1, :], ALU.subtract).then_inc(mlo_ready.sem, 1)
                    if diff and has(-1, t) and h == L_COMBINE:
                        after(pool, cm_ready, t - 1)
                        nc.gpsimd.tensor_tensor(CR[:, :, :].rearrange("p a h -> p (a h)"), CM[:, :, :].rearrange("p a h -> p (a h)"),
                                                c.HALF[:, 0:32], ALU.pow).then_inc(cr_ready.sem, 1)
            steps(pool, step)

        @block.scalar
        def _(act):
            if cfg.get("gate"):
                act.wait_ge(w_in, NW)
                nc.scalar.activation(SG[:, :], SG[:, :], ACT.Sigmoid).then_inc(sg_ready, 1)
            if diff:
                act.wait_ge(ls_ready, 2)
                nc.scalar.activation(LE[:, :, :], LS[:, :, :], ACT.Exp).then_inc(le_ready, 1)

            def copy_set(b, s):
                after(act, pv_done, b, 4 * s + 4)
                after(act, t_ready, b, s - 1)
                nc.scalar.copy(CTS[:, s % 2, :], bank[4 + s % 2][:, 0:T]).then_inc(ct_ready.sem, 1)

            def step(t, m):
                for h in range(NH):
                    if has(2, t):
                        b = t + 2
                        if h == L_MEAN:
                            if centered:
                                after(act, xc_ready, b)
                            after(act, var_ready, b - 1)
                            nc.scalar.activation(SQ[:, :], XC[:, :] if centered else SRC[:, tok(b)], ACT.Square)\
                                .then_inc(sq_ready.sem, 1)
                        if h == L_XN:
                            after(act, xn_ready, b)
                            after(act, v_ready, b - 1)
                            scale, shift = (c.MOD[:, l, 1, one(b)], c.MOD[:, l, 0, one(b)]) if centered else (COL[:, 3:4], 0.0)
                            nc.scalar.activation(H[:, :], XN[:, :], ACT.Identity, bias=shift, scale=scale).then_inc(h_ready.sem, 1)
                        if h == L_V + 1 and not cfg.get("bv"):
                            after(act, v_ready, b)
                            after(act, pv_done, b - 3)
                            nc.scalar.copy(VX[:, (m + 2) % 3, :, :, 0:VW],
                                           bank[6][:, 0:2 * HV * VW].rearrange("p (n h d) -> p n h d", n=2, h=HV)).then_inc(v_copied.sem, 1)
                        for r in range(R):
                            if h == L_SPLIT[r]:
                                after(act, f_ready, b, None if rope else r + 1)
                                after(act, parts_sent[r], b - 1)
                                nc.scalar.copy(SPL[:, r, 0, :, :], QKF[:, :, :]).then_inc(hi_ready.sem, 1)
                            if h == L_SPLIT[r] + 1:
                                after(act, res_ready, b, r + 1)
                                nc.scalar.copy(SPL[:, r, 1, :, :], RES[:, :, :]).then_inc(mid_ready.sem, 1)
                    if has(1, t) and h == L_MSPLIT:
                        b = t + 1
                        after(act, mt_ready, b)
                        after(act, mlo_ready, b - 1)
                        nc.scalar.copy(MF[:, :], bank[7][0:NH, 0:T]).then_inc(mf_ready.sem, 1)
                        after(act, mf_ready, b)
                        after(act, m_sent, b - 1)
                        nc.scalar.copy(M3[:, 0, :], MF[:, :]).then_inc(mhi_ready.sem, 1)
                    if has(1, t) and h == L_MSPLIT + 1:
                        after(act, mres_ready, t + 1)
                        nc.scalar.copy(M3[:, 1, :], MR[:, :]).then_inc(mmid_ready.sem, 1)
                    if has(-1, t):
                        b = t - 1
                        if diff and h == L_COMBINE:
                            after(act, dif_ready, b)
                            nc.scalar.activation(CSQ[:, :, :, :], CX[:, (m - 1) % 3, :, :, :], ACT.Square).then_inc(csq_ready.sem, 1)
                        if h == L_CTT:
                            after(act, ctt_ready, b)
                            after(act, o_ready, b - 1)
                            nc.scalar.activation(CTT[:, :, :].rearrange("p r t -> p (r t)"), bank[7][:, 0:R2 * T], ACT.Identity,
                                                 scale=COL[:, 2:3] if diff else 1.0).then_inc(ctt_copied.sem, 1)
                    if has(0, t):
                        after(act, st_ready, t, h + 1)
                        after(act, pv_done, t, h - 3)
                        nc.scalar.activation(PR[:, h % 4, :], bank[2 + h % 2][:, 0:NC], ACT.Exp, scale=SCALE)\
                            .then_inc(p_ready.sem, 1)
                        if h >= 6 and (h - 6) % 4 == 0:
                            copy_set(t, (h - 6) // 4)
                if has(0, t):
                    copy_set(t, NS - 1)
            steps(act, step)

        @block.tensor
        def _(pe):
            pe.wait_ge(w_in, NW)
            pe.wait_ge(ones_in, 48)
            pe.wait_ge(vx_ones, 1)
            if cfg.get("gate"):
                pe.wait_ge(sgm_ready, 1)
                pe.matmul(bank[6][:, 0:T], SGM[:, :], OH[:, :], start=True, stop=True).then_inc(gate_mm, 1)
                pe.wait_ge(gate_ready, 1)

            def scores(b, j, h):
                after(pe, s_used, b, h - 1)
                if h % 16 == 0:
                    after(pe, parts_sent[h // 16], b)
                o = bank[h % 2]
                q = lambda n: QH[0:MROW, j, h, n * P:(n + 1) * P]
                k = KH[0:MROW, j, kof(h), :]
                if causal:
                    pe.matmul(o[:, :].rearrange("p (n x) -> p n x", n=2)[:, :, 0:P], c.IDB[:, :], c.MASKS[:, 0, :, :],
                              start=True, stop=False, skip_group_check=True)
                    pe.matmul(o[:, 0:P], q(0), k[:, 0:P], start=False, stop=False, skip_group_check=True)
                    mm = pe.matmul(o[:, P:3 * P], q(1), k, start=False, stop=True, skip_group_check=True)
                else:
                    pe.matmul(o[:, 0:T], q(0), k, start=True, stop=True)
                    mm = pe.matmul(o[:, T:2 * T], q(1), k, start=True, stop=True)
                mm.then_inc(s_ready.sem, 1)

            def scores_t(b, j, h):
                after(pe, p_ready, b, h - 1)
                if h == 0:
                    after(pe, m_sent, b)
                o = bank[2 + h % 2]
                k = lambda n: KH[0:KROWS, j, kof(h), n * P:(n + 1) * P]
                q = QH[0:KROWS, j, h, :]
                if causal:
                    pe.matmul(o[:, :].rearrange("p (n x) -> p n x", n=2)[:, :, 0:P], c.IDB[:, :], c.MASKS[:, 1, :, :],
                              start=True, stop=False, skip_group_check=True)
                    pe.matmul(o[:, 0:T], k(0), q, start=False, stop=False, skip_group_check=True)
                    mm = pe.matmul(o[:, T:3 * P], k(1), q[:, P:T], start=False, stop=True, skip_group_check=True)
                else:
                    pe.matmul(o[:, 0:T], k(0), q, start=True, stop=True)
                    mm = pe.matmul(o[:, T:2 * T], k(1), q, start=True, stop=True)
                mm.then_inc(st_ready.sem, 1)

            def values(b, j, h):
                g, s = h % 4, h // 4
                after(pe, p_ready, b, h + 1)
                if g == 0:
                    after(pe, ct_ready, b, s - 1)
                o = bank[4 + s % 2][32 * g:32 * g + 32, :]
                v = lambda n: VX[:, j, n, vof(h), :]
                pe.matmul(o[:, 0:T], v(0), PR[:, h % 4, 0:T], start=True, stop=False)
                rest = (o[:, P:T], PR[:, h % 4, T:3 * P]) if causal else (o[:, 0:T], PR[:, h % 4, T:2 * T])
                pe.matmul(rest[0], v(1), rest[1], start=False, stop=True).then_inc(pv_done.sem, 1)

            def turn(b, s):
                after(pe, ct_ready, b, s + 1)
                for n in range(2):
                    mm = pe.transpose(bank[7][:, n * P:(n + 1) * P], CTS[:, s % 2, n * P:(n + 1) * P], c.ID)
                mm.then_inc(t_ready.sem, 1)

            def step(t, m):
                for h in range(NH):
                    if has(2, t):
                        b = t + 2
                        if h == L_MEAN and centered:
                            after(pe, v_copied, b - 1)
                            pe.matmul(bank[6][:, 0:T], c.MEAN, SRC[:, tok(b)], start=True, stop=True).then_inc(mean_ready.sem, 1)
                        if h == L_VAR:
                            after(pe, v_copied, b - 1)
                            after(pe, sq_ready, b)
                            for n in range(2):
                                mm = pe.matmul(bank[6][:, T + n:T + n + 1], SQ[:, n * P:(n + 1) * P], c.MEAN[:, 0:1],
                                               start=True, stop=True)
                            mm.then_inc(var_ready.sem, 1)
                        if h == L_BC:
                            after(pe, dg_ready, b)
                            for n in range(2):
                                mm = pe.matmul(bank[6][:, T + n * P:T + (n + 1) * P], c.ONES[:, :], DG[:, n, :], start=True, stop=True)
                            mm.then_inc(bc_ready.sem, 1)
                        for n in range(QK):
                            if h == L_QK + 2 * n * U:
                                after(pe, h_ready, b)
                                after(pe, qk_copied, b, n)
                                if rope:
                                    w = (WQ, WK)[n]
                                    pe.matmul(bank[6][:, 0:T], w[:, 0:P], H[:, :], start=True, stop=True)
                                    mm = pe.matmul(bank[6][:, T:2 * T], w[:, P:2 * P], H[:, :], start=True, stop=True)
                                else:
                                    pe.matmul(bank[6][:, 0:T], WQ[:, n * P:(n + 1) * P], H[:, :], start=True, stop=True)
                                    mm = pe.matmul(bank[6][0:KR, T:2 * T], WK[:, n * P:n * P + KR], H[:, :], start=True, stop=True)
                                mm.then_inc(qk_ready.sem, 1)
                        if h == L_V:
                            after(pe, qk_copied, b)
                            for n in range(2):
                                mm = pe.matmul(bank[6][:, n * HV * VW:(n + 1) * HV * VW], H[:, n * P:(n + 1) * P], WV[:, :],
                                               start=True, stop=True)
                            mm.then_inc(v_ready.sem, 1)
                    if has(1, t):
                        if L_SCORES <= h < L_SCORES + NH // 2:
                            scores(t + 1, (m + 1) % 3, 2 * (h - L_SCORES))
                            scores(t + 1, (m + 1) % 3, 2 * (h - L_SCORES) + 1)
                    if has(0, t):
                        scores_t(t, m, h)
                        if h >= 2:
                            values(t, m, h - 2)
                    if has(-1, t):
                        b = t - 1
                        if h == L_LAST:
                            after(pe, cx_ready, b, NS - 1)
                            if has(1, t):
                                after(pe, mf_ready, b + 1)
                            turn(b, NS - 1)
                        if h == L_CTT:
                            if diff:
                                after(pe, cxn_ready, b)
                                if has(0, t):
                                    after(pe, cx_ready, t, 1)
                            else:
                                after(pe, cx_ready, b)
                            for n in range(2):
                                for r in range(R2):
                                    src = CX[:, (m - 1) % 3, n, :, :].rearrange("p h d -> p (h d)")[:, r * P:(r + 1) * P]
                                    mm = pe.transpose(bank[7][:, r * T + n * P:r * T + (n + 1) * P], src, c.ID)
                            mm.then_inc(ctt_ready.sem, 1)
                        if h == L_OUT:
                            after(pe, ctt_copied, b)
                            for r in range(R2):
                                mm = pe.matmul(bank[7][:, 0:T], WO[:, r, :], CTT[:, r, :], start=(r == 0), stop=(r == R2 - 1))
                            mm.then_inc(o_ready.sem, 1)
                    if has(1, t):
                        if h == L_MT:
                            b = t + 1
                            if causal:
                                after(pe, nmq_ready, b)
                            else:
                                after(pe, s_used, b)
                            if has(0, t):
                                after(pe, cx_ready, t, S_MT + 1)
                            for n in range(2):
                                mm = pe.transpose(bank[7][0:NH, n * P:(n + 1) * P], NMQ[:, n, :], c.ID)
                            mm.then_inc(mt_ready.sem, 1)
                    if has(0, t):
                        if h in turn_at:
                            s = turn_at[h]
                            if s == out_at:
                                after(pe, tmp_ready, t - 1)
                            elif s == 0:
                                after(pe, cx_ready, t - 1)
                            else:
                                after(pe, cx_ready, t, s)
                                if s == S_MT + 1 and has(1, t):
                                    after(pe, mf_ready, t + 1)
                            turn(t, s)
                if has(0, t):
                    values(t, m, NH - 2)
                    values(t, m, NH - 1)
            steps(pe, step)

        @block.vector
        def _(v):
            v.memset(QH[:, :, :, :].rearrange("p j h t -> p (j h t)").bitcast(F32), 0.0).then_inc(zeroed, 1)
            v.wait_ge(zeroed, 5)
            v.memset(VX[:, :, :, :, VW:OW], 1.0).then_inc(vx_ones, 1)
            v.wait_ge(w_in, NW)
            if cfg.get("gate"):
                v.wait_ge(sg_ready, 1)
                v.tensor_scalar(SGM[:, :], HM[:, :], SG[:, 0:1], None, ALU.mult).then_inc(sgm_ready, 1)
                v.wait_ge(gate_mm, 1)
                v.tensor_copy(GATE[:, :], bank[6][:, 0:T]).then_inc(gate_ready, 1)
            if diff:
                v.tensor_tensor(LQ[:, 0:4:2, :, :], LQ[:, 0:4:2, :, :], LQ[:, 1:4:2, :, :], ALU.mult).then_inc(ls_ready, 1)
                v.wait_ge(ls_ready, 1)
                v.tensor_reduce(LS[:, :, :], LQ[:, 0:4:2, :, :], AX, ALU.add).then_inc(ls_ready, 1)
                v.wait_ge(le_ready, 1)
                v.scalar_tensor_tensor(NLAM[:, :], LE[:, 1, :], -0.8, LE[:, 0, :], ALU.add, ALU.subtract).then_inc(lam_ready, 1)
                v.tensor_scalar(COL[:, 2:3], COL[:, 2:3], 1.0 - 0.8, None, ALU.mult).then_inc(lam_ready, 1)
                v.wait_ge(lam_ready, 2)

            def turned(b, j, s):
                after(v, t_ready, b, s + 1)
                o = bank[7][:, 0:T].rearrange("p (n g x) -> p n g x", n=2, g=4)
                after(v, cx_ready, b, s)
                v.reciprocal(RC[:, :, :], o[:, :, :, VW:OW].rearrange("p n g x -> p n (g x)")).then_inc(rc_ready.sem, 1)
                after(v, rc_ready, b, s + 1)
                if s == 0:
                    after(v, ctt_ready, b - 3)
                scale = RC[:, :, :].unsqueeze(3).to_broadcast([P, 2, 4, VW])
                if not diff:
                    v.tensor_tensor(CX[:, j, :, 4 * s:4 * s + 4, :], o[:, :, :, 0:VW], scale, ALU.mult).then_inc(cx_ready.sem, 1)
                    return
                lam = NLAM[:, 2 * s:2 * s + 2].unsqueeze(1).to_broadcast([P, 2, 2])
                v.tensor_tensor(RC[:, :, 1:4:2], RC[:, :, 1:4:2], lam, ALU.mult).then_inc(dif_ready.sem, 1)
                after(v, dif_ready, b, 2 * s + 1)
                v.tensor_tensor(CX2[:, :, :, :], o[:, :, :, 0:VW], scale, ALU.mult).then_inc(cx_ready.sem, 1)
                after(v, cx_ready, b, s + 1)
                v.tensor_tensor(CX[:, j, :, 2 * s:2 * s + 2, :], CX2[:, :, 0:4:2, :], CX2[:, :, 1:4:2, :], ALU.add).then_inc(dif_ready.sem, 1)

            def maxima(b, h):
                after(v, s_ready, b, h + 1)
                if h == 0:
                    after(v, mt_ready, b - 1)
                if causal:
                    v.tensor_reduce(NM3[:, h, :], bank[h % 2][:, 0:NC].rearrange("p (n k) -> p n k", n=3), AX, ALU.max,
                                    negate=True).then_inc(s_used.sem, 1)
                else:
                    v.tensor_reduce(NMQ[:, :, h], bank[h % 2][:, 0:NC].rearrange("p (n k) -> p n k", n=2), AX, ALU.max,
                                    negate=True).then_inc(s_used.sem, 1)

            def step(t, m):
                for h in range(NH):
                    if has(2, t):
                        b = t + 2
                        if h == L_MEAN and centered:
                            after(v, mean_ready, b)
                            after(v, xn_ready, b - 1)
                            v.tensor_tensor(XC[:, :], SRC[:, tok(b)], bank[6][:, 0:T], ALU.subtract).then_inc(xc_ready.sem, 1)
                        if h == L_VAR:
                            after(v, var_ready, b)
                            after(v, rs_ready, b - 1)
                            v.tensor_scalar(VE[:, :], bank[6][:, T:T + 2], eps, None, ALU.add).then_inc(ve_ready.sem, 1)
                        if h == L_DG:
                            after(v, rs_ready, b)
                            after(v, bc_ready, b - 1)
                            v.tensor_scalar(DG[:, 0, :], c.ID, RS[:, 0:1], None, ALU.mult)
                            v.tensor_scalar(DG[:, 1, :], c.ID, RS[:, 1:2], None, ALU.mult).then_inc(dg_ready.sem, 1)
                        if h == L_XN:
                            after(v, bc_ready, b)
                            after(v, h_ready, b - 1)
                            v.tensor_tensor(XN[:, :], XC[:, :] if centered else SRC[:, tok(b)], bank[6][:, T:2 * T],
                                            ALU.mult).then_inc(xn_ready.sem, 1)
                        for n in range(QK):
                            if h == L_QK + 2 * n * U + 1:
                                after(v, qk_ready, b, n + 1)
                                if rope:
                                    if n == 0:
                                        after(v, lo_ready, b - 1)
                                    else:
                                        after(v, half_ready, b)
                                    v.tensor_tensor(RES[:, 0, :], bank[6][:, 0:T], c.CST[:, C_COS:C_COS + T], ALU.mult)
                                    v.tensor_tensor(RES[:, 1, :], bank[6][:, T:2 * T], c.CST[:, C_SIN:C_SIN + T], ALU.mult)\
                                        .then_inc(qk_copied.sem, 1)
                                    continue
                                after(v, res_ready, b, n)
                                if cfg.get("gate"):
                                    v.tensor_tensor(QKF[:, 0, :], bank[6][:, 0:T], GATE[:, :], ALU.mult)
                                elif cfg.get("bq"):
                                    v.tensor_scalar(QKF[:, 0, :], bank[6][:, 0:T], COL[:, 0:1], None, ALU.add)
                                else:
                                    v.tensor_copy(QKF[:, 0, :], bank[6][:, 0:T])
                                v.tensor_copy(QKF[0:KR, 1, :], bank[6][0:KR, T:2 * T]).then_inc(qk_copied.sem, 1)
                        if h == L_V + 1 and cfg.get("bv"):
                            after(v, v_ready, b)
                            after(v, pv_done, b - 3)
                            vx = VX[:, (m + 2) % 3, :, :, 0:VW]
                            src = bank[6][:, 0:2 * HV * VW].rearrange("p (n h d) -> p n h d", n=2, h=HV)
                            bv = BV[:, :].rearrange("p (h d) -> p h d", h=HV).unsqueeze(1).to_broadcast([P, 2, HV, VW])
                            v.tensor_tensor(vx, src, bv, ALU.add).then_inc(v_copied.sem, 1)
                    if has(1, t):
                        b = t + 1
                        if L_SCORES <= h < L_SCORES + NH // 2:
                            maxima(b, 2 * (h - L_SCORES))
                            maxima(b, 2 * (h - L_SCORES) + 1)
                        if h == L_NMQ and causal:
                            after(v, s_used, b)
                            v.tensor_copy(NMQ[:, 0, :], NM3[:, :, 0]).then_inc(nmq_ready.sem, 1)
                            v.tensor_tensor(NMQ[:, 1, :], NM3[:, :, 1], NM3[:, :, 2], ALU.min).then_inc(nmq_ready.sem, 1)
                    if has(-1, t):
                        b = t - 1
                        if h == L_LAST:
                            turned(b, (m - 1) % 3, NS - 1)
                        if diff and h == L_COMBINE:
                            after(v, csq_ready, b)
                            after(v, cr_ready, b - 1)
                            v.tensor_reduce(CM[:, :, :], CSQ[:, :, :, :], AX, ALU.add).then_inc(cm_ready.sem, 1)
                            after(v, cm_ready, b, 1)
                            v.tensor_scalar(CM[:, :, :], CM[:, :, :], 1.0 / VW, 1e-5, ALU.mult, ALU.add).then_inc(cm_ready.sem, 1)
                        if diff and h == L_CTT - 1:
                            after(v, cr_ready, b)
                            cx = CX[:, (m - 1) % 3, :, :, :]
                            v.tensor_tensor(cx, cx, CR[:, :, :].unsqueeze(3).to_broadcast([P, 2, 16, VW]),
                                            ALU.mult).then_inc(cxn_ready.sem, 1)
                        if h == L_TMP:
                            after(v, o_ready, b)
                            after(v, x_updated, b - 1)
                            if cfg.get("plain"):
                                v.tensor_copy(TMP[:, :], bank[7][:, 0:T]).then_inc(tmp_ready.sem, 1)
                            else:
                                v.tensor_scalar(TMP[:, :], bank[7][:, 0:T], COL[:, 1:2], c.MOD[:, l, 2, one(b)],
                                                ALU.add, ALU.mult).then_inc(tmp_ready.sem, 1)
                            after(v, tmp_ready, b)
                            v.tensor_tensor(DST[:, tok(b)], DST[:, tok(b)], TMP[:, :], ALU.add).then_inc(x_updated.sem, 1)
                    if has(0, t) and h - 1 in turn_at:
                        turned(t, m, turn_at[h - 1])
                if has(0, t) and NH - 1 in turn_at:
                    turned(t, m, turn_at[NH - 1])
            steps(v, step)
    close(c, S)


def tok(b, n=T):
    return slice(b * n, (b + 1) * n) if isinstance(b, int) else bass.ds(b * n, n)


def one(b):
    return slice(b, b + 1) if isinstance(b, int) else bass.ds(b, 1)


def norm_phase(c, cfg, NT, LG=None, prefetch=()):
    nc, bank, SRC, centered = c.nc, c.bank, cfg["nsrc"], cfg["ncentered"]
    E = cfg.get("E", 0) if LG is not None else 0
    with ExitStack() as ctx:
        sb = lambda name, shape, dt=F32: c.sb(cfg["name"] + "n" + name, shape, dt, ctx)
        XC, SQ, XN = sb("XC", [P, 4, T]), sb("SQ", [P, 2, T]), sb("XN", [P, T])
        H = sb("H", [P, 4, T])
        VE, RS, DG = sb("VE", [P, 2, 2]), sb("RS", [P, 2, 2]), sb("DG", [P, 2, 2, P])
        COL, WR = sb("COL", [P, 2]), sb("WR", [P, max(E, 1)])
        S = signals(c, n_mean=int(centered), n_xc=int(centered), n_sq=1, n_var=1, n_ve=1, n_rs=1, n_dg=1, n_bc=1, n_xn=1,
                    n_h=1, n_copied=1, n_logits=int(E > 0), n_lg=int(E > 0))
        mean, xc, sq, var, ve, rs, dg, bc, xn, hr, copied, logits, lg = S
        w_in = c.sem(cfg["name"] + "n_w_in")
        loads = ([(COL[:, 0:1], cfg["ngain"])] if cfg.get("ngain") else []) \
            + ([(COL[:, 1:2], cfg["nshift"])] if cfg.get("nshift") else []) + ([(WR[:, :], cfg["wr"])] if E else [])
        has = lambda stage, t: not isinstance(t, int) or 0 <= t + stage < NB

        def steps(eng, step):
            for t in range(8):
                step(t, t % 4)
            with eng.Fori(0, 2) as i:
                for k in range(8, 12):
                    step(i * 4 + k, k % 4)
            for t in range(16, NB + 4):
                step(t, t % 4)

        block = ctx.enter_context(nc.Block())

        @block.sync
        def _(sp):
            for dst, src in loads:
                sp.dma_start(dst, c.ins[src]).then_inc(w_in, 16)
            for dst, src, sem in prefetch:
                sp.dma_start(dst, c.ins[src]).then_inc(sem, 16)

        @block.tensor
        def _(pe):
            if loads:
                pe.wait_ge(w_in, 16 * len(loads))

            def step(t, m):
                if has(0, t) and centered:
                    after(pe, xc, t - 2)
                    pe.matmul(bank[m % 2][:, 0:T], c.MEAN, SRC[:, tok(t)], start=True, stop=True).then_inc(mean.sem, 1)
                if has(-3, t):
                    b, d = t - 3, (m - 3) % 2
                    after(pe, dg, b)
                    after(pe, xn, b - 2)
                    for n in range(2):
                        mm = pe.matmul(bank[4 + d][:, n * P:(n + 1) * P], c.ONES[:, :], DG[:, d, n, :], start=True, stop=True)
                    mm.then_inc(bc.sem, 1)
                if has(-1, t):
                    d = (m - 1) % 2
                    after(pe, sq, t - 1)
                    after(pe, ve, t - 3)
                    for n in range(2):
                        mm = pe.matmul(bank[2 + d][:, n:n + 1], SQ[:, d, n * P:(n + 1) * P], c.MEAN[:, 0:1], start=True, stop=True)
                    mm.then_inc(var.sem, 1)
                if E and has(-4, t):
                    b, d = t - 4, m % 2
                    after(pe, hr, b)
                    after(pe, lg, b - 2)
                    for n in range(2):
                        mm = pe.matmul(bank[6 + d][:, n * E:(n + 1) * E], H[:, m % 4, n * P:(n + 1) * P], WR[:, :],
                                       start=True, stop=True)
                    mm.then_inc(logits.sem, 1)
            steps(pe, step)

        @block.gpsimd
        def _(pool):
            def step(t, m):
                if has(-1, t):
                    d = (m - 1) % 2
                    after(pool, ve, t - 1)
                    after(pool, dg, t - 3)
                    nc.gpsimd.tensor_tensor(RS[:, d, :], VE[:, d, :], c.HALF[:, 0:2], ALU.pow).then_inc(rs.sem, 1)
            steps(pool, step)

        @block.scalar
        def _(act):
            def step(t, m):
                if has(0, t):
                    if centered:
                        after(act, xc, t)
                    after(act, var, t - 2)
                    nc.scalar.activation(SQ[:, m % 2, :], XC[:, m, :] if centered else SRC[:, tok(t)], ACT.Square).then_inc(sq.sem, 1)
                if has(-4, t):
                    after(act, hr, t - 4)
                    nc.scalar.copy(NT[:, tok(t - 4)], H[:, m % 4, :]).then_inc(copied.sem, 1)
            steps(act, step)

        @block.vector
        def _(v):
            if loads:
                v.wait_ge(w_in, 16 * len(loads))

            def step(t, m):
                if has(-2, t):
                    b, d = t - 2, m % 2
                    after(v, rs, b)
                    after(v, bc, b - 2)
                    v.tensor_scalar(DG[:, d, 0, :], c.ID, RS[:, d, 0:1], None, ALU.mult)
                    v.tensor_scalar(DG[:, d, 1, :], c.ID, RS[:, d, 1:2], None, ALU.mult).then_inc(dg.sem, 1)
                if has(0, t) and centered:
                    after(v, mean, t)
                    after(v, xn, t - 4)
                    v.tensor_tensor(XC[:, m, :], SRC[:, tok(t)], bank[m % 2][:, 0:T], ALU.subtract).then_inc(xc.sem, 1)
                if has(-3, t):
                    b, j, d = t - 3, (m - 3) % 4, (m - 3) % 2
                    after(v, bc, b)
                    after(v, hr, b - 1)
                    v.tensor_tensor(XN[:, :], XC[:, j, :] if centered else SRC[:, tok(b)], bank[4 + d][:, 0:T],
                                    ALU.mult).then_inc(xn.sem, 1)
                if has(-1, t):
                    b, d = t - 1, (m - 1) % 2
                    after(v, var, b)
                    after(v, rs, b - 2)
                    v.tensor_scalar(VE[:, d, :], bank[2 + d][:, 0:2], cfg["neps"], None, ALU.add).then_inc(ve.sem, 1)
                if has(-3, t):
                    b, j = t - 3, (m - 3) % 4
                    after(v, xn, b)
                    after(v, copied, b - 4)
                    if E:
                        after(v, logits, b - 4)
                    if cfg.get("ngain"):
                        scale, shift = COL[:, 0:1], (COL[:, 1:2] if cfg.get("nshift") else 0.0)
                    else:
                        l, k = cfg["layer"], cfg["nmod"]
                        scale, shift = c.MOD[:, l, k + 1, one(b)], c.MOD[:, l, k, one(b)]
                    v.tensor_scalar(H[:, j, :], XN[:, :], scale, shift, ALU.mult, ALU.add).then_inc(hr.sem, 1)
                if E and has(-4, t):
                    b = t - 4
                    after(v, logits, b)
                    v.tensor_copy(LG[:, bass.ds(b * 2, 2) if not isinstance(b, int) else slice(2 * b, 2 * b + 2), 0:E],
                                  bank[6 + m % 2][:, 0:2 * E].rearrange("p (n e) -> p n e", n=2)).then_inc(lg.sem, 1)
            steps(v, step)
    close(c, S)


NT_TILES = NTOK // P


def combine_phase(c, cfg, LG, CB3, CBF):
    nc, bank, E, kind, name = c.nc, c.bank, cfg["E"], cfg["kind"], cfg["name"]
    N = NT_TILES
    G = 8
    with ExitStack() as ctx:
        sb = lambda nm, shape, dt=F32: c.sb(name + "c" + nm, shape, dt, ctx)
        PB, W = sb("PB", [P, N, E]), sb("W", [P, N, E])
        R1, R2, R3, R4 = (sb(f"R{k}", [P, N]) for k in range(4))
        GG = G if E == 64 else E
        KEY = sb("KEY", [P, N, GG])
        RK, SELG, CMP, EQ = sb("RK", [P, N, GG]), sb("SELG", [P, N, GG]), sb("CMP", [P, N, GG, GG]), sb("EQ", [P, N, GG, GG])
        LOW = sb("LOW", [P, 64])
        TH, TM, TR = sb("TH", [P, 512]), sb("TM", [P, 512], BF16), sb("TR", [P, 512])
        if E == 64:
            SFC, BIAS, M8 = sb("SFC", [P, N, E]), sb("BIAS", [P, E]), sb("M8", [P, N, 8])
            T1, SEL = sb("T1", [P, N, E]), sb("SEL", [P, N, E])
            M1, M2, CNT, GB = (sb(nm, [P, N, 8]) for nm in ("M1", "M2", "CNT", "GB"))
            RUN = sb("RUN", [P, N, E])
        r_in, r_act, r_step, r_run, r_pos, r_val, r_t, r_hi, r_res, r_mid, r_lo, r_z, r_tm = (
            c.sem("r_" + nm) for nm in ("in", "act", "step", "run", "pos", "val", "t", "hi", "res", "mid", "lo", "z", "tm"))
        base = c.counts
        b0 = dict(base)
        block = ctx.enter_context(nc.Block())
        bc3 = lambda a, n: a.unsqueeze(2).to_broadcast([P, N, n])
        loads = [(LOW[:, :], "low8")] + ([(BIAS[:, :], "rbias")] if E == 64 else [])

        @block.sync
        def _(sp):
            for dst, src in loads:
                sp.dma_start(dst, c.ins[src]).then_inc(r_in, 16)

        @block.gpsimd
        def _(pool):
            nc.gpsimd.memset(CB3[:, :, :], 0.0).then_inc(r_z, 1)

        @block.scalar
        def _(act):
            if E == 64:
                nc.scalar.activation(PB[:, :, :], LG[:, :, :], ACT.Sigmoid).then_inc(r_act, 1)
            else:
                act.wait_ge(r_step, b0["step"] + 2)
                nc.scalar.activation(PB[:, :, :], PB[:, :, :], ACT.Exp).then_inc(r_act, 1)
            for g in range(N // 4):
                act.wait_ge(r_t, b0["t"] + g + 1)
                if g == 0:
                    act.wait_ge(r_z, b0["z"] + 1)
                o = bank[4 + g % 2][0:E, :]
                if CBF is not None:
                    nc.scalar.copy(CBF[0:E, tok(g, 512)], o)
                nc.scalar.copy(CB3[0:E, 0, tok(g, 512)], o).then_inc(r_hi, 1)
                act.wait_ge(r_res, b0["res"] + g + 1)
                if g >= 1:
                    act.wait_ge(r_lo, b0["lo"] + g)
                nc.scalar.copy(TM[0:E, :], TR[0:E, :]).then_inc(r_tm, 1)
                act.wait_ge(r_tm, b0["tm"] + g + 1)
                nc.scalar.copy(CB3[(64 if E == 64 else 32):(64 if E == 64 else 32) + E, 0, tok(g, 512)], TM[0:E, :]).then_inc(r_mid, 1)

        @block.tensor
        def _(pe):
            if E == 64:
                for n in range(N):
                    pe.wait_ge(r_run, b0["run"] + max(n, 1))
                    o = bank[n // 8][:, (n % 8) * E:(n % 8 + 1) * E]
                    mm = pe.matmul(o, c.CST[:, C_TRI:C_TRI + P], SEL[:, n, :], start=True, stop=(n == 0))
                    if n:
                        mm = pe.matmul(o, c.ONES[:, :], RUN[:, n, :], start=False, stop=True)
                    mm.then_inc(r_pos, 1)
            pe.wait_ge(r_val, b0["val"] + 1)
            for g in range(N // 4):
                if g >= 2:
                    pe.wait_ge(r_hi, b0["hi"] + g - 1)
                    pe.wait_ge(r_res, b0["res"] + g - 1)
                for k in range(4):
                    mm = pe.transpose(bank[4 + g % 2][0:E, k * P:(k + 1) * P], W[:, 4 * g + k, :], c.ID)
                mm.then_inc(r_t, 1)

        @block.vector
        def _(v):
            count = [b0["step"]]

            def then(ins):
                count[0] += 1
                ins.then_inc(r_step, 1)
                v.wait_ge(r_step, count[0])

            def ranks(key, top, n=GG):
                mine = key.unsqueeze(3).to_broadcast([P, N, n, n])
                other = key.unsqueeze(2).to_broadcast([P, N, n, n])
                low = LOW[:, :].rearrange("p (a b) -> p a b", a=8)[:, 0:n, 0:n].unsqueeze(1).to_broadcast([P, N, n, n])
                then(v.tensor_tensor(EQ[:, :, :, :], other, mine, ALU.is_equal))
                then(v.tensor_tensor(EQ[:, :, :, :], EQ[:, :, :, :], low, ALU.mult))
                then(v.tensor_tensor(CMP[:, :, :, :], other, mine, ALU.is_gt))
                then(v.tensor_tensor(CMP[:, :, :, :], CMP[:, :, :, :], EQ[:, :, :, :], ALU.add))
                then(v.tensor_reduce(RK[:, :, :], CMP[:, :, :, :], AX, ALU.add))
                then(v.tensor_scalar(SELG[:, :, :], RK[:, :, :], top - 0.5, None, ALU.is_lt))

            v.wait_ge(r_in, b0["in"] + 16 * len(loads))
            if E == 64:
                v.wait_ge(r_act, b0["act"] + 1)
                g4 = lambda a: a.rearrange("p n (g k) -> p (n g) k", g=8)
                gb = lambda a: a.rearrange("p n g -> p (n g)").unsqueeze(2).to_broadcast([P, N * 8, 8])
                sfc = g4(SFC[:, :, :])
                then(v.tensor_tensor(SFC[:, :, :], PB[:, :, :], BIAS[:, :].unsqueeze(1).to_broadcast([P, N, E]), ALU.add))
                then(v.tensor_reduce(M1[:, :, :].rearrange("p n g -> p (n g)"), sfc, AX, ALU.max))
                then(v.tensor_tensor(g4(T1[:, :, :]), sfc, gb(M1[:, :, :]), ALU.is_equal))
                then(v.tensor_reduce(CNT[:, :, :].rearrange("p n g -> p (n g)"), g4(T1[:, :, :]), AX, ALU.add))
                then(v.scalar_tensor_tensor(T1[:, :, :], T1[:, :, :], NEG, SFC[:, :, :], ALU.mult, ALU.add))
                then(v.tensor_reduce(M2[:, :, :].rearrange("p n g -> p (n g)"), g4(T1[:, :, :]), AX, ALU.max))
                then(v.tensor_scalar(CNT[:, :, :], CNT[:, :, :], 1.5, None, ALU.is_gt))
                then(v.tensor_scalar(GB[:, :, :], CNT[:, :, :], -1.0, 1.0, ALU.mult, ALU.add))
                then(v.tensor_tensor(CNT[:, :, :], CNT[:, :, :], M1[:, :, :], ALU.mult))
                then(v.tensor_tensor(M2[:, :, :], M2[:, :, :], GB[:, :, :], ALU.mult))
                then(v.tensor_tensor(M2[:, :, :], M2[:, :, :], CNT[:, :, :], ALU.add))
                then(v.tensor_tensor(KEY[:, :, :], M1[:, :, :], M2[:, :, :], ALU.add))
                ranks(KEY[:, :, :], 4)
                then(v.tensor_scalar(GB[:, :, :], SELG[:, :, :], -NEG, NEG, ALU.mult, ALU.add))
                then(v.tensor_tensor(g4(T1[:, :, :]), sfc, gb(SELG[:, :, :]), ALU.mult))
                then(v.tensor_tensor(g4(T1[:, :, :]), g4(T1[:, :, :]), gb(GB[:, :, :]), ALU.add))
                for n in range(N):
                    last = v.max(M8[:, n, :], T1[:, n, :])
                then(last)
                for n in range(N):
                    last = v.match_replace(SFC[:, n, :], M8[:, n, :], T1[:, n, :], 3.0 * NEG)
                then(last)
                then(v.tensor_tensor(SEL[:, :, :], SFC[:, :, :], T1[:, :, :], ALU.not_equal))
                v.tensor_copy(RUN[:, 1, :], SEL[:, 0, :]).then_inc(r_run, 1)
                for n in range(2, N):
                    v.wait_ge(r_run, b0["run"] + n - 1)
                    v.tensor_tensor(RUN[:, n, :], RUN[:, n - 1, :], SEL[:, n - 1, :], ALU.add).then_inc(r_run, 1)
                then(v.tensor_tensor(W[:, :, :], PB[:, :, :], SEL[:, :, :], ALU.mult))
                then(v.tensor_reduce(R1[:, :], W[:, :, :], AX, ALU.add))
                then(v.tensor_scalar(R1[:, :], R1[:, :], 1e-20, None, ALU.add))
                then(v.reciprocal(R2[:, :], R1[:, :]))
                then(v.tensor_scalar(R2[:, :], R2[:, :], 2.5, None, ALU.mult))
                then(v.tensor_tensor(W[:, :, :], W[:, :, :], bc3(R2[:, :], E), ALU.mult))
                v.wait_ge(r_pos, b0["pos"] + N)
                for q in range(4):
                    w = W[:, 8 * q:8 * q + 8, :].rearrange("p n e -> p (n e)")
                    last = v.scalar_tensor_tensor(w, bank[q][:, :], cfg["CAP"] - 0.5, w, ALU.is_lt, ALU.mult)
                last.then_inc(r_val, 1)
            else:
                then(v.tensor_reduce(R1[:, :], LG[:, :, 0:E], AX, ALU.max))
                then(v.tensor_tensor(PB[:, :, :], LG[:, :, 0:E], bc3(R1[:, :], E), ALU.subtract))
                v.wait_ge(r_act, b0["act"] + 1)
                then(v.tensor_reduce(R1[:, :], PB[:, :, :], AX, ALU.add))
                then(v.reciprocal(R2[:, :], R1[:, :]))
                then(v.tensor_tensor(KEY[:, :, :], PB[:, :, :], bc3(R2[:, :], E), ALU.mult))
                ranks(KEY[:, :, :], 2)
                if cfg["renorm"]:
                    then(v.tensor_tensor(PB[:, :, :], KEY[:, :, :], SELG[:, :, :], ALU.mult))
                    then(v.tensor_reduce(R3[:, :], PB[:, :, :], AX, ALU.add))
                    then(v.reciprocal(R4[:, :], R3[:, :]))
                    v.tensor_tensor(W[:, :, :], PB[:, :, :], bc3(R4[:, :], E), ALU.mult).then_inc(r_val, 1)
                else:
                    v.tensor_tensor(W[:, :, :], KEY[:, :, :], SELG[:, :, :], ALU.mult).then_inc(r_val, 1)
            c.counts["step"] = count[0]
            v.wait_ge(r_z, b0["z"] + 1)
            for g in range(N // 4):
                v.wait_ge(r_hi, b0["hi"] + g + 1)
                v.tensor_tensor(TR[0:E, :], bank[4 + g % 2][0:E, :], CB3[0:E, 0, tok(g, 512)], ALU.subtract).then_inc(r_res, 1)
                v.wait_ge(r_tm, b0["tm"] + g + 1)
                low = CB3[0:E, 1, tok(g, 512)] if E == 64 else CB3[64:64 + E, 0, tok(g, 512)]
                v.tensor_tensor(low, TR[0:E, :], TM[0:E, :], ALU.subtract).then_inc(r_lo, 1)
                v.wait_ge(r_lo, b0["lo"] + g + 1)
        for key, k in (("in", 16 * len(loads)), ("act", 1), ("run", N - 1 if E == 64 else 0), ("pos", N if E == 64 else 0),
                       ("val", 1), ("t", 8), ("hi", 8), ("res", 8), ("mid", 8), ("lo", 8), ("z", 1), ("tm", 8)):
            c.counts[key] += k


def experts_phase(c, cfg, NT, W1, W3, W2, CB3, CBF, w_in, nw):
    nc, bank, name = c.nc, c.bank, cfg["name"]
    NCH, sel, glu, fn = cfg["NCH"], cfg["sel"], cfg["glu"], cfg["fn"]
    F = 512
    NI = NTOK // F
    new = [s is not None and (m == 0 or sel[m - 1] != s) for m, s in enumerate(sel)]
    NBC = sum(new)
    kth = [sum(new[:m + 1]) - 1 for m in range(NCH)]
    gated = [s is not None for s in sel]
    NGT = sum(gated)
    gi = [sum(gated[:m]) for m in range(NCH)]
    last_use = [max([m for m in range(NCH) if gated[m] and kth[m] == k]) for k in range(NBC)]
    NPL = 2 if cfg.get("E") == 64 else 1
    l = cfg["layer"]
    with ExitStack() as ctx:
        sb = lambda nm, shape, dt=F32: c.sb(name + "e" + nm, shape, dt, ctx)
        SG, HS, T1 = sb("SG", [P, 2, F]), sb("HS", [P, 2, F]), sb("T1", [P, F])
        SELB = sb("SELB", [P, max(NBC, 1), P], BF16)
        COL, FB, BPJ, TMP = sb("COL", [P, 1]), sb("FB", [P, NCH]), sb("BPJ", [8, P]), sb("TMP", [P, T])
        small = [(COL[:, :], cfg.get("ybias") or "zero")]
        if cfg.get("hbias"):
            small.append((FB[:, :], cfg["hbias"]))
        if cfg.get("ebias"):
            small.append((BPJ[:, :], cfg["ebias"]))
        s_in, sel_in = c.sem(name + "e_s_in"), c.sem(name + "e_sel_in")
        S = signals(c, e_g=NCH, e_u=NCH * int(glu), e_act=NCH, e_bc=NBC, e_t1=NCH * int(glu), e_hs=NGT, e_dn=NCH,
                    e_y=int(CBF is not None), e_tmp=2 * int(bool(cfg.get("ybias") or cfg.get("plus"))), e_used=2)
        g_ready, u_ready, act_done, bc_ready, t1_ready, hs_ready, dn_done, y_ready, y_tmp, y_used = S

        def steps(eng, step):
            for i in range(2):
                step(i, i)
            with eng.Fori(0, (NI - 2) // 2) as k:
                for j in range(2):
                    step(k * 2 + (2 + j), j)

        block = ctx.enter_context(nc.Block())

        @block.sync
        def _(sp):
            for dst, src in small:
                sp.dma_start(dst, c.ins[src]).then_inc(s_in, 16)

        @block.gpsimd
        def _(pool):
            if NBC:
                nc.gpsimd.dma_start(SELB[:, :, :].rearrange("p k x -> p (k x)"), c.ins[cfg["selector"]]).then_inc(sel_in, 16)

        @block.tensor
        def _(pe):
            pe.wait_ge(w_in, 16 * nw)
            pe.wait_ge(s_in, 16 * len(small))
            if NBC:
                pe.wait_ge(sel_in, 16)

            def up(i, j, m):
                q = (j * NCH + m) % 2
                x = NT[:, tok(i, F)]
                after(pe, act_done, i, m - 1)
                pe.matmul(bank[q][:, :], W1[:, m * P:(m + 1) * P], x, start=True, stop=True).then_inc(g_ready.sem, 1)
                if glu:
                    after(pe, t1_ready, i, m - 1)
                    pe.matmul(bank[2 + q][:, :], W3[:, m * P:(m + 1) * P], x, start=True, stop=True).then_inc(u_ready.sem, 1)
                if new[m]:
                    k = kth[m]
                    kb = (j * NBC + k) % 2
                    if k >= 2:
                        after(pe, hs_ready, i, gi[last_use[k - 2]] + 1)
                    else:
                        after(pe, hs_ready, i - 1, gi[last_use[(k - 2) % NBC]] + 1)
                    for n in range(NPL):
                        mm = pe.matmul(bank[4 + kb][:, :], SELB[:, k, :], CB3[:, n, tok(i, F)], start=(n == 0), stop=(n == NPL - 1))
                    mm.then_inc(bc_ready.sem, 1)

            def down(i, j, m):
                q = (j * NCH + m) % 2
                if gated[m]:
                    after(pe, hs_ready, i, gi[m] + 1)
                else:
                    after(pe, act_done, i, m + 1)
                if m == 0:
                    after(pe, y_used, i - 2)
                mm = pe.matmul(bank[6 + j][:, :], W2[:, m, :], HS[:, q, :], start=(m == 0), stop=(m == NCH - 1 and CBF is None))
                mm.then_inc(dn_done.sem, 1)

            def step(i, j):
                for m in range(NCH):
                    up(i, j, m)
                    if m:
                        down(i, j, m - 1)
                down(i, j, NCH - 1)
                if CBF is not None:
                    pe.matmul(bank[6 + j][:, :], BPJ[:, :], CBF[:, tok(i, F)], start=False, stop=True).then_inc(y_ready.sem, 1)
            steps(pe, step)

        @block.scalar
        def _(act):
            act.wait_ge(s_in, 16 * len(small))

            def step(i, j):
                for m in range(NCH):
                    q = (j * NCH + m) % 2
                    after(act, g_ready, i, m + 1)
                    if glu:
                        after(act, t1_ready, i, m - 1)
                    else:
                        after(act, dn_done, i, m - 1)
                    dst = HS[:, q, :] if not gated[m] else SG[:, q, :]
                    nc.scalar.activation(dst, bank[q][:, :], fn, bias=FB[:, m:m + 1] if cfg.get("hbias") else 0.0)\
                        .then_inc(act_done.sem, 1)
            steps(act, step)

        @block.vector
        def _(v):
            v.wait_ge(s_in, 16 * len(small))

            def finish(i, j):
                after(v, y_ready if CBF is not None else dn_done, i)
                for n in range(2):
                    b = i * 2 + n
                    y = bank[6 + j][:, n * T:(n + 1) * T]
                    g = c.MOD[:, l, cfg["gmod"], one(b)]
                    if cfg.get("ybias") or cfg.get("plus"):
                        after(v, y_used, i, n)
                        if cfg.get("plus"):
                            v.scalar_tensor_tensor(TMP[:, :], y, COL[:, 0:1], c.HT[:, tok(b)], ALU.add, ALU.add).then_inc(y_tmp.sem, 1)
                        else:
                            v.tensor_scalar(TMP[:, :], y, COL[:, 0:1], None, ALU.add).then_inc(y_tmp.sem, 1)
                        after(v, y_tmp, i, n + 1)
                        y = TMP[:, :]
                    v.scalar_tensor_tensor(c.XT[:, tok(b)], y, g, c.XT[:, tok(b)], ALU.mult, ALU.add).then_inc(y_used.sem, 1)

            def step(i, j):
                for m in range(NCH):
                    q = (j * NCH + m) % 2
                    if not gated[m]:
                        continue
                    after(v, act_done, i, m + 1)
                    a = SG[:, q, :]
                    if glu:
                        after(v, u_ready, i, m + 1)
                        after(v, hs_ready, i, gi[m])
                        v.tensor_tensor(T1[:, :], a, bank[2 + q][:, :], ALU.mult).then_inc(t1_ready.sem, 1)
                        after(v, t1_ready, i, m + 1)
                        a = T1[:, :]
                    after(v, bc_ready, i, kth[m] + 1)
                    after(v, dn_done, i, m - 1)
                    v.tensor_tensor(HS[:, q, :], a, bank[4 + (j * NBC + kth[m]) % 2][:, :], ALU.mult).then_inc(hs_ready.sem, 1)
                finish(i, j)
            steps(v, step)
    close(c, S, NI)

def linear_attention_phase(c, NT):
    nc, bank = c.nc, c.bank
    N = NT_TILES
    with ExitStack() as ctx:
        sb = lambda nm, shape, dt=F32: c.sb("l" + nm, shape, dt, ctx)
        WQKV, BIAS, WO, BO = sb("WQKV", [P, 384]), sb("BIAS", [P, 384]), sb("WO", [P, P]), sb("BO", [P, 1])
        X, QKV, MN, EX, FQK = sb("X", [P, 2, P]), sb("QKV", [P, 2, 384]), sb("MN", [P, 256]), sb("EX", [P, 256]), sb("F", [P, 2, 256])
        M1, M2 = sb("M1", [P, 8, 8, 16]), sb("M2", [P, 16, 8, 8])
        KV, KS, NUM, DQ = sb("KV", [P, 8, 8]), sb("KS", [P, 8]), sb("NUM", [P, 16, 8]), sb("DQ", [P, 16, 8])
        DN, RD, AT, ATT = sb("DN", [P, 16]), sb("RD", [P, 16]), sb("AT", [P, 2, P]), sb("ATT", [P, P])
        w_in = c.sem("l_w_in")
        S = signals(c, l_x=1, l_p=1, l_qkv=1, l_mn=1, l_ex=1, l_f=1, l_m1=1, l_kv=1, l_ks=1, l_m2=1, l_num=1,
                    l_dq=1, l_dn=2, l_rd=1, l_at=1, l_t=1, l_att=1, l_o=1, l_y=1)
        xr, pr, qkv, mn, ex, fr, m1, kv, ks, m2, num, dq, dn, rd, at, tr, att, orr, yr = S
        has = lambda stage, t: not isinstance(t, int) or 0 <= t + stage < N

        def steps(eng, step):
            for t in range(-1, 2):
                step(t, t % 2)
            with eng.Fori(0, (N - 4) // 2) as i:
                for k in range(2, 4):
                    step(i * 2 + k, k % 2)
            for t in range(N - 2, N + 1):
                step(t, t % 2)

        loads = [(WQKV[:, :], "wqkv3"), (BIAS[:, :], "bqkv3"), (WO[:, :], "wo3"), (BO[:, :], "bo3")]
        block = ctx.enter_context(nc.Block())

        @block.sync
        def _(sp):
            for dst, src in loads:
                sp.dma_start(dst, c.ins[src]).then_inc(w_in, 16)

        @block.scalar
        def _(act):
            def step(t, p):
                if has(1, t):
                    b, j = t + 1, 1 - p
                    after(act, pr, b - 2)
                    nc.scalar.copy(X[:, j, :], NT[:, tok(b, P)]).then_inc(xr.sem, 1)
                if has(-1, t):
                    after(act, tr, t - 1)
                    after(act, orr, t - 2)
                    nc.scalar.copy(ATT[:, :], bank[2][:, 0:P]).then_inc(att.sem, 1)
                if has(1, t):
                    after(act, mn, t + 1)
                    after(act, fr, t)
                    nc.scalar.activation(EX[:, :], MN[:, :], ACT.Exp).then_inc(ex.sem, 1)
            steps(act, step)

        @block.tensor
        def _(pe):
            pe.wait_ge(w_in, 16 * len(loads))

            def step(t, p):
                if has(1, t):
                    b, j = t + 1, 1 - p
                    after(pe, xr, b)
                    after(pe, qkv, b - 2)
                    pe.matmul(bank[j][:, 0:384], X[:, j, :], WQKV[:, :], start=True, stop=True).then_inc(pr.sem, 1)
                if has(-1, t):
                    b, j = t - 1, 1 - p
                    after(pe, at, b)
                    after(pe, att, b - 1)
                    pe.transpose(bank[2][:, 0:P], AT[:, j, :], c.ID).then_inc(tr.sem, 1)
                    after(pe, att, b)
                    after(pe, yr, b - 1)
                    pe.matmul(bank[3][:, 0:P], WO[:, :], ATT[:, :], start=True, stop=True).then_inc(orr.sem, 1)
            steps(pe, step)

        @block.gpsimd
        def _(pool):
            def step(t, p):
                if has(0, t):
                    fk = FQK[:, p, P:2 * P].rearrange("p (h d) -> p d h", d=8).unsqueeze(2).to_broadcast([P, 8, 8, 16])
                    vv = QKV[:, p, 2 * P:3 * P].rearrange("p (h e) -> p e h", e=8).unsqueeze(1).to_broadcast([P, 8, 8, 16])
                    after(pool, fr, t)
                    after(pool, kv, t - 1)
                    nc.gpsimd.tensor_tensor(M1[:, :, :, :], fk, vv, ALU.mult).then_inc(m1.sem, 1)
                    fq = FQK[:, p, 0:P].rearrange("p (h d) -> p h d", d=8).unsqueeze(2).to_broadcast([P, 16, 8, 8])
                    kve = KV[:, :, :].rearrange("p d e -> p e d").unsqueeze(1).to_broadcast([P, 16, 8, 8])
                    after(pool, kv, t)
                    after(pool, num, t - 1)
                    nc.gpsimd.tensor_tensor(M2[:, :, :, :], fq, kve, ALU.mult).then_inc(m2.sem, 1)
            steps(pool, step)

        @block.vector
        def _(v):
            v.wait_ge(w_in, 16 * len(loads))

            def step(t, p):
                if has(0, t):
                    after(v, m1, t)
                    after(v, m2, t - 1)
                    v.tensor_reduce(KV[:, :, :], M1[:, :, :, :], AX, ALU.add).then_inc(kv.sem, 1)
                if has(1, t):
                    b, j = t + 1, 1 - p
                    after(v, pr, b)
                    after(v, m1, b - 2)
                    v.tensor_tensor(QKV[:, j, :], bank[j][:, 0:384], BIAS[:, :], ALU.add).then_inc(qkv.sem, 1)
                    after(v, qkv, b)
                    after(v, ex, b - 1)
                    v.tensor_scalar(MN[:, :], QKV[:, j, 0:256], 0.0, None, ALU.min).then_inc(mn.sem, 1)
                if has(0, t):
                    fq3 = FQK[:, p, 0:P].rearrange("p (h d) -> p h d", d=8)
                    after(v, dq, t - 1)
                    v.tensor_reduce(KS[:, :], FQK[:, p, P:2 * P].rearrange("p (h d) -> p d h", d=8), AX, ALU.add).then_inc(ks.sem, 1)
                    after(v, ks, t)
                    v.tensor_tensor(DQ[:, :, :], fq3, KS[:, :].unsqueeze(1).to_broadcast([P, 16, 8]), ALU.mult).then_inc(dq.sem, 1)
                    after(v, dq, t)
                    v.tensor_reduce(DN[:, :], DQ[:, :, :], AX, ALU.add).then_inc(dn.sem, 1)
                    after(v, dn, t, 1)
                    v.tensor_scalar(DN[:, :], DN[:, :], 1e-6, None, ALU.add).then_inc(dn.sem, 1)
                    after(v, dn, t)
                    v.reciprocal(RD[:, :], DN[:, :]).then_inc(rd.sem, 1)
                if has(1, t):
                    b, j = t + 1, 1 - p
                    after(v, ex, b)
                    after(v, m2, b - 2)
                    v.scalar_tensor_tensor(FQK[:, j, :], QKV[:, j, 0:256], 0.0, EX[:, :], ALU.max, ALU.add).then_inc(fr.sem, 1)
                if has(-1, t):
                    b = t - 1
                    after(v, orr, b)
                    v.scalar_tensor_tensor(c.HT[:, tok(b, P)], bank[3][:, 0:P], BO[:, 0:1], c.HT[:, tok(b, P)], ALU.add, ALU.add)\
                        .then_inc(yr.sem, 1)
                if has(0, t):
                    after(v, m2, t)
                    v.tensor_reduce(NUM[:, :, :], M2[:, :, :, :], AX, ALU.add).then_inc(num.sem, 1)
                    after(v, num, t)
                    after(v, tr, t - 2)
                    v.tensor_tensor(AT[:, p, :].rearrange("p (h e) -> p h e", h=16), NUM[:, :, :],
                                    RD[:, :].unsqueeze(2).to_broadcast([P, 16, 8]), ALU.mult).then_inc(at.sem, 1)
            steps(v, step)
    close(c, S, N)


def ffn(c, cfg):
    with ExitStack() as ctx:
        sb = lambda nm, shape, dt=F32: c.sb(cfg["name"] + nm, shape, dt, ctx)
        NCH, E = cfg["NCH"], cfg.get("E")
        NT = sb("NT", [P, NTOK])
        W1, W2 = sb("W1", [P, NCH * P]), sb("W2", [P, NCH, P])
        W3 = sb("W3", [P, NCH * P]) if cfg["glu"] else None
        w_in = c.sem(cfg["name"] + "w_in")
        loads = [(W1[:, :], cfg["w1"], w_in), (W2[:, :, :].rearrange("p m d -> p (m d)"), cfg["w2"], w_in)]
        if cfg["glu"]:
            loads.append((W3[:, :], cfg["w3"], w_in))
        CB3 = sb("CB3", [P, 2 if E == 64 else 1, NTOK], BF16) if E else None
        CBF = sb("CBF", [8, NTOK]) if cfg.get("ebias") else None
        with ExitStack() as inner:
            LG = c.sb(cfg["name"] + "LG", [P, NT_TILES, E], F32, inner) if E else None
            norm_phase(c, cfg, NT, LG, loads)
            if E:
                combine_phase(c, cfg, LG, CB3, CBF)
        experts_phase(c, cfg, NT, W1, W3, W2, CB3, CBF, w_in, len(loads))


_OUT = (NB, T, D)


def build(nc, ins, out, upto=tuple("0A 0F 1A 1F 2A 2F 3A 3F".split())):
    with ExitStack() as ctx:
        c = Chip(nc, ctx, ins)
        nc.disable_value_cache = True
        start_phase(c, ins["x"])
        ln = dict(centered=True, eps=1e-5)
        xnorm = dict(nsrc=c.XT, ncentered=True, neps=1e-5)
        hnorm = dict(nsrc=c.HT, ncentered=True, neps=1e-5)
        rms = dict(nsrc=c.HT, ncentered=False, neps=1.1920928955078125e-07)
        if "0A" in upto:
            attention_phase(c, dict(ln, name="a0", layer=0, NH=16, HK=16, HV=16, VW=8, CW=128, causal=True,
                                    gate="gate0", wq="wq0", wk="wk0", wv="wv0", wo="wo0", src=c.XT, dst=c.XT))
        if "0F" in upto:
            ffn(c, dict(xnorm, name="f0", layer=0, nmod=3, gmod=5, wr="wr0", E=64, kind=0, CAP=128, NCH=32,
                        sel=list(range(32)), glu=True, fn=ACT.Silu, w1="w1_0", w3="w3_0", w2="w2_0", selector="sel0"))
        if "1A" in upto:
            attention_phase(c, dict(ln, name="a1", layer=1, NH=32, HK=32, HV=16, VW=16, CW=256, causal=True, diff=True,
                                    cscale="cscale", wq="wq1", wk="wk1", wv="wv1", wo="wo1", src=c.XT, dst=c.XT))
        if "1F" in upto:
            ffn(c, dict(xnorm, name="f1", layer=1, nmod=3, gmod=5, wr="wr1", E=8, kind=1, renorm=True, NCH=36,
                        sel=[m // 4 for m in range(32)] + [None] * 4, glu=False, fn=ACT.Gelu_apprx_tanh,
                        w1="w1_1", w2="w2_1", selector="sel1", hbias="hb1", ybias="yb1", ebias="eb1"))
        if "2A" in upto:
            attention_phase(c, dict(ln, name="a2", layer=2, NH=16, HK=1, HV=1, VW=8, CW=128, causal=False,
                                    bq="bq2", bv="bv2", bo="bo2", wq="wq2", wk="wk2", wv="wv2", wo="wo2", src=c.XT, dst=c.XT))
        if "2F" in upto:
            norm_phase(c, dict(xnorm, name="h2", layer=2, nmod=3), c.HT)
            attention_phase(c, dict(name="a4", layer=2, centered=False, eps=rms["neps"], NH=16, HK=16, HV=4, VW=8, CW=128,
                                    causal=True, rope=True, plain=True, gain="g1", wq="wq4", wk="wk4", wv="wv4", wo="wo4",
                                    src=c.HT, dst=c.HT))
            ffn(c, dict(rms, name="f2", layer=2, gmod=5, ngain="g2", wr="wr2", E=4, kind=1, renorm=True, NCH=12,
                        sel=[m // 3 for m in range(12)], glu=True, fn=ACT.Silu, w1="w1_2", w3="w3_2", w2="w2_2",
                        selector="sel2", plus=True))
        if "3A" in upto:
            norm_phase(c, dict(xnorm, name="h3", layer=3, nmod=0), c.HT)
            with ExitStack() as part:
                NT = c.sb("NT3", [P, NTOK], F32, part)
                norm_phase(c, dict(hnorm, name="i3", ngain="ln1w", nshift="ln1b"), NT)
                linear_attention_phase(c, NT)
            ffn(c, dict(hnorm, name="f4", layer=3, gmod=2, ngain="ln2w", nshift="ln2b", NCH=4, sel=[None] * 4, glu=False,
                        fn=ACT.Gelu, w1="w1_4", w2="w2_4", hbias="hb4", ybias="yb4", plus=True))
        if "3F" in upto:
            ffn(c, dict(xnorm, name="f3", layer=3, nmod=3, gmod=5, wr="wr3", E=8, kind=1, renorm=False, NCH=11,
                        sel=list(range(11)), glu=True, fn=ACT.Silu, w1="w1_3", w3="w3_3", w2="w2_3", selector="sel3"))
        end_phase(c, out)


def layout(x):
    f = lambda a: np.ascontiguousarray(np.asarray(a))
    heads = lambda w, n: f(w.reshape(-1, n // 16, 16, HD).transpose(0, 1, 3, 2).reshape(w.shape[0], -1))
    col = lambda a: f(np.asarray(a).reshape(-1, 1))
    i = {"consts": constants(), "x": f(x["L0_attn_x"]), "zero": np.zeros((P, 1), np.float32)}
    for l in range(4):
        i[f"cT{l}"] = f(x[f"L{l}_c"].T)
        i[f"wmod{l}"] = f(x[f"L{l}_wmod"])
    w = x["L0_attn_w_qkv"]
    i["wq0"], i["wk0"], i["wv0"], i["wo0"] = heads(w[:, 0:D], 16), heads(w[:, D:2 * D], 16), f(w[:, 2 * D:]), f(x["L0_attn_w_out"])
    i["gate0"] = col(x["L0_attn_bandha_gate"])
    hm, oh = np.zeros((P, P), np.float32), np.zeros((P, T), np.float32)
    for h in range(16):
        cycle = (5, 6, 7, 8)[h % 4]
        for k in range(8):
            hm[h * 8 + k, h::16] = 1.0
            oh[h * 8 + k] = np.arange(T) % cycle == k
    i["headmask"], i["phases"] = hm, oh
    i["wq1"], i["wk1"], i["wv1"] = heads(x["L1_attn_Wq"], 32), heads(x["L1_attn_Wk"], 32), f(x["L1_attn_Wv"])
    i["wo1"] = f(x["L1_attn_Wo"].reshape(2, P, D).transpose(1, 0, 2).reshape(P, 2 * D))
    for n, key in enumerate(("q1", "k1", "q2", "k2")):
        i[f"lam{n}"] = f(np.broadcast_to(x[f"L1_attn_lambda_{key}"].reshape(1, -1), (P, 128)))
    i["cscale"] = col(np.tile(x["L1_attn_rms_scale"], 8))
    i["wq2"], i["wk2"], i["wv2"], i["wo2"] = heads(x["L2_attn_Wq"].T, 16), f(x["L2_attn_Wk"].T), f(x["L2_attn_Wv"].T), f(x["L2_attn_Wo"].T)
    i["bq2"] = col(x["L2_attn_bq"].reshape(16, 8).T)
    i["bv2"] = f(np.broadcast_to(x["L2_attn_bv"], (P, 8)))
    i["bo2"] = col(x["L2_attn_bo"])
    swap = lambda w: w.reshape(D, -1, 2, HD // 2)[:, :, ::-1].reshape(w.shape)
    wq, wk = x["L2_ffn_wq"], np.repeat(x["L2_ffn_wk"].reshape(D, 4, HD), 4, axis=1).reshape(D, -1)
    i["wq4"] = f(np.concatenate([heads(wq, 16), heads(swap(wq), 16)], 1))
    i["wk4"] = f(np.concatenate([heads(wk, 16), heads(swap(wk), 16)], 1))
    i["wv4"], i["wo4"], i["g1"], i["g2"] = f(x["L2_ffn_wv"]), f(x["L2_ffn_wo"]), col(x["L2_ffn_g1"]), col(x["L2_ffn_g2"])
    i["wqkv3"] = f(np.concatenate([x[f"L3_attn_w{k}"] for k in "qkv"], 1))
    i["bqkv3"] = f(np.broadcast_to(np.concatenate([x[f"L3_attn_b{k}"] for k in "qkv"]), (P, 3 * D)))
    i["wo3"], i["bo3"] = f(x["L3_attn_wo"]), col(x["L3_attn_bo"])
    for n in ("ln1", "ln2"):
        i[n + "w"], i[n + "b"] = col(x[f"L3_attn_{n}_w"]), col(x[f"L3_attn_{n}_b"])
    up = lambda w: f(w.transpose(1, 0, 2).reshape(D, -1))
    down = lambda w: f(w.reshape(-1, P, D).transpose(1, 0, 2).reshape(P, -1))
    chunks = lambda b: f(b.reshape(-1, P).T)
    i["w1_0"], i["w3_0"], i["w2_0"] = up(x["L0_ffn_w_gate"]), up(x["L0_ffn_w_up"]), down(x["L0_ffn_w_down"])
    i["wr0"], i["rbias"] = f(x["L0_ffn_gate_w"].T), f(np.broadcast_to(x["L0_ffn_gate_bias"], (P, 64)))
    i["w1_1"] = f(np.concatenate([up(x["L1_ffn_Wfc"]), x["L1_ffn_Wfc_s"]], 1))
    i["w2_1"] = f(np.concatenate([down(x["L1_ffn_Wproj"]), down(x["L1_ffn_Wproj_s"])], 1))
    i["hb1"] = f(np.concatenate([chunks(x["L1_ffn_bfc"]), chunks(x["L1_ffn_bfc_s"])], 1))
    i["wr1"], i["yb1"], i["eb1"] = f(x["L1_ffn_Wr"]), col(x["L1_ffn_bproj_s"]), f(x["L1_ffn_bproj"])
    i["w1_2"], i["w3_2"], i["w2_2"], i["wr2"] = up(x["L2_ffn_w1"]), up(x["L2_ffn_w3"]), down(x["L2_ffn_w2"]), f(x["L2_ffn_gate"])
    i["w1_3"], i["w3_3"], i["w2_3"], i["wr3"] = up(x["L3_ffn_w1"]), up(x["L3_ffn_w3"]), down(x["L3_ffn_w2"]), f(x["L3_ffn_w_router"].T)
    i["w1_4"], i["w2_4"] = f(x["L3_attn_fc_w"]), down(x["L3_attn_proj_w"])
    i["hb4"], i["yb4"] = chunks(x["L3_attn_fc_b"]), col(x["L3_attn_proj_b"])
    i["low8"] = f(np.broadcast_to((np.arange(8)[None, :] < np.arange(8)[:, None]).astype(np.float32).reshape(1, 64), (P, 64)))
    i["sel0"], i["sel1"], i["sel2"], i["sel3"] = selector(64, 64, 32), selector(8, 128, 8), selector(4, 128, 4), selector(8, 176, 11)
    return i


def selector(E, width, n):
    s = np.zeros((P, n, P), np.float32)
    step = 64 if E == 64 else 32
    for m in range(n):
        for p in range(P):
            s[(m * P + p) // width:P:step, m, p] = 1.0
    return s.reshape(P, -1)


def kernel(**inputs):
    import concourse.bacc as _bacc
    from concourse.bass_utils import run_bass_kernel_spmd as _run

    nc = _bacc.Bacc("TRN2", target_bir_lowering=False, num_devices=1)
    arrays = layout(inputs)
    ins = {n: nc.dram_tensor(f"in_{n}", a.shape, mybir.dt.from_np(a.dtype), kind="ExternalInput").ap()
           for n, a in arrays.items()}
    out = nc.dram_tensor("out_0", _OUT, F32, kind="ExternalOutput").ap()
    build(nc, ins, out, *UPTO)
    r = _run(nc, [{f"in_{n}": a for n, a in arrays.items()}], core_ids=[0])
    return r.results[0]["out_0"]


UPTO = ()
```

```python
from contextlib import ExitStack

import numpy as np
import concourse.bass as bass
from concourse import mybir

P = 128
F32 = mybir.dt.float32
BF16 = mybir.dt.bfloat16
ALU = mybir.AluOpType
ACT = mybir.ActivationFunctionType
AX = mybir.AxisListType.X

NB, T, D = 16, 256, 128
NTOK = NB * T
HD = 8
NEG = -1.0e30
PAIRS = [(0, 0), (0, 1), (1, 0), (0, 2), (2, 0), (1, 1)]
ROWS = HD * len(PAIRS)
MROW = 66
KROWS = MROW + 3

C_ID, C_MEAN, C_MQ, C_MK, C_TRI, C_COS, C_SIN = 0, 128, 256, 384, 512, 640, 896
C_END = C_SIN + T


def constants():
    c = np.zeros((P, C_END), np.float32)
    i = np.arange(P)
    c[:, C_ID:C_ID + P] = np.eye(P)
    c[:, C_MEAN:C_MEAN + P] = 1.0 / D
    c[:, C_MQ:C_MQ + P] = np.where(i[None, :] > i[:, None], NEG, 0.0)
    c[:, C_MK:C_MK + P] = np.where(i[:, None] > i[None, :], NEG, 0.0)
    c[:, C_TRI:C_TRI + P] = (i[:, None] < i[None, :])
    freq = (1.0 / 10000.0 ** (np.arange(0, HD, 2, dtype=np.float32) / HD)).astype(np.float32)
    ang = (np.arange(T, dtype=np.float32)[None, :] * freq[:, None]).astype(np.float32)
    cos, sin = np.cos(ang), np.sin(ang)
    for r in range(P):
        d = r // 16 % HD
        c[r, C_COS:C_COS + T] = cos[d % 4]
        c[r, C_SIN:C_SIN + T] = sin[d % 4] * (-1.0 if d < 4 else 1.0)
    return c


class Chip:

    def __init__(self, nc, ctx, ins):
        self.nc, self.ctx, self.ins = nc, ctx, ins
        self.sems, self.free = {}, []
        self.XT = self.sb("XT", [P, NTOK])
        self.HT = self.sb("HT", [P, NTOK])
        self.CST = self.sb("CST", [P, C_END])
        self.IDB = self.sb("IDB", [P, P], BF16)
        self.MASKS = self.sb("MASKS", [P, 2, 2, P], BF16)
        self.MOD = self.sb("MOD", [P, 4, 6, NB])
        self.HALF = self.sb("HALF", [P, 64])
        self.ONES = self.sb("ONES", [P, P])
        self.counts = {k: 0 for k in ("in", "act", "step", "run", "pos", "val", "t", "hi", "res", "mid", "lo", "z", "tm")}
        self.bank = [ctx.enter_context(nc.psum_tensor(f"bank{i}", [P, 512], F32)) for i in range(8)]
        self.ID = self.CST[:, C_ID:C_ID + P]
        self.MEAN = self.CST[:, C_MEAN:C_MEAN + P]

    def sb(self, name, shape, dt=F32, ctx=None):
        return (ctx or self.ctx).enter_context(self.nc.sbuf_tensor(name, shape, dt))

    def sem(self, name):
        if name not in self.sems:
            self.sems[name] = self.ctx.enter_context(self.nc.semaphore(name))
        return self.sems[name]


def start_phase(c, x_in):
    nc, b = c.nc, c.bank
    G = 4
    NG = NTOK // (G * P)
    with ExitStack() as ctx:
        WM = c.sb("WM", [P, 4, 6 * D], ctx=ctx)
        CT = c.sb("CTm", [P, 4, NB], ctx=ctx)
        SC = c.sb("SCm", [P, 4, NB], ctx=ctx)
        SG = c.sb("SGm", [P, 4, 2, NB], ctx=ctx)
        AG = c.sb("AGm", [P, 4, 2, NB], ctx=ctx)
        XS = c.sb("XS", [P, NG, G, D], ctx=ctx)
        const_in, mod_in, x_landed = c.sem("const_in"), c.sem("mod_in"), [c.sem(f"landed{g}") for g in range(NG)]
        const_ready, silu_ready, mod_mm, mod_copied, mod_done, sign_done = (
            c.sem(n) for n in ("const_ready", "silu_ready", "mod_mm", "mod_copied", "mod_done", "sign_done"))
        x_turned, x_copied = c.sem("x_turned"), c.sem("x_copied")
        xv = x_in.rearrange("b (g p) d -> p (b g) d", p=P)
        block = ctx.enter_context(nc.Block())

        @block.sync
        def _(sp):
            sp.dma_start(c.CST[:, :], c.ins["consts"]).then_inc(const_in, 16)
            for g in range(NG):
                sp.dma_start(XS[:, g, :, :], xv[:, g * G:(g + 1) * G, :]).then_inc(x_landed[g], 16)

        @block.scalar
        def _(act):
            for l in range(4):
                act.dma_start(CT[:, l, :], c.ins[f"cT{l}"]).then_inc(mod_in, 16)
                act.dma_start(WM[:, l, :], c.ins[f"wmod{l}"]).then_inc(mod_in, 16)
            act.wait_ge(mod_in, 16 * 8)
            nc.scalar.activation(SC[:, :, :], CT[:, :, :], ACT.Silu).then_inc(silu_ready, 1)

        @block.gpsimd
        def _(pool):
            nc.gpsimd.memset(c.HALF[:, :], -0.5).then_inc(const_ready, 1)
            nc.gpsimd.memset(c.ONES[:, :], 1.0).then_inc(const_ready, 1)

        @block.tensor
        def _(pe):
            pe.wait_ge(const_in, 16)
            for g in range(NG):
                pe.wait_ge(x_landed[g], 16)
                if g >= 2:
                    pe.wait_ge(x_copied, g - 1)
                for k in range(G):
                    m = pe.transpose(b[g % 2][:, k * P:(k + 1) * P], XS[:, g, k, :], c.ID)
                m.then_inc(x_turned, 1)
            pe.wait_ge(silu_ready, 1)
            for l in range(4):
                for j in range(6):
                    m = pe.matmul(b[2][:, (l * 6 + j) * NB:(l * 6 + j + 1) * NB],
                                  WM[:, l, j * D:(j + 1) * D], SC[:, l, :], start=True, stop=True)
            m.then_inc(mod_mm, 1)

        @block.vector
        def _(v):
            v.wait_ge(const_in, 16)
            v.tensor_copy(c.IDB[:, :], c.ID).then_inc(const_ready, 1)
            for k in range(2):
                v.tensor_copy(c.MASKS[:, 0, k, :], c.CST[:, C_MQ:C_MQ + P]).then_inc(const_ready, 1)
                v.tensor_copy(c.MASKS[:, 1, k, :], c.CST[:, C_MK:C_MK + P]).then_inc(const_ready, 1)
            for g in range(NG):
                v.wait_ge(x_turned, g + 1)
                v.tensor_copy(c.XT[:, g * G * P:(g + 1) * G * P], b[g % 2][:, :]).then_inc(x_copied, 1)
            v.wait_ge(mod_mm, 1)
            v.tensor_copy(c.MOD[:, :, :, :].rearrange("p l j b -> p (l j b)"), b[2][:, 0:24 * NB]).then_inc(mod_copied, 1)
            v.wait_ge(mod_copied, 1)
            for n, j in enumerate((2, 5)):
                g = c.MOD[:, :, j, :]
                v.scalar_tensor_tensor(AG[:, :, n, :], g, -1.0, g, ALU.mult, ALU.max).then_inc(sign_done, 1)
                v.tensor_scalar(SG[:, :, n, :], g, 0.0, 2.0, ALU.is_ge, ALU.mult).then_inc(sign_done, 1)
                v.wait_ge(sign_done, 4 * n + 2)
                v.tensor_scalar(SG[:, :, n, :], SG[:, :, n, :], -1.0, None, ALU.add).then_inc(sign_done, 1)
                v.tensor_scalar(AG[:, :, n, :], AG[:, :, n, :], 0.25, None, ALU.max).then_inc(sign_done, 1)
                v.wait_ge(sign_done, 4 * n + 4)
                v.tensor_tensor(g, AG[:, :, n, :], SG[:, :, n, :], ALU.mult).then_inc(mod_done, 1)
            for j in (1, 4):
                v.tensor_scalar(c.MOD[:, :, j, :], c.MOD[:, :, j, :], 1.0, None, ALU.add).then_inc(mod_done, 1)


def end_phase(c, out):
    nc, b = c.nc, c.bank
    G = 4
    NG = NTOK // (G * P)
    ov = out.rearrange("b (g p) d -> p (b g) d", p=P)
    with ExitStack() as ctx:
        XS = c.sb("XO", [P, NG, G, D], ctx=ctx)
        o_turned, o_copied, o_out = c.sem("o_turned"), c.sem("o_copied"), c.sem("o_out")
        block = ctx.enter_context(nc.Block())

        @block.tensor
        def _(pe):
            for g in range(NG):
                if g >= 2:
                    pe.wait_ge(o_copied, g - 1)
                for k in range(G):
                    t = g * G + k
                    m = pe.transpose(b[g % 2][:, k * P:(k + 1) * P], c.XT[:, t * P:(t + 1) * P], c.ID)
                m.then_inc(o_turned, 1)

        @block.vector
        def _(v):
            for g in range(NG):
                v.wait_ge(o_turned, g + 1)
                v.tensor_copy(XS[:, g, :, :].rearrange("p k d -> p (k d)"), b[g % 2][:, :]).then_inc(o_copied, 1)

        @block.sync
        def _(sp):
            for g in range(NG):
                sp.wait_ge(o_copied, g + 1)
                sp.dma_start(ov[:, g * G:(g + 1) * G, :], XS[:, g, :, :]).then_inc(o_out, 16)
            sp.wait_ge(o_out, 16 * NG)


class Signal:

    def __init__(self, sem):
        self.sem, self.base, self.per = sem, 0, 1

    def value(self, b, k=None):
        return b * self.per + (self.base + (self.per if k is None else k))


def after(eng, signal, b, k=None):
    value = signal.value(b, k)
    if not isinstance(value, int) or value > 0:
        eng.wait_ge(signal.sem, value)


def signals(c, **per):
    found = []
    for name, n in per.items():
        s = c.free.pop() if c.free else Signal(c.sem(name))
        s.per = n
        found.append(s)
    return found


def close(c, found, n=NB):
    for s in found:
        s.base += n * s.per
    c.free.extend(reversed(found))


def attention_phase(c, cfg):
    nc, bank = c.nc, c.bank
    NH, HK, HV, VW = cfg["NH"], cfg["HK"], cfg["HV"], cfg["VW"]
    causal, rope, diff = cfg["causal"], cfg.get("rope"), cfg.get("diff")
    centered, eps = cfg["centered"], cfg["eps"]
    R = NH // 16
    KR = HD * min(HK, 16)
    QK = 2 if rope else R
    U = NH // 16
    DF = int(bool(diff))
    NS = NH // 4
    R2 = cfg["CW"] // P
    OW = VW + 1
    kof = lambda h: h * HK // NH
    vof = lambda h: h * HV // NH
    NC = 3 * P if causal else 4 * P
    SCALE = float(HD) ** -0.5
    l = cfg["layer"]
    SRC, DST = cfg["src"], cfg["dst"]

    with ExitStack() as ctx:
        sb = lambda name, shape, dt=F32: c.sb(cfg["name"] + name, shape, dt, ctx)
        QH = sb("QH", [KROWS, 3, NH, T], BF16)
        KH = sb("KH", [KROWS, 3, HK, T], BF16)
        VX = sb("VX", [P, 3, 2, HV, 32])
        PR = sb("PR", [P, 4, NC])
        XC, SQ, XN, H = (sb(n, [P, T]) for n in ("XC", "SQ", "XN", "H"))
        VE, RS, DG = sb("VE", [P, 2]), sb("RS", [P, 2]), sb("DG", [P, 2, P])
        QKF = sb("QKF", [P, 2, T])
        RES = sb("RES", [P, 2, T])
        SPL = sb("SPL", [P, R, 3, 2, T], BF16)
        NM3 = sb("NM3", [P, NH, 3])
        NMQ = sb("NMQ", [P, 2, NH])
        MF, MR = sb("MF", [NH, T]), sb("MR", [NH, T])
        M3 = sb("M3", [NH, 3, T], BF16)
        CTS = sb("CTS", [P, 2, T])
        RC = sb("RC", [P, 2, 4])
        CX = sb("CX", [P, 3, 2, cfg["CW"] // VW, VW])
        CTT = sb("CTT", [P, R2, T])
        TMP = sb("TMP", [P, T])
        ONE = sb("ONE", [3, T], BF16)
        WQ = sb("WQ", [P, (2 if rope else 1) * R * P])
        WK = sb("WK", [P, (2 if rope else 1) * (R * P if HK > 1 else HD)])
        WV = sb("WV", [P, HV * VW])
        WO = sb("WO", [P, R2, D])
        COL = sb("COL", [P, 4])
        if cfg.get("bv"):
            BV = sb("BV", [P, HV * VW])
        if cfg.get("gate"):
            HM, OH, SG, SGM, GATE = sb("HM", [P, P]), sb("OH", [P, T]), sb("SG", [P, 1]), sb("SGM", [P, P]), sb("GATE", [P, T])
        if diff:
            CX2 = sb("CX2", [P, 2, 4, VW])
            LQ = sb("LQ", [P, 4, 16, HD])
            LS, LE, NLAM = sb("LS", [P, 2, 16]), sb("LE", [P, 2, 16]), sb("NLAM", [P, 16])
            CSQ = sb("CSQ", [P, 2, 16, VW])
            CM, CR = sb("CM", [P, 2, 16]), sb("CR", [P, 2, 16])

        w_in, ones_in, zeroed, q_zeroed, vx_ones, sg_ready, sgm_ready, gate_mm, gate_ready, ls_ready, le_ready, lam_ready = (
            c.sem(cfg["name"][0:2] + n) if n in ("w_in", "ones_in", "zeroed", "q_zeroed", "vx_ones") else c.sem(n)
            for n in ("w_in", "ones_in", "zeroed", "q_zeroed", "vx_ones", "sg_ready", "sgm_ready", "gate_mm", "gate_ready",
                      "ls_ready", "le_ready", "lam_ready"))
        S = signals(c, mean_ready=int(centered), xc_ready=int(centered), sq_ready=1, var_ready=1, ve_ready=1, rs_ready=1, dg_ready=1, bc_ready=1,
                    xn_ready=1, h_ready=1, qk_ready=QK, qk_copied=QK, half_ready=int(bool(rope)), rope_ready=int(bool(rope)),
                    hi_ready=R, res_ready=R, mid_ready=R, lo_ready=R, parts_sent=16 * 12, parts_sent_1=16 * 12 * (R - 1),
                    v_ready=1, v_copied=1, s_ready=NH, s_used=NH, nmq_ready=2 * int(causal), mt_ready=1, mf_ready=1,
                    mhi_ready=1, mres_ready=1, mmid_ready=1, mlo_ready=1, m_sent=16 * 3,
                    st_ready=NH, p_ready=NH, pv_done=NH, ct_ready=NS, t_ready=NS, rc_ready=NS, cx_ready=NS,
                    dif_ready=2 * NS * DF, csq_ready=DF, cm_ready=2 * DF, cr_ready=DF, cxn_ready=DF,
                    ctt_ready=1, ctt_copied=1, o_ready=1, tmp_ready=1, x_updated=1)
        (mean_ready, xc_ready, sq_ready, var_ready, ve_ready, rs_ready, dg_ready, bc_ready, xn_ready, h_ready, qk_ready,
         qk_copied, half_ready, rope_ready, hi_ready, res_ready, mid_ready, lo_ready, parts_sent_0, parts_sent_1,
         v_ready, v_copied, s_ready, s_used, nmq_ready, mt_ready, mf_ready, mhi_ready, mres_ready,
         mmid_ready, mlo_ready, m_sent, st_ready, p_ready, pv_done, ct_ready, t_ready, rc_ready,
         cx_ready, dif_ready, csq_ready, cm_ready, cr_ready, cxn_ready, ctt_ready, ctt_copied,
         o_ready, tmp_ready, x_updated) = S
        parts_sent = (parts_sent_0, parts_sent_1)[:R]
        f_ready = rope_ready if rope else qk_copied

        loads = [(WQ[:, :], cfg["wq"]), (WK[:, :], cfg["wk"]), (WV[:, :], cfg["wv"]),
                 (WO[:, :, :].rearrange("p r d -> p (r d)"), cfg["wo"])]
        for n, key in enumerate(("bq", "bo", "cscale", "gain")):
            loads.append((COL[:, n:n + 1], cfg.get(key) or "zero"))
        if cfg.get("bv"):
            loads.append((BV[:, :], cfg["bv"]))
        if cfg.get("gate"):
            loads += [(HM[:, :], "headmask"), (OH[:, :], "phases"), (SG[:, :], cfg["gate"])]
        if diff:
            loads += [(LQ[:, n, :, :].rearrange("p h d -> p (h d)"), f"lam{n}") for n in range(4)]
        NW = 16 * len(loads)
        has = lambda stage, t: not isinstance(t, int) or 0 <= t + stage < NB
        tok = lambda b: slice(b * T, (b + 1) * T) if isinstance(b, int) else bass.ds(b * T, T)
        one = lambda b: slice(b, b + 1) if isinstance(b, int) else bass.ds(b, 1)

        def steps(eng, step):
            for t in range(-2, 2):
                step(t, t % 3)
            with eng.Fori(0, 4) as i:
                for k in range(2, 5):
                    step(i * 3 + k, k % 3)
            for t in range(14, 17):
                step(t, t % 3)

        L_MEAN, L_VAR, L_POW, L_DG, L_BC, L_XN, L_QK, L_V = 0, 2, 2, 3 * U, 4 * U, 5 * U, 6 * U, 10 * U + 2
        L_SPLIT = [10] if rope else [L_QK + 2 + 2 * r * U for r in range(R)]
        L_SCORES = 2
        N_SCORES = cfg["score_slots"]
        heads_at = lambda h: range(*(min(max(k - L_SCORES, 0), N_SCORES) * NH // N_SCORES for k in (h, h + 1)))
        L_NMQ = L_SCORES + N_SCORES
        L_MT = L_NMQ
        L_MSPLIT = L_MT + 1
        L_LAST, L_COMBINE = 1, 2
        L_CTT, L_OUT, L_TMP = (9, 10, 10) if diff else (3, 4, 5)
        out_at = int(bool(diff))
        turn_at = {4 * s + 7: s for s in range(NS - 1)}
        S_MT = (L_MT - 8) // 4

        nc.disable_value_cache = True
        block = ctx.enter_context(nc.Block())

        @block.sync
        def _(sp):
            for dst, src in loads:
                sp.dma_start(dst, c.ins[src]).then_inc(w_in, 16)

            def send_maxima(t, m):
                after(sp, mlo_ready, t + 1)
                for a in range(3):
                    sp.dma_start(QH[MROW + a:MROW + a + 1, (m + 1) % 3, :, :], M3[:, a, :]).then_inc(m_sent.sem, 16)

            def step(t, m):
                if isinstance(t, int) and t <= 0:
                    sp.wait_ge(zeroed, 4 + (t + 2))
                    sp.wait_ge(q_zeroed, 1 + (t + 2))
                    sp.dma_start(KH[MROW:KROWS, t + 2, :, :], ONE[:, :].unsqueeze(1).to_broadcast([3, HK, T])).then_inc(ones_in, 16)
                if not has(2, t) and has(1, t):
                    send_maxima(t, m)
                if has(2, t):
                    b, j = t + 2, (m + 2) % 3
                    for r in range(R):
                        after(sp, pv_done, b - 3)
                        for a, ready in enumerate((hi_ready, mid_ready, lo_ready)):
                            if has(1, t) and r == R - 1 and a == 2:
                                send_maxima(t, m)
                            after(sp, ready, b, r + 1)
                            for n, pair in enumerate(PAIRS):
                                rows = slice(HD * n, HD * n + HD)
                                if pair[0] == a:
                                    sp.dma_start(QH[rows, j, 16 * r:16 * r + 16, :], SPL[:, r, a, 0, :]).then_inc(parts_sent[r].sem, 16)
                                if pair[1] == a:
                                    sp.dma_start(KH[rows, j, 16 * r:16 * r + min(HK, 16), :], SPL[0:KR, r, a, 1, :]).then_inc(parts_sent[r].sem, 16)
            steps(sp, step)

        @block.gpsimd
        def _(pool):
            nc.gpsimd.memset(ONE[:, :], 1.0).then_inc(zeroed, 1)
            nc.gpsimd.memset(QKF[:, :, :], 0.0).then_inc(zeroed, 1)
            nc.gpsimd.memset(VX[:, :, :, :, :], 0.0).then_inc(zeroed, 1)
            zero_k = lambda j: nc.gpsimd.memset(KH[:, j, :, :].rearrange("p h t -> p (h t)").bitcast(F32), 0.0).then_inc(zeroed, 1)
            zero_k(0)
            pool.wait_ge(zeroed, 3)
            nc.gpsimd.memset(VX[:, :, :, :, VW:OW], 1.0).then_inc(vx_ones, 1)

            def step(t, m):
                for h in range(NH):
                    if has(2, t):
                        b = t + 2
                        if h == L_POW:
                            after(pool, ve_ready, b)
                            after(pool, dg_ready, b - 1)
                            nc.gpsimd.tensor_tensor(RS[:, :], VE[:, :], c.HALF[:, 0:2], ALU.pow).then_inc(rs_ready.sem, 1)
                        for n in range(2 if rope else 0):
                            if h == L_QK + 1 + 2 * n:
                                after(pool, qk_copied, b, n + 1)
                                nc.gpsimd.tensor_tensor(QKF[:, n, :], RES[:, 0, :], RES[:, 1, :], ALU.add)\
                                    .then_inc((half_ready, rope_ready)[n].sem, 1)
                        for r in range(R):
                            if h == L_SPLIT[r]:
                                after(pool, hi_ready, b, r + 1)
                                after(pool, lo_ready, b, r)
                                nc.gpsimd.tensor_tensor(RES[:, :, :], QKF[:, :, :], SPL[:, r, 0, :, :], ALU.subtract)\
                                    .then_inc(res_ready.sem, 1)
                                after(pool, mid_ready, b, r + 1)
                                nc.gpsimd.tensor_tensor(SPL[:, r, 2, :, :], RES[:, :, :], SPL[:, r, 1, :, :], ALU.subtract)\
                                    .then_inc(lo_ready.sem, 1)
                    if has(1, t) and h == L_MSPLIT:
                        b = t + 1
                        after(pool, mhi_ready, b)
                        nc.gpsimd.tensor_tensor(MR[:, :], MF[:, :], M3[:, 0, :], ALU.subtract).then_inc(mres_ready.sem, 1)
                        after(pool, mmid_ready, b)
                        nc.gpsimd.tensor_tensor(M3[:, 2, :], MR[:, :], M3[:, 1, :], ALU.subtract).then_inc(mlo_ready.sem, 1)
                    if diff and has(-1, t) and h == L_COMBINE:
                        after(pool, cm_ready, t - 1)
                        nc.gpsimd.tensor_tensor(CR[:, :, :].rearrange("p a h -> p (a h)"), CM[:, :, :].rearrange("p a h -> p (a h)"),
                                                c.HALF[:, 0:32], ALU.pow).then_inc(cr_ready.sem, 1)
                if isinstance(t, int) and t < 0:
                    zero_k(t + 3)
            steps(pool, step)

        @block.scalar
        def _(act):
            if cfg.get("gate"):
                act.wait_ge(w_in, NW)
                nc.scalar.activation(SG[:, :], SG[:, :], ACT.Sigmoid).then_inc(sg_ready, 1)
            if diff:
                act.wait_ge(ls_ready, 2)
                nc.scalar.activation(LE[:, :, :], LS[:, :, :], ACT.Exp).then_inc(le_ready, 1)

            def copy_set(b, s):
                after(act, pv_done, b, 4 * s + 4)
                after(act, t_ready, b, s - 1)
                nc.scalar.copy(CTS[:, s % 2, :], bank[4 + s % 2][:, 0:T]).then_inc(ct_ready.sem, 1)

            def step(t, m):
                for h in range(NH):
                    if has(2, t):
                        b = t + 2
                        if h == L_MEAN:
                            if centered:
                                after(act, xc_ready, b)
                            after(act, var_ready, b - 1)
                            nc.scalar.activation(SQ[:, :], XC[:, :] if centered else SRC[:, tok(b)], ACT.Square)\
                                .then_inc(sq_ready.sem, 1)
                        if h == L_XN:
                            after(act, xn_ready, b)
                            after(act, v_ready, b - 1)
                            scale, shift = (c.MOD[:, l, 1, one(b)], c.MOD[:, l, 0, one(b)]) if centered else (COL[:, 3:4], 0.0)
                            nc.scalar.activation(H[:, :], XN[:, :], ACT.Identity, bias=shift, scale=scale).then_inc(h_ready.sem, 1)
                        if h == L_V + 1 and not cfg.get("bv"):
                            after(act, v_ready, b)
                            if isinstance(t, int) and t == -2:
                                act.wait_ge(vx_ones, 1)
                            after(act, pv_done, b - 3)
                            nc.scalar.copy(VX[:, (m + 2) % 3, :, :, 0:VW],
                                           bank[6][:, 0:2 * HV * VW].rearrange("p (n h d) -> p n h d", n=2, h=HV)).then_inc(v_copied.sem, 1)
                        for r in range(R):
                            if h == L_SPLIT[r]:
                                after(act, f_ready, b, None if rope else r + 1)
                                after(act, parts_sent[r], b - 1)
                                nc.scalar.copy(SPL[:, r, 0, :, :], QKF[:, :, :]).then_inc(hi_ready.sem, 1)
                            if h == L_SPLIT[r] + 1:
                                after(act, res_ready, b, r + 1)
                                nc.scalar.copy(SPL[:, r, 1, :, :], RES[:, :, :]).then_inc(mid_ready.sem, 1)
                    if has(1, t) and h == L_MSPLIT:
                        b = t + 1
                        after(act, mt_ready, b)
                        after(act, mlo_ready, b - 1)
                        nc.scalar.copy(MF[:, :], bank[7][0:NH, 0:T]).then_inc(mf_ready.sem, 1)
                        after(act, mf_ready, b)
                        after(act, m_sent, b - 1)
                        nc.scalar.copy(M3[:, 0, :], MF[:, :]).then_inc(mhi_ready.sem, 1)
                    if has(1, t) and h == L_MSPLIT + 1:
                        after(act, mres_ready, t + 1)
                        nc.scalar.copy(M3[:, 1, :], MR[:, :]).then_inc(mmid_ready.sem, 1)
                    if has(-1, t):
                        b = t - 1
                        if diff and h == L_COMBINE:
                            after(act, dif_ready, b)
                            nc.scalar.activation(CSQ[:, :, :, :], CX[:, (m - 1) % 3, :, :, :], ACT.Square).then_inc(csq_ready.sem, 1)
                        if h == L_CTT:
                            after(act, ctt_ready, b)
                            after(act, o_ready, b - 1)
                            nc.scalar.activation(CTT[:, :, :].rearrange("p r t -> p (r t)"), bank[7][:, 0:R2 * T], ACT.Identity,
                                                 scale=COL[:, 2:3] if diff else 1.0).then_inc(ctt_copied.sem, 1)
                    if has(0, t):
                        after(act, st_ready, t, h + 1)
                        after(act, pv_done, t, h - 3)
                        nc.scalar.activation(PR[:, h % 4, :], bank[2 + h % 2][:, 0:NC], ACT.Exp, scale=SCALE)\
                            .then_inc(p_ready.sem, 1)
                        if h >= 6 and (h - 6) % 4 == 0:
                            copy_set(t, (h - 6) // 4)
                if has(0, t):
                    copy_set(t, NS - 1)
            steps(act, step)

        @block.tensor
        def _(pe):
            pe.wait_ge(w_in, NW)
            if cfg.get("gate"):
                pe.wait_ge(sgm_ready, 1)
                pe.matmul(bank[6][:, 0:T], SGM[:, :], OH[:, :], start=True, stop=True).then_inc(gate_mm, 1)
                pe.wait_ge(gate_ready, 1)

            def scores(b, j, h):
                after(pe, s_used, b, h - 1)
                if h % 16 == 0:
                    after(pe, parts_sent[h // 16], b)
                o = bank[h % 2]
                q = lambda n: QH[0:MROW, j, h, n * P:(n + 1) * P]
                k = KH[0:MROW, j, kof(h), :]
                if causal:
                    pe.matmul(o[:, :].rearrange("p (n x) -> p n x", n=2)[:, :, 0:P], c.IDB[:, :], c.MASKS[:, 0, :, :],
                              start=True, stop=False, skip_group_check=True)
                    pe.matmul(o[:, 0:P], q(0), k[:, 0:P], start=False, stop=False, skip_group_check=True)
                    mm = pe.matmul(o[:, P:3 * P], q(1), k, start=False, stop=True, skip_group_check=True)
                else:
                    pe.matmul(o[:, 0:T], q(0), k, start=True, stop=True)
                    mm = pe.matmul(o[:, T:2 * T], q(1), k, start=True, stop=True)
                mm.then_inc(s_ready.sem, 1)

            def scores_t(b, j, h):
                after(pe, p_ready, b, h - 1)
                if h == 0:
                    after(pe, m_sent, b)
                o = bank[2 + h % 2]
                k = lambda n: KH[0:KROWS, j, kof(h), n * P:(n + 1) * P]
                q = QH[0:KROWS, j, h, :]
                if causal:
                    pe.matmul(o[:, :].rearrange("p (n x) -> p n x", n=2)[:, :, 0:P], c.IDB[:, :], c.MASKS[:, 1, :, :],
                              start=True, stop=False, skip_group_check=True)
                    pe.matmul(o[:, 0:T], k(0), q, start=False, stop=False, skip_group_check=True)
                    mm = pe.matmul(o[:, T:3 * P], k(1), q[:, P:T], start=False, stop=True, skip_group_check=True)
                else:
                    pe.matmul(o[:, 0:T], k(0), q, start=True, stop=True)
                    mm = pe.matmul(o[:, T:2 * T], k(1), q, start=True, stop=True)
                mm.then_inc(st_ready.sem, 1)

            def values(b, j, h):
                g, s = h % 4, h // 4
                after(pe, p_ready, b, h + 1)
                if g == 0:
                    after(pe, ct_ready, b, s - 1)
                o = bank[4 + s % 2][32 * g:32 * g + 32, :]
                v = lambda n: VX[:, j, n, vof(h), :]
                pe.matmul(o[:, 0:T], v(0), PR[:, h % 4, 0:T], start=True, stop=False)
                rest = (o[:, P:T], PR[:, h % 4, T:3 * P]) if causal else (o[:, 0:T], PR[:, h % 4, T:2 * T])
                pe.matmul(rest[0], v(1), rest[1], start=False, stop=True).then_inc(pv_done.sem, 1)

            def turn(b, s):
                after(pe, ct_ready, b, s + 1)
                for n in range(2):
                    mm = pe.transpose(bank[7][:, n * P:(n + 1) * P], CTS[:, s % 2, n * P:(n + 1) * P], c.ID)
                mm.then_inc(t_ready.sem, 1)

            def step(t, m):
                if isinstance(t, int) and t == 0:
                    pe.wait_ge(ones_in, 48)
                for h in range(NH):
                    if has(2, t):
                        b = t + 2
                        if h == L_MEAN and centered:
                            after(pe, v_copied, b - 1)
                            pe.matmul(bank[6][:, 0:T], c.MEAN, SRC[:, tok(b)], start=True, stop=True).then_inc(mean_ready.sem, 1)
                        if h == L_VAR:
                            after(pe, v_copied, b - 1)
                            after(pe, sq_ready, b)
                            for n in range(2):
                                mm = pe.matmul(bank[6][:, T + n:T + n + 1], SQ[:, n * P:(n + 1) * P], c.MEAN[:, 0:1],
                                               start=True, stop=True)
                            mm.then_inc(var_ready.sem, 1)
                        if h == L_BC:
                            after(pe, dg_ready, b)
                            for n in range(2):
                                mm = pe.matmul(bank[6][:, T + n * P:T + (n + 1) * P], c.ONES[:, :], DG[:, n, :], start=True, stop=True)
                            mm.then_inc(bc_ready.sem, 1)
                        for n in range(QK):
                            if h == L_QK + 2 * n * U:
                                after(pe, h_ready, b)
                                after(pe, qk_copied, b, n)
                                if rope:
                                    w = (WQ, WK)[n]
                                    pe.matmul(bank[6][:, 0:T], w[:, 0:P], H[:, :], start=True, stop=True)
                                    mm = pe.matmul(bank[6][:, T:2 * T], w[:, P:2 * P], H[:, :], start=True, stop=True)
                                else:
                                    pe.matmul(bank[6][:, 0:T], WQ[:, n * P:(n + 1) * P], H[:, :], start=True, stop=True)
                                    mm = pe.matmul(bank[6][0:KR, T:2 * T], WK[:, n * P:n * P + KR], H[:, :], start=True, stop=True)
                                mm.then_inc(qk_ready.sem, 1)
                        if h == L_V:
                            after(pe, qk_copied, b)
                            for n in range(2):
                                mm = pe.matmul(bank[6][:, n * HV * VW:(n + 1) * HV * VW], H[:, n * P:(n + 1) * P], WV[:, :],
                                               start=True, stop=True)
                            mm.then_inc(v_ready.sem, 1)
                    if has(1, t):
                        for n in heads_at(h):
                            scores(t + 1, (m + 1) % 3, n)
                    if has(0, t):
                        scores_t(t, m, h)
                        if h >= 2:
                            values(t, m, h - 2)
                    if has(-1, t):
                        b = t - 1
                        if h == L_LAST:
                            after(pe, cx_ready, b, NS - 1)
                            if has(1, t):
                                after(pe, mf_ready, b + 1)
                            turn(b, NS - 1)
                        if h == L_CTT:
                            if diff:
                                after(pe, cxn_ready, b)
                                if has(0, t):
                                    after(pe, cx_ready, t, 1)
                            else:
                                after(pe, cx_ready, b)
                            for n in range(2):
                                for r in range(R2):
                                    src = CX[:, (m - 1) % 3, n, :, :].rearrange("p h d -> p (h d)")[:, r * P:(r + 1) * P]
                                    mm = pe.transpose(bank[7][:, r * T + n * P:r * T + (n + 1) * P], src, c.ID)
                            mm.then_inc(ctt_ready.sem, 1)
                        if h == L_OUT:
                            after(pe, ctt_copied, b)
                            for r in range(R2):
                                mm = pe.matmul(bank[7][:, 0:T], WO[:, r, :], CTT[:, r, :], start=(r == 0), stop=(r == R2 - 1))
                            mm.then_inc(o_ready.sem, 1)
                    if has(1, t):
                        if h == L_MT:
                            b = t + 1
                            if causal:
                                after(pe, nmq_ready, b)
                            else:
                                after(pe, s_used, b)
                            if has(0, t):
                                after(pe, cx_ready, t, S_MT + 1)
                            for n in range(2):
                                mm = pe.transpose(bank[7][0:NH, n * P:(n + 1) * P], NMQ[:, n, :], c.ID)
                            mm.then_inc(mt_ready.sem, 1)
                    if has(0, t):
                        if h in turn_at:
                            s = turn_at[h]
                            if s == out_at:
                                after(pe, tmp_ready, t - 1)
                            elif s == 0:
                                after(pe, cx_ready, t - 1)
                            else:
                                after(pe, cx_ready, t, s)
                                if s == S_MT + 1 and has(1, t):
                                    after(pe, mf_ready, t + 1)
                            turn(t, s)
                if has(0, t):
                    values(t, m, NH - 2)
                    values(t, m, NH - 1)
            steps(pe, step)

        @block.vector
        def _(v):
            zero_q = lambda j: v.memset(QH[:, j, :, :].rearrange("p h t -> p (h t)").bitcast(F32), 0.0).then_inc(q_zeroed, 1)
            zero_q(0)
            v.wait_ge(w_in, NW)
            if cfg.get("gate"):
                v.wait_ge(sg_ready, 1)
                v.tensor_scalar(SGM[:, :], HM[:, :], SG[:, 0:1], None, ALU.mult).then_inc(sgm_ready, 1)
                v.wait_ge(gate_mm, 1)
                v.tensor_copy(GATE[:, :], bank[6][:, 0:T]).then_inc(gate_ready, 1)
            if diff:
                v.tensor_tensor(LQ[:, 0:4:2, :, :], LQ[:, 0:4:2, :, :], LQ[:, 1:4:2, :, :], ALU.mult).then_inc(ls_ready, 1)
                v.wait_ge(ls_ready, 1)
                v.tensor_reduce(LS[:, :, :], LQ[:, 0:4:2, :, :], AX, ALU.add).then_inc(ls_ready, 1)
                v.wait_ge(le_ready, 1)
                v.scalar_tensor_tensor(NLAM[:, :], LE[:, 1, :], -0.8, LE[:, 0, :], ALU.add, ALU.subtract).then_inc(lam_ready, 1)
                v.tensor_scalar(COL[:, 2:3], COL[:, 2:3], 1.0 - 0.8, None, ALU.mult).then_inc(lam_ready, 1)
                v.wait_ge(lam_ready, 2)

            def turned(b, j, s):
                after(v, t_ready, b, s + 1)
                o = bank[7][:, 0:T].rearrange("p (n g x) -> p n g x", n=2, g=4)
                after(v, cx_ready, b, s)
                v.reciprocal(RC[:, :, :], o[:, :, :, VW:OW].rearrange("p n g x -> p n (g x)")).then_inc(rc_ready.sem, 1)
                after(v, rc_ready, b, s + 1)
                if s == 0:
                    after(v, ctt_ready, b - 3)
                scale = RC[:, :, :].unsqueeze(3).to_broadcast([P, 2, 4, VW])
                if not diff:
                    v.tensor_tensor(CX[:, j, :, 4 * s:4 * s + 4, :], o[:, :, :, 0:VW], scale, ALU.mult).then_inc(cx_ready.sem, 1)
                    return
                lam = NLAM[:, 2 * s:2 * s + 2].unsqueeze(1).to_broadcast([P, 2, 2])
                v.tensor_tensor(RC[:, :, 1:4:2], RC[:, :, 1:4:2], lam, ALU.mult).then_inc(dif_ready.sem, 1)
                after(v, dif_ready, b, 2 * s + 1)
                v.tensor_tensor(CX2[:, :, :, :], o[:, :, :, 0:VW], scale, ALU.mult).then_inc(cx_ready.sem, 1)
                after(v, cx_ready, b, s + 1)
                v.tensor_tensor(CX[:, j, :, 2 * s:2 * s + 2, :], CX2[:, :, 0:4:2, :], CX2[:, :, 1:4:2, :], ALU.add).then_inc(dif_ready.sem, 1)

            def maxima(b, h):
                after(v, s_ready, b, h + 1)
                if h == 0:
                    after(v, mt_ready, b - 1)
                if causal:
                    v.tensor_reduce(NM3[:, h, :], bank[h % 2][:, 0:NC].rearrange("p (n k) -> p n k", n=3), AX, ALU.max,
                                    negate=True).then_inc(s_used.sem, 1)
                else:
                    v.tensor_reduce(NMQ[:, :, h], bank[h % 2][:, 0:NC].rearrange("p (n k) -> p n k", n=2), AX, ALU.max,
                                    negate=True).then_inc(s_used.sem, 1)

            def step(t, m):
                for h in range(NH):
                    if has(2, t):
                        b = t + 2
                        if h == L_MEAN and centered:
                            after(v, mean_ready, b)
                            after(v, xn_ready, b - 1)
                            v.tensor_tensor(XC[:, :], SRC[:, tok(b)], bank[6][:, 0:T], ALU.subtract).then_inc(xc_ready.sem, 1)
                        if h == L_VAR:
                            after(v, var_ready, b)
                            after(v, rs_ready, b - 1)
                            v.tensor_scalar(VE[:, :], bank[6][:, T:T + 2], eps, None, ALU.add).then_inc(ve_ready.sem, 1)
                        if h == L_DG:
                            after(v, rs_ready, b)
                            after(v, bc_ready, b - 1)
                            v.tensor_scalar(DG[:, 0, :], c.ID, RS[:, 0:1], None, ALU.mult)
                            v.tensor_scalar(DG[:, 1, :], c.ID, RS[:, 1:2], None, ALU.mult).then_inc(dg_ready.sem, 1)
                        if h == L_XN:
                            after(v, bc_ready, b)
                            after(v, h_ready, b - 1)
                            v.tensor_tensor(XN[:, :], XC[:, :] if centered else SRC[:, tok(b)], bank[6][:, T:2 * T],
                                            ALU.mult).then_inc(xn_ready.sem, 1)
                        for n in range(QK):
                            if h == L_QK + 2 * n * U + 1:
                                if isinstance(t, int) and t == -2 and n == 0:
                                    v.wait_ge(zeroed, 2)
                                after(v, qk_ready, b, n + 1)
                                if rope:
                                    if n == 0:
                                        after(v, lo_ready, b - 1)
                                    else:
                                        after(v, half_ready, b)
                                    v.tensor_tensor(RES[:, 0, :], bank[6][:, 0:T], c.CST[:, C_COS:C_COS + T], ALU.mult)
                                    v.tensor_tensor(RES[:, 1, :], bank[6][:, T:2 * T], c.CST[:, C_SIN:C_SIN + T], ALU.mult)\
                                        .then_inc(qk_copied.sem, 1)
                                    continue
                                after(v, res_ready, b, n)
                                if cfg.get("gate"):
                                    v.tensor_tensor(QKF[:, 0, :], bank[6][:, 0:T], GATE[:, :], ALU.mult)
                                elif cfg.get("bq"):
                                    v.tensor_scalar(QKF[:, 0, :], bank[6][:, 0:T], COL[:, 0:1], None, ALU.add)
                                else:
                                    v.tensor_copy(QKF[:, 0, :], bank[6][:, 0:T])
                                v.tensor_copy(QKF[0:KR, 1, :], bank[6][0:KR, T:2 * T]).then_inc(qk_copied.sem, 1)
                        if h == L_V + 1 and cfg.get("bv"):
                            after(v, v_ready, b)
                            if isinstance(t, int) and t == -2:
                                v.wait_ge(vx_ones, 1)
                            after(v, pv_done, b - 3)
                            vx = VX[:, (m + 2) % 3, :, :, 0:VW]
                            src = bank[6][:, 0:2 * HV * VW].rearrange("p (n h d) -> p n h d", n=2, h=HV)
                            bv = BV[:, :].rearrange("p (h d) -> p h d", h=HV).unsqueeze(1).to_broadcast([P, 2, HV, VW])
                            v.tensor_tensor(vx, src, bv, ALU.add).then_inc(v_copied.sem, 1)
                    if has(1, t):
                        b = t + 1
                        for n in heads_at(h):
                            maxima(b, n)
                        if h == L_NMQ and causal:
                            after(v, s_used, b)
                            v.tensor_copy(NMQ[:, 0, :], NM3[:, :, 0]).then_inc(nmq_ready.sem, 1)
                            v.tensor_tensor(NMQ[:, 1, :], NM3[:, :, 1], NM3[:, :, 2], ALU.min).then_inc(nmq_ready.sem, 1)
                    if has(-1, t):
                        b = t - 1
                        if h == L_LAST:
                            turned(b, (m - 1) % 3, NS - 1)
                        if diff and h == L_COMBINE:
                            after(v, csq_ready, b)
                            after(v, cr_ready, b - 1)
                            v.tensor_reduce(CM[:, :, :], CSQ[:, :, :, :], AX, ALU.add).then_inc(cm_ready.sem, 1)
                            after(v, cm_ready, b, 1)
                            v.tensor_scalar(CM[:, :, :], CM[:, :, :], 1.0 / VW, 1e-5, ALU.mult, ALU.add).then_inc(cm_ready.sem, 1)
                        if diff and h == L_CTT - 1:
                            after(v, cr_ready, b)
                            cx = CX[:, (m - 1) % 3, :, :, :]
                            v.tensor_tensor(cx, cx, CR[:, :, :].unsqueeze(3).to_broadcast([P, 2, 16, VW]),
                                            ALU.mult).then_inc(cxn_ready.sem, 1)
                        if h == L_TMP:
                            after(v, o_ready, b)
                            after(v, x_updated, b - 1)
                            if cfg.get("plain"):
                                v.tensor_copy(TMP[:, :], bank[7][:, 0:T]).then_inc(tmp_ready.sem, 1)
                            else:
                                v.tensor_scalar(TMP[:, :], bank[7][:, 0:T], COL[:, 1:2], c.MOD[:, l, 2, one(b)],
                                                ALU.add, ALU.mult).then_inc(tmp_ready.sem, 1)
                            after(v, tmp_ready, b)
                            v.tensor_tensor(DST[:, tok(b)], DST[:, tok(b)], TMP[:, :], ALU.add).then_inc(x_updated.sem, 1)
                    if has(0, t) and h - 1 in turn_at:
                        turned(t, m, turn_at[h - 1])
                if has(0, t) and NH - 1 in turn_at:
                    turned(t, m, turn_at[NH - 1])
                if isinstance(t, int) and t < 0:
                    zero_q(t + 3)
            steps(v, step)
    close(c, S)


def tok(b, n=T):
    return slice(b * n, (b + 1) * n) if isinstance(b, int) else bass.ds(b * n, n)


def one(b):
    return slice(b, b + 1) if isinstance(b, int) else bass.ds(b, 1)


def norm_phase(c, cfg, NT, LG=None, prefetch=()):
    nc, bank, SRC, centered = c.nc, c.bank, cfg["nsrc"], cfg["ncentered"]
    E = cfg.get("E", 0) if LG is not None else 0
    with ExitStack() as ctx:
        sb = lambda name, shape, dt=F32: c.sb(cfg["name"] + "n" + name, shape, dt, ctx)
        XC, SQ, XN = sb("XC", [P, 4, T]), sb("SQ", [P, 2, T]), sb("XN", [P, T])
        H = sb("H", [P, 4, T])
        VE, RS, DG = sb("VE", [P, 2, 2]), sb("RS", [P, 2, 2]), sb("DG", [P, 2, 2, P])
        COL, WR = sb("COL", [P, 2]), sb("WR", [P, max(E, 1)])
        S = signals(c, n_mean=int(centered), n_xc=int(centered), n_sq=1, n_var=1, n_ve=1, n_rs=1, n_dg=1, n_bc=1, n_xn=1,
                    n_h=1, n_copied=1, n_logits=int(E > 0), n_lg=int(E > 0))
        mean, xc, sq, var, ve, rs, dg, bc, xn, hr, copied, logits, lg = S
        w_in = c.sem(cfg["name"] + "n_w_in")
        loads = ([(COL[:, 0:1], cfg["ngain"])] if cfg.get("ngain") else []) \
            + ([(COL[:, 1:2], cfg["nshift"])] if cfg.get("nshift") else []) + ([(WR[:, :], cfg["wr"])] if E else [])
        has = lambda stage, t: not isinstance(t, int) or 0 <= t + stage < NB

        def steps(eng, step):
            for t in range(8):
                step(t, t % 4)
            with eng.Fori(0, 2) as i:
                for k in range(8, 12):
                    step(i * 4 + k, k % 4)
            for t in range(16, NB + 4):
                step(t, t % 4)

        block = ctx.enter_context(nc.Block())

        @block.sync
        def _(sp):
            for dst, src in loads:
                sp.dma_start(dst, c.ins[src]).then_inc(w_in, 16)
            for dst, src, sem in prefetch:
                sp.dma_start(dst, c.ins[src]).then_inc(sem, 16)

        @block.tensor
        def _(pe):
            if loads:
                pe.wait_ge(w_in, 16 * len(loads))

            def step(t, m):
                if has(0, t) and centered:
                    after(pe, xc, t - 2)
                    pe.matmul(bank[m % 2][:, 0:T], c.MEAN, SRC[:, tok(t)], start=True, stop=True).then_inc(mean.sem, 1)
                if has(-3, t):
                    b, d = t - 3, (m - 3) % 2
                    after(pe, dg, b)
                    after(pe, xn, b - 2)
                    for n in range(2):
                        mm = pe.matmul(bank[4 + d][:, n * P:(n + 1) * P], c.ONES[:, :], DG[:, d, n, :], start=True, stop=True)
                    mm.then_inc(bc.sem, 1)
                if has(-1, t):
                    d = (m - 1) % 2
                    after(pe, sq, t - 1)
                    after(pe, ve, t - 3)
                    for n in range(2):
                        mm = pe.matmul(bank[2 + d][:, n:n + 1], SQ[:, d, n * P:(n + 1) * P], c.MEAN[:, 0:1], start=True, stop=True)
                    mm.then_inc(var.sem, 1)
                if E and has(-4, t):
                    b, d = t - 4, m % 2
                    after(pe, hr, b)
                    after(pe, lg, b - 2)
                    for n in range(2):
                        mm = pe.matmul(bank[6 + d][:, n * E:(n + 1) * E], H[:, m % 4, n * P:(n + 1) * P], WR[:, :],
                                       start=True, stop=True)
                    mm.then_inc(logits.sem, 1)
            steps(pe, step)

        @block.gpsimd
        def _(pool):
            def step(t, m):
                if has(-1, t):
                    d = (m - 1) % 2
                    after(pool, ve, t - 1)
                    after(pool, dg, t - 3)
                    nc.gpsimd.tensor_tensor(RS[:, d, :], VE[:, d, :], c.HALF[:, 0:2], ALU.pow).then_inc(rs.sem, 1)
            steps(pool, step)

        @block.scalar
        def _(act):
            def step(t, m):
                if has(0, t):
                    if centered:
                        after(act, xc, t)
                    after(act, var, t - 2)
                    nc.scalar.activation(SQ[:, m % 2, :], XC[:, m, :] if centered else SRC[:, tok(t)], ACT.Square).then_inc(sq.sem, 1)
                if has(-4, t):
                    after(act, hr, t - 4)
                    nc.scalar.copy(NT[:, tok(t - 4)], H[:, m % 4, :]).then_inc(copied.sem, 1)
            steps(act, step)

        @block.vector
        def _(v):
            if loads:
                v.wait_ge(w_in, 16 * len(loads))

            def step(t, m):
                if has(-2, t):
                    b, d = t - 2, m % 2
                    after(v, rs, b)
                    after(v, bc, b - 2)
                    v.tensor_scalar(DG[:, d, 0, :], c.ID, RS[:, d, 0:1], None, ALU.mult)
                    v.tensor_scalar(DG[:, d, 1, :], c.ID, RS[:, d, 1:2], None, ALU.mult).then_inc(dg.sem, 1)
                if has(0, t) and centered:
                    after(v, mean, t)
                    after(v, xn, t - 4)
                    v.tensor_tensor(XC[:, m, :], SRC[:, tok(t)], bank[m % 2][:, 0:T], ALU.subtract).then_inc(xc.sem, 1)
                if has(-1, t):
                    b, d = t - 1, (m - 1) % 2
                    after(v, var, b)
                    after(v, rs, b - 2)
                    v.tensor_scalar(VE[:, d, :], bank[2 + d][:, 0:2], cfg["neps"], None, ALU.add).then_inc(ve.sem, 1)
                if has(-3, t):
                    b, j, d = t - 3, (m - 3) % 4, (m - 3) % 2
                    after(v, bc, b)
                    after(v, hr, b - 1)
                    v.tensor_tensor(XN[:, :], XC[:, j, :] if centered else SRC[:, tok(b)], bank[4 + d][:, 0:T],
                                    ALU.mult).then_inc(xn.sem, 1)
                if has(-3, t):
                    b, j = t - 3, (m - 3) % 4
                    after(v, xn, b)
                    after(v, copied, b - 4)
                    if E:
                        after(v, logits, b - 4)
                    if cfg.get("ngain"):
                        scale, shift = COL[:, 0:1], (COL[:, 1:2] if cfg.get("nshift") else 0.0)
                    else:
                        l, k = cfg["layer"], cfg["nmod"]
                        scale, shift = c.MOD[:, l, k + 1, one(b)], c.MOD[:, l, k, one(b)]
                    v.tensor_scalar(H[:, j, :], XN[:, :], scale, shift, ALU.mult, ALU.add).then_inc(hr.sem, 1)
                if E and has(-4, t):
                    b = t - 4
                    after(v, logits, b)
                    v.tensor_copy(LG[:, bass.ds(b * 2, 2) if not isinstance(b, int) else slice(2 * b, 2 * b + 2), 0:E],
                                  bank[6 + m % 2][:, 0:2 * E].rearrange("p (n e) -> p n e", n=2)).then_inc(lg.sem, 1)
            steps(v, step)
    close(c, S)


NT_TILES = NTOK // P


def combine_phase(c, cfg, LG, CB3, CBF):
    nc, bank, E, name = c.nc, c.bank, cfg["E"], cfg["name"]
    N = NT_TILES
    G = 8
    with ExitStack() as ctx:
        sb = lambda nm, shape, dt=F32: c.sb(name + "c" + nm, shape, dt, ctx)
        PB, W = sb("PB", [P, N, E]), sb("W", [P, N, E])
        R1, R2, R3, R4 = (sb(f"R{k}", [P, N]) for k in range(4))
        GG = G if E == 64 else E
        KEY = sb("KEY", [P, N, GG])
        RK, SELG, CMP = sb("RK", [P, N, GG]), sb("SELG", [P, N, GG]), sb("CMP", [P, N, GG, GG])
        EP = min(E, 32)
        NK = E // EP * (N // 4)
        piece = lambda k: (k // (N // 4), tok(k % (N // 4), 512))
        TM, TR = sb("TM", [P, 2, 512], BF16), sb("TR", [P, 2, 512])
        if E == 64:
            SFC, BIAS, M8 = sb("SFC", [P, N, E]), sb("BIAS", [P, E]), sb("M8", [P, N, 8])
            T1, SEL = sb("T1", [P, N, E]), sb("SEL", [P, N, E])
            M1, M2, CNT, GB = (sb(nm, [P, N, 8]) for nm in ("M1", "M2", "CNT", "GB"))
            RUN = sb("RUN", [P, N, E])
        r_in, r_act, r_step, r_run, r_pos, r_val, r_t, r_hi, r_res, r_mid, r_lo, r_z, r_tm = (
            c.sem("r_" + nm) for nm in ("in", "act", "step", "run", "pos", "val", "t", "hi", "res", "mid", "lo", "z", "tm"))
        base = c.counts
        b0 = dict(base)
        block = ctx.enter_context(nc.Block())
        bc3 = lambda a, n: a.unsqueeze(2).to_broadcast([P, N, n])
        loads = [(BIAS[:, :], "rbias")] if E == 64 else []

        @block.sync
        def _(sp):
            for dst, src in loads:
                sp.dma_start(dst, c.ins[src]).then_inc(r_in, 16)

        @block.gpsimd
        def _(pool):
            nc.gpsimd.memset(CB3[:, :, :], 0.0).then_inc(r_z, 1)

        @block.scalar
        def _(act):
            if E == 64:
                nc.scalar.activation(PB[:, :, :], LG[:, :, :], ACT.Sigmoid).then_inc(r_act, 1)
            else:
                act.wait_ge(r_step, b0["step"] + 2)
                nc.scalar.activation(PB[:, :, :], PB[:, :, :], ACT.Exp).then_inc(r_act, 1)
            for k in range(NK + 1):
                if k < NK:
                    pl, t = piece(k)
                    act.wait_ge(r_t, b0["t"] + k + 1)
                    if k == 0:
                        act.wait_ge(r_z, b0["z"] + 1)
                    o = bank[4 + k % 4][0:EP, :]
                    if CBF is not None:
                        nc.scalar.copy(CBF[0:E, t], o)
                    nc.scalar.copy(CB3[0:EP, pl, t], o).then_inc(r_hi, 1)
                if k >= 1:
                    pl, t = piece(k - 1)
                    act.wait_ge(r_res, b0["res"] + k)
                    if k >= 3:
                        act.wait_ge(r_lo, b0["lo"] + k - 2)
                    nc.scalar.copy(TM[0:EP, k % 2, :], TR[0:EP, k % 2, :]).then_inc(r_tm, 1)
                    act.wait_ge(r_tm, b0["tm"] + k)
                    nc.scalar.copy(CB3[32:32 + EP, pl, t], TM[0:EP, k % 2, :]).then_inc(r_mid, 1)

        @block.tensor
        def _(pe):
            if E == 64:
                for n in range(N):
                    pe.wait_ge(r_run, b0["run"] + max(n, 1))
                    o = bank[n // 8][:, (n % 8) * E:(n % 8 + 1) * E]
                    mm = pe.matmul(o, c.CST[:, C_TRI:C_TRI + P], SEL[:, n, :], start=True, stop=(n == 0))
                    if n:
                        mm = pe.matmul(o, c.ONES[:, :], RUN[:, n, :], start=False, stop=True)
                    mm.then_inc(r_pos, 1)
            pe.wait_ge(r_val, b0["val"] + 1)
            for k in range(NK):
                if k >= 4:
                    pe.wait_ge(r_hi, b0["hi"] + k - 3)
                    pe.wait_ge(r_res, b0["res"] + k - 3)
                pl, g = k // (N // 4), k % (N // 4)
                for n in range(4):
                    mm = pe.transpose(bank[4 + k % 4][0:EP, n * P:(n + 1) * P], W[:, 4 * g + n, pl * EP:(pl + 1) * EP], c.ID)
                mm.then_inc(r_t, 1)

        @block.vector
        def _(v):
            count = [b0["step"]]

            def then(ins):
                count[0] += 1
                ins.then_inc(r_step, 1)
                v.wait_ge(r_step, count[0])

            def ranks(key, top, n=GG):
                for a in range(n):
                    if a:
                        v.tensor_tensor(CMP[:, :, a, 0:a], key[:, :, 0:a], key[:, :, a:a + 1].to_broadcast([P, N, a]), ALU.is_ge)
                    last = v.tensor_tensor(CMP[:, :, a, a:n], key[:, :, a:n], key[:, :, a:a + 1].to_broadcast([P, N, n - a]), ALU.is_gt)
                then(last)
                then(v.tensor_reduce(RK[:, :, :], CMP[:, :, :, :], AX, ALU.add))
                then(v.tensor_scalar(SELG[:, :, :], RK[:, :, :], top - 0.5, None, ALU.is_lt))

            if loads:
                v.wait_ge(r_in, b0["in"] + 16 * len(loads))
            if E == 64:
                v.wait_ge(r_act, b0["act"] + 1)
                g4 = lambda a: a.rearrange("p n (g k) -> p (n g) k", g=8)
                gb = lambda a: a.rearrange("p n g -> p (n g)").unsqueeze(2).to_broadcast([P, N * 8, 8])
                sfc = g4(SFC[:, :, :])
                then(v.tensor_tensor(SFC[:, :, :], PB[:, :, :], BIAS[:, :].unsqueeze(1).to_broadcast([P, N, E]), ALU.add))
                then(v.tensor_reduce(M1[:, :, :].rearrange("p n g -> p (n g)"), sfc, AX, ALU.max))
                then(v.tensor_tensor(g4(T1[:, :, :]), sfc, gb(M1[:, :, :]), ALU.is_equal))
                then(v.tensor_reduce(CNT[:, :, :].rearrange("p n g -> p (n g)"), g4(T1[:, :, :]), AX, ALU.add))
                then(v.scalar_tensor_tensor(T1[:, :, :], T1[:, :, :], NEG, SFC[:, :, :], ALU.mult, ALU.add))
                then(v.tensor_reduce(M2[:, :, :].rearrange("p n g -> p (n g)"), g4(T1[:, :, :]), AX, ALU.max))
                then(v.tensor_scalar(CNT[:, :, :], CNT[:, :, :], 1.5, None, ALU.is_gt))
                then(v.tensor_scalar(GB[:, :, :], CNT[:, :, :], -1.0, 1.0, ALU.mult, ALU.add))
                then(v.tensor_tensor(CNT[:, :, :], CNT[:, :, :], M1[:, :, :], ALU.mult))
                then(v.tensor_tensor(M2[:, :, :], M2[:, :, :], GB[:, :, :], ALU.mult))
                then(v.tensor_tensor(M2[:, :, :], M2[:, :, :], CNT[:, :, :], ALU.add))
                then(v.tensor_tensor(KEY[:, :, :], M1[:, :, :], M2[:, :, :], ALU.add))
                ranks(KEY[:, :, :], 4)
                then(v.tensor_scalar(GB[:, :, :], SELG[:, :, :], -NEG, NEG, ALU.mult, ALU.add))
                then(v.tensor_tensor(g4(T1[:, :, :]), sfc, gb(GB[:, :, :]), ALU.add))
                for n in range(N):
                    last = v.max(M8[:, n, :], T1[:, n, :])
                then(last)
                for n in range(N):
                    last = v.match_replace(SFC[:, n, :], M8[:, n, :], T1[:, n, :], 3.0 * NEG)
                then(last)
                then(v.tensor_tensor(SEL[:, :, :], SFC[:, :, :], T1[:, :, :], ALU.not_equal))
                v.tensor_copy(RUN[:, 1, :], SEL[:, 0, :]).then_inc(r_run, 1)
                for n in range(2, N):
                    v.wait_ge(r_run, b0["run"] + n - 1)
                    v.tensor_tensor(RUN[:, n, :], RUN[:, n - 1, :], SEL[:, n - 1, :], ALU.add).then_inc(r_run, 1)
                then(v.tensor_tensor(W[:, :, :], PB[:, :, :], SEL[:, :, :], ALU.mult))
                then(v.tensor_reduce(R1[:, :], W[:, :, :], AX, ALU.add))
                then(v.tensor_scalar(R1[:, :], R1[:, :], 1e-20, None, ALU.add))
                then(v.reciprocal(R2[:, :], R1[:, :]))
                then(v.tensor_scalar(R2[:, :], R2[:, :], 2.5, None, ALU.mult))
                then(v.tensor_tensor(W[:, :, :], W[:, :, :], bc3(R2[:, :], E), ALU.mult))
                v.wait_ge(r_pos, b0["pos"] + N)
                for q in range(4):
                    w = W[:, 8 * q:8 * q + 8, :].rearrange("p n e -> p (n e)")
                    last = v.scalar_tensor_tensor(w, bank[q][:, :], cfg["CAP"] - 0.5, w, ALU.is_lt, ALU.mult)
                last.then_inc(r_val, 1)
            else:
                then(v.tensor_reduce(R1[:, :], LG[:, :, 0:E], AX, ALU.max))
                then(v.tensor_tensor(PB[:, :, :], LG[:, :, 0:E], bc3(R1[:, :], E), ALU.subtract))
                v.wait_ge(r_act, b0["act"] + 1)
                then(v.tensor_reduce(R1[:, :], PB[:, :, :], AX, ALU.add))
                then(v.reciprocal(R2[:, :], R1[:, :]))
                then(v.tensor_tensor(KEY[:, :, :], PB[:, :, :], bc3(R2[:, :], E), ALU.mult))
                ranks(KEY[:, :, :], 2)
                if cfg["renorm"]:
                    then(v.tensor_tensor(PB[:, :, :], KEY[:, :, :], SELG[:, :, :], ALU.mult))
                    then(v.tensor_reduce(R3[:, :], PB[:, :, :], AX, ALU.add))
                    then(v.reciprocal(R4[:, :], R3[:, :]))
                    v.tensor_tensor(W[:, :, :], PB[:, :, :], bc3(R4[:, :], E), ALU.mult).then_inc(r_val, 1)
                else:
                    v.tensor_tensor(W[:, :, :], KEY[:, :, :], SELG[:, :, :], ALU.mult).then_inc(r_val, 1)
            c.counts["step"] = count[0]
            v.wait_ge(r_z, b0["z"] + 1)
            for k in range(NK + 1):
                if k < NK:
                    pl, t = piece(k)
                    v.wait_ge(r_hi, b0["hi"] + k + 1)
                    if k >= 2:
                        v.wait_ge(r_lo, b0["lo"] + k - 1)
                    v.tensor_tensor(TR[0:EP, (k + 1) % 2, :], bank[4 + k % 4][0:EP, :], CB3[0:EP, pl, t], ALU.subtract)\
                        .then_inc(r_res, 1)
                if k >= 1:
                    pl, t = piece(k - 1)
                    v.wait_ge(r_tm, b0["tm"] + k)
                    v.tensor_tensor(CB3[64:64 + EP, pl, t], TR[0:EP, k % 2, :], TM[0:EP, k % 2, :], ALU.subtract).then_inc(r_lo, 1)
            v.wait_ge(r_lo, b0["lo"] + NK)
        for key, k in (("in", 16 * len(loads)), ("act", 1), ("run", N - 1 if E == 64 else 0), ("pos", N if E == 64 else 0),
                       ("val", 1), ("t", NK), ("hi", NK), ("res", NK), ("mid", NK), ("lo", NK), ("z", 1), ("tm", NK)):
            c.counts[key] += k


def experts_phase(c, cfg, NT, W1, W3, W2, CB3, CBF, w_in, nw):
    nc, bank, name = c.nc, c.bank, cfg["name"]
    NCH, sel, glu, fn = cfg["NCH"], cfg["sel"], cfg["glu"], cfg["fn"]
    F = 512
    NI = NTOK // F
    new = [s is not None and (m == 0 or sel[m - 1] != s) for m, s in enumerate(sel)]
    NBC = sum(new)
    kth = [sum(new[:m + 1]) - 1 for m in range(NCH)]
    gated = [s is not None for s in sel]
    NGT = sum(gated)
    gi = [sum(gated[:m]) for m in range(NCH)]
    last_use = [max([m for m in range(NCH) if gated[m] and kth[m] == k]) for k in range(NBC)]
    NPL = max(cfg.get("E", 0) // 32, 1)
    l = cfg["layer"]
    with ExitStack() as ctx:
        sb = lambda nm, shape, dt=F32: c.sb(name + "e" + nm, shape, dt, ctx)
        SG, HS, T1 = sb("SG", [P, 2, F]), sb("HS", [P, 4, F]), sb("T1", [P, F])
        SELB = sb("SELB", [P, max(NBC, 1), P], BF16)
        COL, FB, BPJ, TMP = sb("COL", [P, 1]), sb("FB", [P, NCH]), sb("BPJ", [8, P]), sb("TMP", [P, T])
        small = [(COL[:, :], cfg.get("ybias") or "zero")]
        if cfg.get("hbias"):
            small.append((FB[:, :], cfg["hbias"]))
        if cfg.get("ebias"):
            small.append((BPJ[:, :], cfg["ebias"]))
        s_in, sel_in = c.sem(name + "e_s_in"), c.sem(name + "e_sel_in")
        S = signals(c, e_g=NCH, e_u=NCH * int(glu), e_act=NCH, e_bc=NBC, e_t1=NCH * int(glu), e_hs=NGT, e_dn=NCH,
                    e_y=int(CBF is not None), e_tmp=2 * int(bool(cfg.get("ybias") or cfg.get("plus"))), e_used=2)
        g_ready, u_ready, act_done, bc_ready, t1_ready, hs_ready, dn_done, y_ready, y_tmp, y_used = S

        def slot_used(eng, i, m):
            if m >= 4:
                after(eng, dn_done, i, m - 3)
            else:
                after(eng, dn_done, i - 1, max(n for n in range(NCH) if n % 4 == m) + 1)

        def steps(eng, step):
            for i in range(2):
                step(i, i)
            with eng.Fori(0, (NI - 2) // 2) as k:
                for j in range(2):
                    step(k * 2 + (2 + j), j)

        block = ctx.enter_context(nc.Block())

        @block.sync
        def _(sp):
            for dst, src in small:
                sp.dma_start(dst, c.ins[src]).then_inc(s_in, 16)

        @block.gpsimd
        def _(pool):
            if NBC:
                nc.gpsimd.dma_start(SELB[:, :, :].rearrange("p k x -> p (k x)"), c.ins[cfg["selector"]]).then_inc(sel_in, 16)

        @block.tensor
        def _(pe):
            pe.wait_ge(w_in, 16 * nw)
            pe.wait_ge(s_in, 16 * len(small))
            if NBC:
                pe.wait_ge(sel_in, 16)

            def up(i, j, m):
                q = (j * NCH + m) % 2
                x = NT[:, tok(i, F)]
                after(pe, act_done, i, m - 1)
                pe.matmul(bank[q][:, :], W1[:, m * P:(m + 1) * P], x, start=True, stop=True).then_inc(g_ready.sem, 1)
                if glu:
                    after(pe, t1_ready, i, m - 1)
                    pe.matmul(bank[2 + q][:, :], W3[:, m * P:(m + 1) * P], x, start=True, stop=True).then_inc(u_ready.sem, 1)
                if new[m]:
                    k = kth[m]
                    kb = (j * NBC + k) % 2
                    if k >= 2:
                        after(pe, hs_ready, i, gi[last_use[k - 2]] + 1)
                    else:
                        after(pe, hs_ready, i - 1, gi[last_use[(k - 2) % NBC]] + 1)
                    pe.matmul(bank[4 + kb][:, :], SELB[:, k, :], CB3[:, k * NPL // NBC, tok(i, F)], start=True, stop=True)\
                        .then_inc(bc_ready.sem, 1)

            def down(i, j, m):
                if gated[m]:
                    after(pe, hs_ready, i, gi[m] + 1)
                else:
                    after(pe, act_done, i, m + 1)
                if m == 0:
                    after(pe, y_used, i - 2)
                mm = pe.matmul(bank[6 + j][:, :], W2[:, m, :], HS[:, m % 4, :], start=(m == 0), stop=(m == NCH - 1 and CBF is None))
                mm.then_inc(dn_done.sem, 1)
                if m == NCH - 1 and CBF is not None:
                    pe.matmul(bank[6 + j][:, :], BPJ[:, :], CBF[:, tok(i, F)], start=False, stop=True).then_inc(y_ready.sem, 1)

            def step(i, j):
                for m in range(NCH):
                    up(i, j, m)
                    if m >= 2:
                        down(i, j, m - 2)
                    elif not isinstance(i, int) or i > 0:
                        down(i - 1, 1 - j, NCH - 2 + m)
            steps(pe, step)
            for m in (NCH - 2, NCH - 1):
                down(NI - 1, 1, m)

        @block.scalar
        def _(act):
            act.wait_ge(s_in, 16 * len(small))

            def step(i, j):
                for m in range(NCH):
                    q = (j * NCH + m) % 2
                    after(act, g_ready, i, m + 1)
                    if glu:
                        after(act, t1_ready, i, m - 1)
                    elif gated[m]:
                        after(act, hs_ready, i - 1 if m == 0 else i, gi[(m - 1) % NCH])
                    if not gated[m]:
                        slot_used(act, i, m)
                    dst = HS[:, m % 4, :] if not gated[m] else SG[:, q, :]
                    nc.scalar.activation(dst, bank[q][:, :], fn, bias=FB[:, m:m + 1] if cfg.get("hbias") else 0.0)\
                        .then_inc(act_done.sem, 1)
            steps(act, step)

        @block.vector
        def _(v):
            v.wait_ge(s_in, 16 * len(small))

            def finish(i, j):
                after(v, y_ready if CBF is not None else dn_done, i)
                for n in range(2):
                    b = i * 2 + n
                    y = bank[6 + j][:, n * T:(n + 1) * T]
                    g = c.MOD[:, l, cfg["gmod"], one(b)]
                    if cfg.get("ybias") or cfg.get("plus"):
                        after(v, y_used, i, n)
                        if cfg.get("plus"):
                            v.scalar_tensor_tensor(TMP[:, :], y, COL[:, 0:1], c.HT[:, tok(b)], ALU.add, ALU.add).then_inc(y_tmp.sem, 1)
                        else:
                            v.tensor_scalar(TMP[:, :], y, COL[:, 0:1], None, ALU.add).then_inc(y_tmp.sem, 1)
                        after(v, y_tmp, i, n + 1)
                        y = TMP[:, :]
                    v.scalar_tensor_tensor(c.XT[:, tok(b)], y, g, c.XT[:, tok(b)], ALU.mult, ALU.add).then_inc(y_used.sem, 1)

            def step(i, j):
                for m in range(NCH):
                    q = (j * NCH + m) % 2
                    if m == 2 and (not isinstance(i, int) or i > 0):
                        finish(i - 1, 1 - j)
                    if not gated[m]:
                        continue
                    after(v, act_done, i, m + 1)
                    a = SG[:, q, :]
                    if glu:
                        after(v, u_ready, i, m + 1)
                        after(v, hs_ready, i, gi[m])
                        v.tensor_tensor(T1[:, :], a, bank[2 + q][:, :], ALU.mult).then_inc(t1_ready.sem, 1)
                        after(v, t1_ready, i, m + 1)
                        a = T1[:, :]
                    after(v, bc_ready, i, kth[m] + 1)
                    slot_used(v, i, m)
                    v.tensor_tensor(HS[:, m % 4, :], a, bank[4 + (j * NBC + kth[m]) % 2][:, :], ALU.mult).then_inc(hs_ready.sem, 1)
            steps(v, step)
            finish(NI - 1, 1)
    close(c, S, NI)

def linear_attention_phase(c, NT):
    nc, bank = c.nc, c.bank
    N = NT_TILES
    with ExitStack() as ctx:
        sb = lambda nm, shape, dt=F32: c.sb("l" + nm, shape, dt, ctx)
        WQKV, BIAS, WO, BO = sb("WQKV", [P, 384]), sb("BIAS", [1, 384]), sb("WO", [P, P]), sb("BO", [P, 1])
        X, V, RL, EX, FQK = sb("X", [P, 2, P]), sb("V", [P, 2, P]), sb("RL", [P, 256]), sb("EX", [P, 256]), sb("F", [P, 2, 256])
        M1, M2 = sb("M1", [P, 2, 8, 8, 16]), sb("M2", [P, 16, 8, 8])
        KV, KS, NUM, DQ = sb("KV", [P, 8, 8]), sb("KS", [P, 8]), sb("NUM", [P, 16, 8]), sb("DQ", [P, 16, 8])
        DN, RD, AT, ATT = sb("DN", [P, 16]), sb("RD", [P, 16]), sb("AT", [P, 2, P]), sb("ATT", [P, P])
        w_in = c.sem("l_w_in")
        S = signals(c, l_x=1, l_p=1, l_v=1, l_rl=1, l_ex=1, l_f=1, l_m1=1, l_kv=1, l_ks=1, l_m2=1, l_num=1,
                    l_dq=1, l_dn=2, l_rd=1, l_at=1, l_t=1, l_att=1, l_o=1, l_y=1)
        xr, pr, vr, rl, ex, fr, m1, kv, ks, m2, num, dq, dn, rd, at, tr, att, orr, yr = S
        has = lambda stage, t: not isinstance(t, int) or 0 <= t + stage < N

        def steps(eng, step):
            for t in range(-2, 2):
                step(t, t % 2)
            with eng.Fori(0, (N - 4) // 2) as i:
                for k in range(2, 4):
                    step(i * 2 + k, k % 2)
            for t in range(N - 2, N + 1):
                step(t, t % 2)

        loads = [(WQKV[:, :], "wqkv3"), (BIAS[:, :], "bqkv3"), (WO[:, :], "wo3"), (BO[:, :], "bo3")]
        block = ctx.enter_context(nc.Block())

        @block.sync
        def _(sp):
            for dst, src in loads:
                sp.dma_start(dst, c.ins[src]).then_inc(w_in, 16)

        @block.scalar
        def _(act):
            def step(t, p):
                if has(1, t):
                    after(act, pr, t + 1)
                    after(act, fr, t)
                    qk = bank[1 - p][:, 0:256]
                    nc.scalar.activation(EX[:, :], qk, ACT.Exp).then_inc(ex.sem, 1)
                    nc.scalar.activation(RL[:, :], qk, ACT.Relu).then_inc(rl.sem, 1)
                    after(act, m1, t - 1)
                    nc.scalar.copy(V[:, 1 - p, :], bank[1 - p][:, 256:384]).then_inc(vr.sem, 1)
                if has(-1, t):
                    after(act, tr, t - 1)
                    after(act, orr, t - 2)
                    nc.scalar.copy(ATT[:, :], bank[2][:, 0:P]).then_inc(att.sem, 1)
                if has(2, t):
                    b, j = t + 2, p
                    after(act, pr, b - 2)
                    nc.scalar.copy(X[:, j, :], NT[:, tok(b, P)]).then_inc(xr.sem, 1)
            steps(act, step)

        @block.tensor
        def _(pe):
            pe.wait_ge(w_in, 16 * len(loads))

            def step(t, p):
                if has(-1, t):
                    b, j = t - 1, 1 - p
                    after(pe, at, b)
                    after(pe, att, b - 1)
                    pe.transpose(bank[2][:, 0:P], AT[:, j, :], c.ID).then_inc(tr.sem, 1)
                    after(pe, att, b)
                    after(pe, yr, b - 1)
                    pe.matmul(bank[3][:, 0:P], WO[:, :], ATT[:, :], start=True, stop=True).then_inc(orr.sem, 1)
                if has(2, t):
                    b, j = t + 2, p
                    after(pe, xr, b)
                    after(pe, vr, b - 2)
                    pe.matmul(bank[j][:, 0:384], c.ONES[0:1, :], BIAS[:, :], start=True, stop=False)
                    pe.matmul(bank[j][:, 0:384], X[:, j, :], WQKV[:, :], start=False, stop=True).then_inc(pr.sem, 1)
            steps(pe, step)

        @block.gpsimd
        def _(pool):
            def step(t, p):
                if has(1, t):
                    b, j = t + 1, 1 - p
                    fk = FQK[:, j, P:2 * P].rearrange("p (h d) -> p d h", d=8).unsqueeze(2).to_broadcast([P, 8, 8, 16])
                    vv = V[:, j, :].rearrange("p (h e) -> p e h", e=8).unsqueeze(1).to_broadcast([P, 8, 8, 16])
                    after(pool, vr, b)
                    after(pool, fr, b)
                    after(pool, kv, b - 2)
                    nc.gpsimd.tensor_tensor(M1[:, j, :, :, :], fk, vv, ALU.mult).then_inc(m1.sem, 1)
            steps(pool, step)

        @block.vector
        def _(v):
            v.wait_ge(w_in, 16 * len(loads))

            def step(t, p):
                if has(1, t):
                    b, j = t + 1, 1 - p
                    after(v, rl, b)
                    after(v, m1, b - 2)
                    after(v, m2, b - 2)
                    v.scalar_tensor_tensor(FQK[:, j, :], EX[:, :], 1.0, RL[:, :], ALU.min, ALU.add).then_inc(fr.sem, 1)
                if has(0, t):
                    after(v, m1, t)
                    after(v, m2, t - 1)
                    v.tensor_reduce(KV[:, :, :], M1[:, p, :, :, :], AX, ALU.add).then_inc(kv.sem, 1)
                    after(v, dq, t - 1)
                    v.tensor_reduce(KS[:, :], FQK[:, p, P:2 * P].rearrange("p (h d) -> p d h", d=8), AX, ALU.add).then_inc(ks.sem, 1)
                if has(0, t):
                    fq = FQK[:, p, 0:P].rearrange("p (h d) -> p h d", d=8).unsqueeze(2).to_broadcast([P, 16, 8, 8])
                    kve = KV[:, :, :].rearrange("p d e -> p e d").unsqueeze(1).to_broadcast([P, 16, 8, 8])
                    after(v, ks, t)
                    v.tensor_tensor(DQ[:, :, :], FQK[:, p, 0:P].rearrange("p (h d) -> p h d", d=8),
                                    KS[:, :].unsqueeze(1).to_broadcast([P, 16, 8]), ALU.mult).then_inc(dq.sem, 1)
                    after(v, kv, t)
                    after(v, num, t - 1)
                    v.tensor_tensor(M2[:, :, :, :], fq, kve, ALU.mult).then_inc(m2.sem, 1)
                    after(v, dq, t)
                    v.tensor_reduce(DN[:, :], DQ[:, :, :], AX, ALU.add).then_inc(dn.sem, 1)
                    after(v, m2, t)
                    v.tensor_reduce(NUM[:, :, :], M2[:, :, :, :], AX, ALU.add).then_inc(num.sem, 1)
                    after(v, dn, t, 1)
                    v.tensor_scalar(DN[:, :], DN[:, :], 1e-6, None, ALU.add).then_inc(dn.sem, 1)
                    after(v, dn, t)
                    v.reciprocal(RD[:, :], DN[:, :]).then_inc(rd.sem, 1)
                if has(-1, t):
                    b = t - 1
                    after(v, orr, b)
                    v.scalar_tensor_tensor(c.HT[:, tok(b, P)], bank[3][:, 0:P], BO[:, 0:1], c.HT[:, tok(b, P)], ALU.add, ALU.add)\
                        .then_inc(yr.sem, 1)
                if has(0, t):
                    after(v, num, t)
                    after(v, rd, t)
                    after(v, tr, t - 2)
                    v.tensor_tensor(AT[:, p, :].rearrange("p (h e) -> p h e", h=16), NUM[:, :, :],
                                    RD[:, :].unsqueeze(2).to_broadcast([P, 16, 8]), ALU.mult).then_inc(at.sem, 1)
            steps(v, step)
    close(c, S, N)


def ffn(c, cfg):
    with ExitStack() as ctx:
        sb = lambda nm, shape, dt=F32: c.sb(cfg["name"] + nm, shape, dt, ctx)
        NCH, E = cfg["NCH"], cfg.get("E")
        NT = sb("NT", [P, NTOK])
        W1, W2 = sb("W1", [P, NCH * P]), sb("W2", [P, NCH, P])
        W3 = sb("W3", [P, NCH * P]) if cfg["glu"] else None
        w_in = c.sem(cfg["name"] + "w_in")
        loads = [(W1[:, :], cfg["w1"], w_in), (W2[:, :, :].rearrange("p m d -> p (m d)"), cfg["w2"], w_in)]
        if cfg["glu"]:
            loads.append((W3[:, :], cfg["w3"], w_in))
        CB3 = sb("CB3", [P, 2 if E == 64 else 1, NTOK], BF16) if E else None
        CBF = sb("CBF", [8, NTOK]) if cfg.get("ebias") else None
        with ExitStack() as inner:
            LG = c.sb(cfg["name"] + "LG", [P, NT_TILES, E], F32, inner) if E else None
            norm_phase(c, cfg, NT, LG, loads)
            if E:
                combine_phase(c, cfg, LG, CB3, CBF)
        experts_phase(c, cfg, NT, W1, W3, W2, CB3, CBF, w_in, len(loads))


_OUT = (NB, T, D)


def build(nc, ins, out):
    with ExitStack() as ctx:
        c = Chip(nc, ctx, ins)
        nc.disable_value_cache = True
        start_phase(c, ins["x"])
        ln = dict(centered=True, eps=1e-5)
        xnorm = dict(nsrc=c.XT, ncentered=True, neps=1e-5)
        hnorm = dict(nsrc=c.HT, ncentered=True, neps=1e-5)
        rms = dict(nsrc=c.HT, ncentered=False, neps=1.1920928955078125e-07)
        attention_phase(c, dict(ln, name="a0", score_slots=8, layer=0, NH=16, HK=16, HV=16, VW=8, CW=128, causal=True,
                                gate="gate0", wq="wq0", wk="wk0", wv="wv0", wo="wo0", src=c.XT, dst=c.XT))
        ffn(c, dict(xnorm, name="f0", layer=0, nmod=3, gmod=5, wr="wr0", E=64, CAP=128, NCH=32,
                    sel=list(range(32)), glu=True, fn=ACT.Silu, w1="w1_0", w3="w3_0", w2="w2_0", selector="sel0"))
        attention_phase(c, dict(ln, name="a1", score_slots=21, layer=1, NH=32, HK=32, HV=16, VW=16, CW=256, causal=True, diff=True,
                                cscale="cscale", wq="wq1", wk="wk1", wv="wv1", wo="wo1", src=c.XT, dst=c.XT))
        ffn(c, dict(xnorm, name="f1", layer=1, nmod=3, gmod=5, wr="wr1", E=8, renorm=True, NCH=36,
                    sel=[m // 4 for m in range(32)] + [None] * 4, glu=False, fn=ACT.Gelu_apprx_tanh,
                    w1="w1_1", w2="w2_1", selector="sel1", hbias="hb1", ybias="yb1", ebias="eb1"))
        attention_phase(c, dict(ln, name="a2", score_slots=8, layer=2, NH=16, HK=1, HV=1, VW=8, CW=128, causal=False,
                                bq="bq2", bv="bv2", bo="bo2", wq="wq2", wk="wk2", wv="wv2", wo="wo2", src=c.XT, dst=c.XT))
        norm_phase(c, dict(xnorm, name="h2", layer=2, nmod=3), c.HT)
        attention_phase(c, dict(name="a4", score_slots=8, layer=2, centered=False, eps=rms["neps"], NH=16, HK=16, HV=4, VW=8, CW=128,
                                causal=True, rope=True, plain=True, gain="g1", wq="wq4", wk="wk4", wv="wv4", wo="wo4",
                                src=c.HT, dst=c.HT))
        ffn(c, dict(rms, name="f2", layer=2, gmod=5, ngain="g2", wr="wr2", E=4, renorm=True, NCH=12,
                    sel=[m // 3 for m in range(12)], glu=True, fn=ACT.Silu, w1="w1_2", w3="w3_2", w2="w2_2",
                    selector="sel2", plus=True))
        norm_phase(c, dict(xnorm, name="h3", layer=3, nmod=0), c.HT)
        with ExitStack() as part:
            NT = c.sb("NT3", [P, NTOK], F32, part)
            norm_phase(c, dict(hnorm, name="i3", ngain="ln1w", nshift="ln1b"), NT)
            linear_attention_phase(c, NT)
        ffn(c, dict(hnorm, name="f4", layer=3, gmod=2, ngain="ln2w", nshift="ln2b", NCH=4, sel=[None] * 4, glu=False,
                    fn=ACT.Gelu, w1="w1_4", w2="w2_4", hbias="hb4", ybias="yb4", plus=True))
        ffn(c, dict(xnorm, name="f3", layer=3, nmod=3, gmod=5, wr="wr3", E=8, renorm=False, NCH=11,
                    sel=list(range(11)), glu=True, fn=ACT.Silu, w1="w1_3", w3="w3_3", w2="w2_3", selector="sel3"))
        end_phase(c, out)


def layout(x):
    f = lambda a: np.ascontiguousarray(np.asarray(a))
    heads = lambda w, n: f(w.reshape(-1, n // 16, 16, HD).transpose(0, 1, 3, 2).reshape(w.shape[0], -1))
    col = lambda a: f(np.asarray(a).reshape(-1, 1))
    i = {"consts": constants(), "x": f(x["L0_attn_x"]), "zero": np.zeros((P, 1), np.float32)}
    for l in range(4):
        i[f"cT{l}"] = f(x[f"L{l}_c"].T)
        i[f"wmod{l}"] = f(x[f"L{l}_wmod"])
    w = x["L0_attn_w_qkv"]
    i["wq0"], i["wk0"], i["wv0"], i["wo0"] = heads(w[:, 0:D], 16), heads(w[:, D:2 * D], 16), f(w[:, 2 * D:]), f(x["L0_attn_w_out"])
    i["gate0"] = col(x["L0_attn_bandha_gate"])
    hm, oh = np.zeros((P, P), np.float32), np.zeros((P, T), np.float32)
    for h in range(16):
        cycle = (5, 6, 7, 8)[h % 4]
        for k in range(8):
            hm[h * 8 + k, h::16] = 1.0
            oh[h * 8 + k] = np.arange(T) % cycle == k
    i["headmask"], i["phases"] = hm, oh
    i["wq1"], i["wk1"], i["wv1"] = heads(x["L1_attn_Wq"], 32), heads(x["L1_attn_Wk"], 32), f(x["L1_attn_Wv"])
    i["wo1"] = f(x["L1_attn_Wo"].reshape(2, P, D).transpose(1, 0, 2).reshape(P, 2 * D))
    for n, key in enumerate(("q1", "k1", "q2", "k2")):
        i[f"lam{n}"] = f(np.broadcast_to(x[f"L1_attn_lambda_{key}"].reshape(1, -1), (P, 128)))
    i["cscale"] = col(np.tile(x["L1_attn_rms_scale"], 8))
    i["wq2"], i["wk2"], i["wv2"], i["wo2"] = heads(x["L2_attn_Wq"].T, 16), f(x["L2_attn_Wk"].T), f(x["L2_attn_Wv"].T), f(x["L2_attn_Wo"].T)
    i["bq2"] = col(x["L2_attn_bq"].reshape(16, 8).T)
    i["bv2"] = f(np.broadcast_to(x["L2_attn_bv"], (P, 8)))
    i["bo2"] = col(x["L2_attn_bo"])
    swap = lambda w: w.reshape(D, -1, 2, HD // 2)[:, :, ::-1].reshape(w.shape)
    wq, wk = x["L2_ffn_wq"], np.repeat(x["L2_ffn_wk"].reshape(D, 4, HD), 4, axis=1).reshape(D, -1)
    i["wq4"] = f(np.concatenate([heads(wq, 16), heads(swap(wq), 16)], 1))
    i["wk4"] = f(np.concatenate([heads(wk, 16), heads(swap(wk), 16)], 1))
    i["wv4"], i["wo4"], i["g1"], i["g2"] = f(x["L2_ffn_wv"]), f(x["L2_ffn_wo"]), col(x["L2_ffn_g1"]), col(x["L2_ffn_g2"])
    i["wqkv3"] = f(np.concatenate([x[f"L3_attn_w{k}"] for k in "qkv"], 1))
    i["bqkv3"] = f(np.concatenate([x[f"L3_attn_b{k}"] for k in "qkv"]).reshape(1, -1))
    i["wo3"], i["bo3"] = f(x["L3_attn_wo"]), col(x["L3_attn_bo"])
    for n in ("ln1", "ln2"):
        i[n + "w"], i[n + "b"] = col(x[f"L3_attn_{n}_w"]), col(x[f"L3_attn_{n}_b"])
    up = lambda w: f(w.transpose(1, 0, 2).reshape(D, -1))
    down = lambda w: f(w.reshape(-1, P, D).transpose(1, 0, 2).reshape(P, -1))
    chunks = lambda b: f(b.reshape(-1, P).T)
    i["w1_0"], i["w3_0"], i["w2_0"] = up(x["L0_ffn_w_gate"]), up(x["L0_ffn_w_up"]), down(x["L0_ffn_w_down"])
    i["wr0"], i["rbias"] = f(x["L0_ffn_gate_w"].T), f(np.broadcast_to(x["L0_ffn_gate_bias"], (P, 64)))
    i["w1_1"] = f(np.concatenate([up(x["L1_ffn_Wfc"]), x["L1_ffn_Wfc_s"]], 1))
    i["w2_1"] = f(np.concatenate([down(x["L1_ffn_Wproj"]), down(x["L1_ffn_Wproj_s"])], 1))
    i["hb1"] = f(np.concatenate([chunks(x["L1_ffn_bfc"]), chunks(x["L1_ffn_bfc_s"])], 1))
    i["wr1"], i["yb1"], i["eb1"] = f(x["L1_ffn_Wr"]), col(x["L1_ffn_bproj_s"]), f(x["L1_ffn_bproj"])
    i["w1_2"], i["w3_2"], i["w2_2"], i["wr2"] = up(x["L2_ffn_w1"]), up(x["L2_ffn_w3"]), down(x["L2_ffn_w2"]), f(x["L2_ffn_gate"])
    i["w1_3"], i["w3_3"], i["w2_3"], i["wr3"] = up(x["L3_ffn_w1"]), up(x["L3_ffn_w3"]), down(x["L3_ffn_w2"]), f(x["L3_ffn_w_router"].T)
    i["w1_4"], i["w2_4"] = f(x["L3_attn_fc_w"]), down(x["L3_attn_proj_w"])
    i["hb4"], i["yb4"] = chunks(x["L3_attn_fc_b"]), col(x["L3_attn_proj_b"])
    i["sel0"], i["sel1"], i["sel2"], i["sel3"] = selector(64, 64, 32), selector(8, 128, 8), selector(4, 128, 4), selector(8, 176, 11)
    return i


def selector(E, width, n):
    s = np.zeros((P, n, P), np.float32)
    for m in range(n):
        for p in range(P):
            s[(m * P + p) // width % 32:P:32, m, p] = 1.0
    return s.reshape(P, -1)


def kernel(**inputs):
    import concourse.bacc as _bacc
    from concourse.bass_utils import run_bass_kernel_spmd as _run

    nc = _bacc.Bacc("TRN2", target_bir_lowering=False, num_devices=1)
    arrays = layout(inputs)
    ins = {n: nc.dram_tensor(f"in_{n}", a.shape, mybir.dt.from_np(a.dtype), kind="ExternalInput").ap()
           for n, a in arrays.items()}
    out = nc.dram_tensor("out_0", _OUT, F32, kind="ExternalOutput").ap()
    build(nc, ins, out)
    r = _run(nc, [{f"in_{n}": a for n, a in arrays.items()}], core_ids=[0])
    return r.results[0]["out_0"]
```
